# Optimizing a Trainium2 kernel written in Bass

```python
import numpy as np
import jax
import jax.numpy as jnp

def _softmax(x, axis=-1):
    return jax.nn.softmax(x, axis=axis)

def _gelu(x):
    return jax.nn.gelu(x, approximate=True)

def _silu(x):
    return jax.nn.silu(x)

def _sigmoid(x):
    return jax.nn.sigmoid(x)

def _layernorm(x, axis=-1, eps=1e-05):
    m = jnp.mean(x, axis=axis, keepdims=True)
    v = jnp.var(x, axis=axis, keepdims=True)
    return (x - m) / jnp.sqrt(v + eps)

def _scatter_add(tgt, idx, src, axis=0):
    return tgt.at[idx].add(src)

def _segment_sum(src, seg, n):
    return jax.ops.segment_sum(src, seg, n)
kernel_name = 'mk_gnn_ffn_d4_gnn_r32_4fab12'

def setup_inputs(seed: int=0):
    np.random.seed(seed)
    _w = jnp.asarray

    def _rec_inputs():
        import jax
        import jax.numpy as jnp
        _gk = jax.random.key(seed)
        x = -0.0002117 + 1 * jax.random.normal(jax.random.fold_in(_gk, 1), (3125, 256), jnp.float32)
        src = jax.random.randint(jax.random.fold_in(_gk, 2), (50000,), 0, 3125, jnp.int32)
        dst = jax.random.randint(jax.random.fold_in(_gk, 3), (50000,), 0, 3125, jnp.int32)
        _o = jnp.argsort(dst, stable=True)
        src = src[_o]
        dst = dst[_o]
        edge_weight = jax.random.uniform(jax.random.fold_in(_gk, 13), (50000,), jnp.float32, 0.0, 0.999996)
        return (x, src, dst, edge_weight)
    x, src, dst, edge_weight = _rec_inputs()

    def _L0_gnn_setup():
        import jax, jax.numpy as jnp
        import numpy as np
        NEG = -1000.0
        SLOPE = 0.01
        N_NODES, N_EDGES, D_IN, D_OUT, N_HEADS = (3125, 50000, 256, 64, 4)
        key = jax.random.key(seed)
        k0, k1, k2, k3, k4 = jax.random.split(key, 5)
        h = jax.random.normal(k0, (N_NODES, D_IN), jnp.float32)
        src = jax.random.randint(k1, (N_EDGES,), 0, N_NODES)
        dst = jax.random.randint(k2, (N_EDGES,), 0, N_NODES)
        W = jax.random.normal(k3, (N_HEADS, D_IN, D_OUT), jnp.float32) / np.sqrt(D_IN)
        att = jax.random.normal(k4, (N_HEADS, 2 * D_OUT), jnp.float32) / np.sqrt(2.0 * D_OUT)
        return {'h': h, 'W': W, 'att': att, 'src': src, 'dst': dst}
    _L0_gnn_all = _L0_gnn_setup()
    _L0_gnn_in = {k: v for k, v in _L0_gnn_all.items() if k in ('W', 'att')}
    del _L0_gnn_all

    def _L0_ffn_setup():
        import jax, jax.numpy as jnp
        import numpy as np
        B, T, D, H, E = (16, 128, 256, 512, 8)
        key = jax.random.key(seed)
        ks = jax.random.split(key, 5)
        x = jax.random.normal(ks[0], (B, T, D), dtype=jnp.float32)
        gate_w = jax.random.normal(ks[1], (D, E), dtype=jnp.float32) * 0.02
        gate_b = jnp.zeros((E,), dtype=jnp.float32)
        W1 = jax.random.normal(ks[2], (E, D, H), dtype=jnp.float32) * 0.02
        b1 = jnp.zeros((E, H), dtype=jnp.float32)
        W2 = jax.random.normal(ks[3], (E, H, D), dtype=jnp.float32) * 0.02
        b2 = jnp.zeros((E, D), dtype=jnp.float32)
        return {'x': x, 'gate_w': gate_w, 'gate_b': gate_b, 'W1': W1, 'b1': b1, 'W2': W2, 'b2': b2}
    _L0_ffn_all = _L0_ffn_setup()
    _L0_ffn_in = {k: v for k, v in _L0_ffn_all.items() if k in ('gate_w', 'gate_b', 'W1', 'b1', 'W2', 'b2')}
    del _L0_ffn_all

    def _L1_gnn_setup():
        import jax, jax.numpy as jnp
        import numpy as np
        N_NODES = 50000
        N_EDGES = 25000
        DIM = 256
        NUM_HEADS = 8
        key = jax.random.key(seed)
        k_x, k_wu, k_bu, k_wv, k_src, k_dst = jax.random.split(key, 6)
        x = jax.random.normal(k_x, (N_NODES, DIM), dtype=jnp.float32)
        W_u = jax.random.normal(k_wu, (NUM_HEADS, DIM), dtype=jnp.float32) * (1.0 / np.sqrt(DIM))
        b_u = jax.random.normal(k_bu, (NUM_HEADS,), dtype=jnp.float32) * 0.01
        W_v = jax.random.normal(k_wv, (NUM_HEADS, DIM), dtype=jnp.float32) * (1.0 / np.sqrt(DIM))
        src = jax.random.randint(k_src, (N_EDGES,), 0, N_NODES, dtype=jnp.int32)
        dst = jax.random.randint(k_dst, (N_EDGES,), 0, N_NODES, dtype=jnp.int32)
        return {'x': x, 'W_u': W_u, 'b_u': b_u, 'W_v': W_v, 'src': src, 'dst': dst}
    _L1_gnn_all = _L1_gnn_setup()
    _L1_gnn_in = {k: v for k, v in _L1_gnn_all.items() if k in ('W_u', 'b_u', 'W_v')}
    del _L1_gnn_all

    def _L1_ffn_setup():
        import jax, jax.numpy as jnp
        import numpy as np
        B, S, D = (8, 128, 256)
        H = 4 * D
        CAPACITY = 0.5
        key = jax.random.key(seed)
        ks = jax.random.split(key, 6)
        x = jax.random.normal(ks[0], (B, S, D), dtype=jnp.float32)
        attention_mask = jnp.zeros((B, 1, 1, S), dtype=jnp.float32)
        wr = jax.random.normal(ks[1], (D, 1), dtype=jnp.float32) * 0.02
        br = jnp.zeros((1,), dtype=jnp.float32)
        w1 = jax.random.normal(ks[2], (D, H), dtype=jnp.float32) * 0.02
        b1 = jnp.zeros((H,), dtype=jnp.float32)
        w2 = jax.random.normal(ks[3], (H, D), dtype=jnp.float32) * 0.02
        b2 = jnp.zeros((D,), dtype=jnp.float32)
        return {'x': x, 'attention_mask': attention_mask, 'wr': wr, 'br': br, 'w1': w1, 'b1': b1, 'w2': w2, 'b2': b2}
    _L1_ffn_all = _L1_ffn_setup()
    _L1_ffn_in = {k: v for k, v in _L1_ffn_all.items() if k in ('attention_mask', 'wr', 'br', 'w1', 'b1', 'w2', 'b2')}
    del _L1_ffn_all

    def _L2_gnn_setup():
        import jax, jax.numpy as jnp
        import numpy as np
        N, E, L, C, D = (50000, 12500, 3, 4, 64)
        IN_DIM = C * D
        key = jax.random.key(seed)
        ks = jax.random.split(key, 10)
        return {'features': jax.random.normal(ks[0], (N, IN_DIM), dtype=jnp.float32), 'src': jax.random.randint(ks[1], (E,), 0, N, dtype=jnp.int32), 'dst': jax.random.randint(ks[2], (E,), 0, N, dtype=jnp.int32), 'edge_w': jax.random.uniform(ks[3], (E,), dtype=jnp.float32), 'fc_w': jax.random.normal(ks[4], (L, IN_DIM, IN_DIM), dtype=jnp.float32) * 0.05, 'fc_b': jax.random.normal(ks[5], (L, IN_DIM), dtype=jnp.float32) * 0.05, 'ch_w': jax.random.normal(ks[6], (L, C, D, D), dtype=jnp.float32) * 0.1, 'ch_b': jax.random.normal(ks[7], (L, C, D), dtype=jnp.float32) * 0.1, 'mlp_w': jax.random.normal(ks[8], (IN_DIM, L * IN_DIM), dtype=jnp.float32) * 0.05, 'mlp_b': jax.random.normal(ks[9], (IN_DIM,), dtype=jnp.float32) * 0.05}
    _L2_gnn_all = _L2_gnn_setup()
    _L2_gnn_in = {k: v for k, v in _L2_gnn_all.items() if k in ('fc_w', 'fc_b', 'ch_w', 'ch_b', 'mlp_w', 'mlp_b')}
    del _L2_gnn_all

    def _L2_ffn_setup():
        import jax, jax.numpy as jnp
        import numpy as np
        B, N, D = (16, 128, 256)
        NUM_EXPERTS, TOP_K, HEADS = (4, 2, 4)
        N_EDGES = 32768
        LN_EPS = 1e-05

        def _layernorm(x, g, b):
            mu = x.mean(-1, keepdims=True)
            var = ((x - mu) ** 2).mean(-1, keepdims=True)
            return (x - mu) * jax.lax.rsqrt(var + LN_EPS) * g + b

        def _forward(x, edge_index, W_gat, att_src, att_dst, b_gat, ln_gamma, ln_beta, W1, b1, W2, b2):
            Bc, Nc, Dc = x.shape
            M = Bc * Nc
            x_flat = x.reshape(M, Dc)
            h = (x_flat @ W_gat).reshape(M, HEADS, NUM_EXPERTS)
            loops = jnp.arange(M, dtype=edge_index.dtype)
            src = jnp.concatenate([edge_index[0], loops])
            dst = jnp.concatenate([edge_index[1], loops])
            a_src = (h * att_src).sum(-1)
            a_dst = (h * att_dst).sum(-1)
            e = jax.nn.leaky_relu(a_src[src] + a_dst[dst], negative_slope=0.2)
            e_max = jax.ops.segment_max(e, dst, num_segments=M)
            ee = jnp.exp(e - e_max[dst])
            denom = jax.ops.segment_sum(ee, dst, num_segments=M)
            alpha = ee / (denom[dst] + 1e-16)
            msg = h[src] * alpha[:, :, None]
            agg = jax.ops.segment_sum(msg, dst, num_segments=M).reshape(M, HEADS * NUM_EXPERTS) + b_gat
            scores = _layernorm(agg, ln_gamma, ln_beta).reshape(M, HEADS, NUM_EXPERTS).mean(1)
            scores = scores.reshape(Bc, Nc, NUM_EXPERTS)
            topk_s, topk_i = jax.lax.top_k(scores, TOP_K)
            w = jax.nn.softmax(topk_s, axis=-1)
            out = jnp.zeros_like(x)
            for ei in range(NUM_EXPERTS):
                g = jnp.where(topk_i == ei, w, 0.0).sum(-1)
                hh = jax.nn.gelu(x @ W1[ei] + b1[ei], approximate=False)
                out = out + g[..., None] * (hh @ W2[ei] + b2[ei])
            return out
        key = jax.random.key(seed)
        ks = jax.random.split(key, 8)
        s = 0.05
        return {'x': jax.random.normal(ks[0], (B, N, D), jnp.float32), 'W_gat': jax.random.normal(ks[1], (D, HEADS * NUM_EXPERTS), jnp.float32) * s, 'att_src': jax.random.normal(ks[2], (HEADS, NUM_EXPERTS), jnp.float32) * s, 'att_dst': jax.random.normal(ks[3], (HEADS, NUM_EXPERTS), jnp.float32) * s, 'b_gat': jnp.zeros((HEADS * NUM_EXPERTS,), jnp.float32), 'ln_gamma': jnp.ones((HEADS * NUM_EXPERTS,), jnp.float32), 'ln_beta': jnp.zeros((HEADS * NUM_EXPERTS,), jnp.float32), 'W1': jax.random.normal(ks[4], (NUM_EXPERTS, D, 2 * D), jnp.float32) * s, 'b1': jnp.zeros((NUM_EXPERTS, 2 * D), jnp.float32), 'W2': jax.random.normal(ks[5], (NUM_EXPERTS, 2 * D, D), jnp.float32) * s, 'b2': jnp.zeros((NUM_EXPERTS, D), jnp.float32), 'edge_index': jax.random.randint(ks[6], (2, N_EDGES), 0, B * N, jnp.int32)}
    _L2_ffn_all = _L2_ffn_setup()
    _L2_ffn_in = {k: v for k, v in _L2_ffn_all.items() if k in ('W_gat', 'att_src', 'att_dst', 'b_gat', 'ln_gamma', 'ln_beta', 'W1', 'b1', 'W2', 'b2', 'edge_index')}
    del _L2_ffn_all

    def _L3_gnn_setup():
        import jax, jax.numpy as jnp
        import numpy as np
        N = 50000
        E = 12500
        IN = 256
        HID = 128
        HEADS = 4
        OUT = 256
        NEG = 0.2

        def _glorot(key, shape, fan_in):
            return jax.random.normal(key, shape, jnp.float32) * (1.0 / np.sqrt(fan_in))

        def gatv2_conv(x, src, dst, Wl, Wr, att, bias, heads, ch, concat):
            n = x.shape[0]
            xl = (x @ Wl).reshape(n, heads, ch)
            xr = (x @ Wr).reshape(n, heads, ch)
            g = xl[src] + xr[dst]
            e = jnp.einsum('ehc,hc->eh', jax.nn.leaky_relu(g, NEG), att)
            e_max = jax.ops.segment_max(e, dst, num_segments=n)
            p = jnp.exp(e - e_max[dst])
            denom = jax.ops.segment_sum(p, dst, num_segments=n)
            alpha = p / denom[dst]
            out = jax.ops.segment_sum(alpha[:, :, None] * xl[src], dst, num_segments=n)
            out = out.reshape(n, heads * ch) if concat else out.mean(axis=1)
            return out + bias
        key = jax.random.key(seed)
        ks = jax.random.split(key, 8)
        x = jax.random.normal(ks[0], (N, IN), jnp.float32)
        edge_index = jax.random.randint(ks[1], (2, E), 0, N, dtype=jnp.int64)
        W1l = _glorot(ks[2], (IN, HEADS * HID), IN)
        W1r = _glorot(ks[3], (IN, HEADS * HID), IN)
        a1 = _glorot(ks[4], (HEADS, HID), HID)
        b1 = jnp.zeros((HEADS * HID,), jnp.float32)
        W2l = _glorot(ks[5], (HEADS * HID, OUT), HEADS * HID)
        W2r = _glorot(ks[6], (HEADS * HID, OUT), HEADS * HID)
        a2 = _glorot(ks[7], (1, OUT), OUT)
        b2 = jnp.zeros((OUT,), jnp.float32)
        return dict(x=x, edge_index=edge_index, W1l=W1l, W1r=W1r, a1=a1, b1=b1, W2l=W2l, W2r=W2r, a2=a2, b2=b2)
    _L3_gnn_all = _L3_gnn_setup()
    _L3_gnn_in = {k: v for k, v in _L3_gnn_all.items() if k in ('W1l', 'W1r', 'a1', 'b1', 'W2l', 'W2r', 'a2', 'b2')}
    del _L3_gnn_all

    def _L3_ffn_setup():
        import jax, jax.numpy as jnp
        import numpy as np
        B, S, D, H, E, K = (8, 256, 256, 1024, 8, 2)
        key = jax.random.key(seed)
        ks = jax.random.split(key, 7)
        s_in = 1.0 / np.sqrt(D)
        s_hid = 1.0 / np.sqrt(H)
        return {'x': jax.random.normal(ks[0], (B, S, D), dtype=jnp.float32), 'Wg': jax.random.uniform(ks[1], (E, D), jnp.float32, -s_in, s_in), 'bg': jax.random.uniform(ks[2], (E,), jnp.float32, -s_in, s_in), 'W1': jax.random.uniform(ks[3], (E, H, D), jnp.float32, -s_in, s_in), 'b1': jax.random.uniform(ks[4], (E, H), jnp.float32, -s_in, s_in), 'W2': jax.random.uniform(ks[5], (E, D, H), jnp.float32, -s_hid, s_hid), 'b2': jax.random.uniform(ks[6], (E, D), jnp.float32, -s_hid, s_hid)}
    _L3_ffn_all = _L3_ffn_setup()
    _L3_ffn_in = {k: v for k, v in _L3_ffn_all.items() if k in ('Wg', 'bg', 'W1', 'b1', 'W2', 'b2')}
    del _L3_ffn_all
    return {'x': x, 'src': src, 'dst': dst, 'edge_weight': edge_weight, 'L0_gnn_W': _L0_gnn_in['W'], 'L0_gnn_att': _L0_gnn_in['att'], 'L0_ffn_gate_w': _L0_ffn_in['gate_w'], 'L0_ffn_gate_b': _L0_ffn_in['gate_b'], 'L0_ffn_W1': _L0_ffn_in['W1'], 'L0_ffn_b1': _L0_ffn_in['b1'], 'L0_ffn_W2': _L0_ffn_in['W2'], 'L0_ffn_b2': _L0_ffn_in['b2'], 'L1_gnn_W_u': _L1_gnn_in['W_u'], 'L1_gnn_b_u': _L1_gnn_in['b_u'], 'L1_gnn_W_v': _L1_gnn_in['W_v'], 'L1_ffn_attention_mask': _L1_ffn_in['attention_mask'], 'L1_ffn_wr': _L1_ffn_in['wr'], 'L1_ffn_br': _L1_ffn_in['br'], 'L1_ffn_w1': _L1_ffn_in['w1'], 'L1_ffn_b1': _L1_ffn_in['b1'], 'L1_ffn_w2': _L1_ffn_in['w2'], 'L1_ffn_b2': _L1_ffn_in['b2'], 'L2_gnn_fc_w': _L2_gnn_in['fc_w'], 'L2_gnn_fc_b': _L2_gnn_in['fc_b'], 'L2_gnn_ch_w': _L2_gnn_in['ch_w'], 'L2_gnn_ch_b': _L2_gnn_in['ch_b'], 'L2_gnn_mlp_w': _L2_gnn_in['mlp_w'], 'L2_gnn_mlp_b': _L2_gnn_in['mlp_b'], 'L2_ffn_W_gat': _L2_ffn_in['W_gat'], 'L2_ffn_att_src': _L2_ffn_in['att_src'], 'L2_ffn_att_dst': _L2_ffn_in['att_dst'], 'L2_ffn_b_gat': _L2_ffn_in['b_gat'], 'L2_ffn_ln_gamma': _L2_ffn_in['ln_gamma'], 'L2_ffn_ln_beta': _L2_ffn_in['ln_beta'], 'L2_ffn_W1': _L2_ffn_in['W1'], 'L2_ffn_b1': _L2_ffn_in['b1'], 'L2_ffn_W2': _L2_ffn_in['W2'], 'L2_ffn_b2': _L2_ffn_in['b2'], 'L2_ffn_edge_index': _L2_ffn_in['edge_index'], 'L3_gnn_W1l': _L3_gnn_in['W1l'], 'L3_gnn_W1r': _L3_gnn_in['W1r'], 'L3_gnn_a1': _L3_gnn_in['a1'], 'L3_gnn_b1': _L3_gnn_in['b1'], 'L3_gnn_W2l': _L3_gnn_in['W2l'], 'L3_gnn_W2r': _L3_gnn_in['W2r'], 'L3_gnn_a2': _L3_gnn_in['a2'], 'L3_gnn_b2': _L3_gnn_in['b2'], 'L3_ffn_Wg': _L3_ffn_in['Wg'], 'L3_ffn_bg': _L3_ffn_in['bg'], 'L3_ffn_W1': _L3_ffn_in['W1'], 'L3_ffn_b1': _L3_ffn_in['b1'], 'L3_ffn_W2': _L3_ffn_in['W2'], 'L3_ffn_b2': _L3_ffn_in['b2']}

def reference(x, src, dst, edge_weight, L0_gnn_W, L0_gnn_att, L0_ffn_gate_w, L0_ffn_gate_b, L0_ffn_W1, L0_ffn_b1, L0_ffn_W2, L0_ffn_b2, L1_gnn_W_u, L1_gnn_b_u, L1_gnn_W_v, L1_ffn_attention_mask, L1_ffn_wr, L1_ffn_br, L1_ffn_w1, L1_ffn_b1, L1_ffn_w2, L1_ffn_b2, L2_gnn_fc_w, L2_gnn_fc_b, L2_gnn_ch_w, L2_gnn_ch_b, L2_gnn_mlp_w, L2_gnn_mlp_b, L2_ffn_W_gat, L2_ffn_att_src, L2_ffn_att_dst, L2_ffn_b_gat, L2_ffn_ln_gamma, L2_ffn_ln_beta, L2_ffn_W1, L2_ffn_b1, L2_ffn_W2, L2_ffn_b2, L2_ffn_edge_index, L3_gnn_W1l, L3_gnn_W1r, L3_gnn_a1, L3_gnn_b1, L3_gnn_W2l, L3_gnn_W2r, L3_gnn_a2, L3_gnn_b2, L3_ffn_Wg, L3_ffn_bg, L3_ffn_W1, L3_ffn_b1, L3_ffn_W2, L3_ffn_b2):
    import jax
    import jax.numpy as jnp

    def _L0_gnn_ref(h, W, att, src, dst):
        import jax, jax.numpy as jnp
        import numpy as np
        NEG = -1000.0
        SLOPE = 0.01
        N_NODES, N_EDGES, D_IN, D_OUT, N_HEADS = (3125, 50000, 256, 64, 4)
        N = h.shape[0]
        H, _, F = W.shape
        z = jnp.einsum('nd,hdf->nhf', h, W)
        a_src, a_dst = (att[:, :F], att[:, F:])
        es = jnp.einsum('nhf,hf->nh', z, a_src)
        ed = jnp.einsum('nhf,hf->nh', z, a_dst)
        e = jax.nn.leaky_relu(es[src] + ed[dst], SLOPE)
        e = jnp.where(e == 0.0, NEG, e)
        m = jax.ops.segment_max(e, dst, num_segments=N)
        m = jnp.where(jnp.isfinite(m), m, 0.0)
        ex = jnp.exp(e - m[dst])
        denom = jax.ops.segment_sum(ex, dst, num_segments=N)
        safe = jnp.where(denom[dst] > 0.0, denom[dst], 1.0)
        alpha = ex / safe
        out = jax.ops.segment_sum(alpha[:, :, None] * z[src], dst, num_segments=N)
        return out.reshape(N, H * F)

    def _L0_ffn_ref(x, gate_w, gate_b, W1, b1, W2, b2):
        import jax, jax.numpy as jnp
        import numpy as np
        B, T, D, H, E = (16, 128, 256, 512, 8)
        Bb, Tt, Dd = x.shape
        Ee = gate_w.shape[1]
        xf = x.reshape(-1, Dd)
        N = xf.shape[0]
        logits = xf @ gate_w + gate_b
        probs = jax.nn.softmax(logits, axis=-1)
        top2_vals, top2_idx = jax.lax.top_k(probs, 2)
        cw = jnp.zeros((N, Ee), dtype=xf.dtype).at[jnp.arange(N)[:, None], top2_idx].add(top2_vals)

        def step(acc, params):
            w1, bb1, w2, bb2, we = params
            h = jax.nn.gelu(xf @ w1 + bb1, approximate=False)
            y = h @ w2 + bb2
            return (acc + we[:, None] * y, None)
        out, _ = jax.lax.scan(step, jnp.zeros_like(xf), (W1, b1, W2, b2, cw.T))
        return out.reshape(Bb, Tt, Dd)

    def _L1_gnn_ref(x, W_u, b_u, W_v, src, dst):
        import jax, jax.numpy as jnp
        import numpy as np
        N_NODES = 50000
        N_EDGES = 25000
        DIM = 256
        NUM_HEADS = 8
        n_nodes, dim = x.shape
        num_heads = W_u.shape[0]
        head_dim = dim // num_heads
        s_u = x @ W_u.T + b_u
        s_v = x @ W_v.T
        e = s_u[src] + s_v[dst]
        e = jnp.where(e >= 0, e, 0.2 * e)
        m = jax.ops.segment_max(e, dst, num_segments=n_nodes)
        e_exp = jnp.exp(e - m[dst])
        denom = jax.ops.segment_sum(e_exp, dst, num_segments=n_nodes)
        probs = e_exp / denom[dst]
        xh = x.reshape(n_nodes, head_dim, num_heads)
        msg = xh[src] * probs[:, None, :]
        out = jax.ops.segment_sum(msg, dst, num_segments=n_nodes)
        return out.reshape(n_nodes, dim)

    def _L1_ffn_ref(x, attention_mask, wr, br, w1, b1, w2, b2):
        import jax, jax.numpy as jnp
        import numpy as np
        B, S, D = (8, 128, 256)
        H = 4 * D
        CAPACITY = 0.5
        b, s, d = x.shape
        weights = (jnp.einsum('bsd,do->bso', x, wr) + br)[..., 0]
        k = max(1, int(CAPACITY * s))
        kk = k - 1 if k > 1 else 1
        _, idx = jax.lax.top_k(weights, k)
        sel_idx = idx[:, :kk]
        sel = jnp.take_along_axis(x, sel_idx[:, :, None], axis=1)
        h = jax.nn.gelu(jnp.einsum('bkd,dh->bkh', sel, w1) + b1)
        y = jnp.einsum('bkh,hd->bkd', h, w2) + b2
        w_sel = jnp.take_along_axis(weights, sel_idx, axis=1)
        y = y * w_sel[..., None]
        batch_idx = jnp.arange(b)[:, None]
        processed = jnp.zeros_like(x).at[batch_idx, sel_idx].set(y)
        return processed + x

    def _L2_gnn_ref(features, src, dst, edge_w, fc_w, fc_b, ch_w, ch_b, mlp_w, mlp_b):
        import jax, jax.numpy as jnp
        import numpy as np
        N, E, L, C, D = (50000, 12500, 3, 4, 64)
        IN_DIM = C * D
        n = features.shape[0]
        ones = jnp.ones_like(edge_w)
        deg_out = jnp.maximum(jax.ops.segment_sum(ones, src, num_segments=n), 1.0)
        deg_in = jnp.maximum(jax.ops.segment_sum(ones, dst, num_segments=n), 1.0)
        norm_out = (deg_out ** (-0.5))[:, None, None]
        norm_in = (deg_in ** (-0.5))[:, None, None]
        x = features
        outs = []
        for l in range(L):
            h = x @ fc_w[l].T + fc_b[l]
            f = h.reshape(n, C, D) * norm_out
            f = jnp.einsum('ncd,cde->nce', f, ch_w[l])
            m = f[src] * edge_w[:, None, None]
            agg = jax.ops.segment_sum(m, dst, num_segments=n)
            r = agg * norm_in + ch_b[l]
            r = jax.nn.relu(r)
            x = r.reshape(n, C * D)
            outs.append(x)
        hcat = jnp.concatenate(outs, axis=-1)
        return hcat @ mlp_w.T + mlp_b

    def _L2_ffn_ref(x, W_gat, att_src, att_dst, b_gat, ln_gamma, ln_beta, W1, b1, W2, b2, edge_index):
        import jax, jax.numpy as jnp
        import numpy as np
        B, N, D = (16, 128, 256)
        NUM_EXPERTS, TOP_K, HEADS = (4, 2, 4)
        N_EDGES = 32768
        LN_EPS = 1e-05

        def _layernorm(x, g, b):
            mu = x.mean(-1, keepdims=True)
            var = ((x - mu) ** 2).mean(-1, keepdims=True)
            return (x - mu) * jax.lax.rsqrt(var + LN_EPS) * g + b

        def _forward(x, edge_index, W_gat, att_src, att_dst, b_gat, ln_gamma, ln_beta, W1, b1, W2, b2):
            Bc, Nc, Dc = x.shape
            M = Bc * Nc
            x_flat = x.reshape(M, Dc)
            h = (x_flat @ W_gat).reshape(M, HEADS, NUM_EXPERTS)
            loops = jnp.arange(M, dtype=edge_index.dtype)
            src = jnp.concatenate([edge_index[0], loops])
            dst = jnp.concatenate([edge_index[1], loops])
            a_src = (h * att_src).sum(-1)
            a_dst = (h * att_dst).sum(-1)
            e = jax.nn.leaky_relu(a_src[src] + a_dst[dst], negative_slope=0.2)
            e_max = jax.ops.segment_max(e, dst, num_segments=M)
            ee = jnp.exp(e - e_max[dst])
            denom = jax.ops.segment_sum(ee, dst, num_segments=M)
            alpha = ee / (denom[dst] + 1e-16)
            msg = h[src] * alpha[:, :, None]
            agg = jax.ops.segment_sum(msg, dst, num_segments=M).reshape(M, HEADS * NUM_EXPERTS) + b_gat
            scores = _layernorm(agg, ln_gamma, ln_beta).reshape(M, HEADS, NUM_EXPERTS).mean(1)
            scores = scores.reshape(Bc, Nc, NUM_EXPERTS)
            topk_s, topk_i = jax.lax.top_k(scores, TOP_K)
            w = jax.nn.softmax(topk_s, axis=-1)
            out = jnp.zeros_like(x)
            for ei in range(NUM_EXPERTS):
                g = jnp.where(topk_i == ei, w, 0.0).sum(-1)
                hh = jax.nn.gelu(x @ W1[ei] + b1[ei], approximate=False)
                out = out + g[..., None] * (hh @ W2[ei] + b2[ei])
            return out
        return _forward(x, edge_index, W_gat, att_src, att_dst, b_gat, ln_gamma, ln_beta, W1, b1, W2, b2)

    def _L3_gnn_ref(x, edge_index, W1l, W1r, a1, b1, W2l, W2r, a2, b2):
        import jax, jax.numpy as jnp
        import numpy as np
        N = 50000
        E = 12500
        IN = 256
        HID = 128
        HEADS = 4
        OUT = 256
        NEG = 0.2

        def _glorot(key, shape, fan_in):
            return jax.random.normal(key, shape, jnp.float32) * (1.0 / np.sqrt(fan_in))

        def gatv2_conv(x, src, dst, Wl, Wr, att, bias, heads, ch, concat):
            n = x.shape[0]
            xl = (x @ Wl).reshape(n, heads, ch)
            xr = (x @ Wr).reshape(n, heads, ch)
            g = xl[src] + xr[dst]
            e = jnp.einsum('ehc,hc->eh', jax.nn.leaky_relu(g, NEG), att)
            e_max = jax.ops.segment_max(e, dst, num_segments=n)
            p = jnp.exp(e - e_max[dst])
            denom = jax.ops.segment_sum(p, dst, num_segments=n)
            alpha = p / denom[dst]
            out = jax.ops.segment_sum(alpha[:, :, None] * xl[src], dst, num_segments=n)
            out = out.reshape(n, heads * ch) if concat else out.mean(axis=1)
            return out + bias
        loop = jnp.arange(x.shape[0], dtype=edge_index.dtype)
        src = jnp.concatenate([edge_index[0], loop])
        dst = jnp.concatenate([edge_index[1], loop])
        h = jax.nn.relu(gatv2_conv(x, src, dst, W1l, W1r, a1, b1, HEADS, HID, True))
        return gatv2_conv(h, src, dst, W2l, W2r, a2, b2, 1, OUT, False)

    def _L3_ffn_ref(x, Wg, bg, W1, b1, W2, b2):
        import jax, jax.numpy as jnp
        import numpy as np
        B, S, D, H, E, K = (8, 256, 256, 1024, 8, 2)
        gate_scores = jnp.einsum('bsd,ed->bse', x, Wg) + bg
        topk_scores, topk_idx = jax.lax.top_k(gate_scores, K)
        topk_probs = jax.nn.softmax(topk_scores, axis=-1)
        combine = jnp.sum(topk_probs[..., None] * jax.nn.one_hot(topk_idx, E, dtype=x.dtype), axis=-2)
        out = jnp.zeros_like(x)
        for e in range(E):
            h = jax.nn.relu(jnp.einsum('bsd,hd->bsh', x, W1[e]) + b1[e])
            y = jnp.einsum('bsh,dh->bsd', h, W2[e]) + b2[e]
            out = out + combine[..., e:e + 1] * y
        return out
    edge_index = jnp.stack([src, dst])
    x = x + _L0_gnn_ref(_layernorm(x, axis=-1), L0_gnn_W, L0_gnn_att, src, dst)
    x = x + _L0_ffn_ref(_layernorm(x, axis=-1)[None], L0_ffn_gate_w, L0_ffn_gate_b, L0_ffn_W1, L0_ffn_b1, L0_ffn_W2, L0_ffn_b2)[0]
    x = x + _L1_gnn_ref(_layernorm(x, axis=-1), L1_gnn_W_u, L1_gnn_b_u, L1_gnn_W_v, src, dst)
    x = x + _L1_ffn_ref(_layernorm(x, axis=-1)[None], L1_ffn_attention_mask, L1_ffn_wr, L1_ffn_br, L1_ffn_w1, L1_ffn_b1, L1_ffn_w2, L1_ffn_b2)[0]
    x = x + _L2_gnn_ref(_layernorm(x, axis=-1), src, dst, edge_weight, L2_gnn_fc_w, L2_gnn_fc_b, L2_gnn_ch_w, L2_gnn_ch_b, L2_gnn_mlp_w, L2_gnn_mlp_b)
    x = x + _L2_ffn_ref(_layernorm(x, axis=-1)[None], L2_ffn_W_gat, L2_ffn_att_src, L2_ffn_att_dst, L2_ffn_b_gat, L2_ffn_ln_gamma, L2_ffn_ln_beta, L2_ffn_W1, L2_ffn_b1, L2_ffn_W2, L2_ffn_b2, L2_ffn_edge_index)[0]
    x = x + _L3_gnn_ref(_layernorm(x, axis=-1), edge_index, L3_gnn_W1l, L3_gnn_W1r, L3_gnn_a1, L3_gnn_b1, L3_gnn_W2l, L3_gnn_W2r, L3_gnn_a2, L3_gnn_b2)
    x = x + _L3_ffn_ref(_layernorm(x, axis=-1)[None], L3_ffn_Wg, L3_ffn_bg, L3_ffn_W1, L3_ffn_b1, L3_ffn_W2, L3_ffn_b2)[0]
    return x

_drawn_inputs = setup_inputs


def setup_inputs(seed=0):
    import zlib

    import numpy as np

    out = dict(_drawn_inputs(seed))
    spreads = {'L0_ffn_gate_b': (0.0, 0.1),
     'L0_ffn_b1': (0.0, 0.302),
     'L0_ffn_b2': (0.0, 0.1),
     'L1_ffn_b1': (0.0, 0.8),
     'L1_ffn_b2': (0.0, 0.465),
     'L2_ffn_b_gat': (0.0, 0.1),
     'L2_ffn_ln_gamma': (1.0, 0.2),
     'L2_ffn_ln_beta': (0.0, 0.355),
     'L2_ffn_b1': (0.0, 0.302),
     'L2_ffn_b2': (0.0, 0.1),
     'L3_gnn_b1': (0.0, 0.297),
     'L3_gnn_b2': (0.0, 0.1)}
    factors = {'edge_weight': 3.389,
     'L1_gnn_b_u': 42.158,
     'L1_ffn_wr': 3.254,
     'L1_ffn_w1': 3.759,
     'L1_ffn_w2': 3.476,
     'L2_ffn_att_src': 2.686,
     'L2_ffn_att_dst': 3.695,
     'L3_gnn_W1r': 8.0,
     'L3_gnn_a1': 2.7,
     'L3_gnn_W2r': 8.0,
     'L3_gnn_a2': 8.0,
     'L3_ffn_bg': 3.772,
     'L3_ffn_b1': 8.0,
     'L3_ffn_b2': 8.0}
    for name, (base, spread) in spreads.items():
        noise = np.random.default_rng([zlib.crc32(name.encode()), seed]).standard_normal(out[name].shape)
        drawn = base * np.exp(spread * noise) if base else spread * noise
        out[name] = jnp.asarray(drawn.astype(out[name].dtype))
    for name, factor in factors.items():
        out[name] = (out[name] * factor).astype(out[name].dtype)
    return out
```

```python
from contextlib import ExitStack, contextmanager

import numpy as np

import concourse.bass as bass
from concourse import mybir

F32 = mybir.dt.float32
BF16 = mybir.dt.bfloat16
I32 = mybir.dt.int32
ALU = mybir.AluOpType
ACT = mybir.ActivationFunctionType
AX = mybir.AxisListType

P = 128
D = 256
N = 3125
NT = -(-N // P)
NP = NT * P
GRP = 5
NG = NT // GRP
SLOTS = 4
DC = D // P
UNIT = GRP * P
HALF = UNIT // 2
LN_EPS = 1e-5
MASKED = 1e30
APART = 1e38
TAB = D + 8


class Phase:

    count = 0

    def __init__(self, nc, ctx):
        self.nc, self.ctx, self.sems = nc, ctx, []
        Phase.count += 1
        self.n = Phase.count

    def sb(self, name, shape, dt=F32):
        return self.ctx.enter_context(self.nc.sbuf_tensor(f"{name}_{self.n}", shape, dt))

    def ps(self, name, shape, dt=F32):
        return self.ctx.enter_context(self.nc.psum_tensor(f"{name}_{self.n}", shape, dt))

    def sem(self, name):
        self.sems.append(self.nc.alloc_semaphore(f"{name}_{self.n}"))
        return self.sems[-1]

    def sem_ring(self, name, n):
        return [self.sem(f"{name}{i}") for i in range(n)]


@contextmanager
def phase(nc):
    with ExitStack() as ctx:
        ph = Phase(nc, ctx)
        yield ph
        nc.clear_and_free_semaphores(ph.sems)
        nc.all_engine_barrier()


def hold(eng, sem, value, passed):
    eng.wait_ge(sem, value)
    eng.sem_inc(passed, 1)


def wide(ap, dim, n):
    ap = ap.unsqueeze(dim)
    shape = list(ap.shape)
    shape[dim] = n
    return ap.broadcast_to(shape)


def build_constants(nc, C, x):
    with phase(nc) as ph:
        loaded, filled, made = ph.sem("loaded"), ph.sem("filled"), ph.sem("made")
        iota_i = ph.sb("iota_i", [P, P], I32)
        col_i = ph.sb("col_i", [P, 1], I32)
        with nc.Block() as block:
            @block.sync
            def _(sp):
                sp.wait_ge(filled, 1)
                sp.dma_start(C.X[:, 0:NT - 1, :],
                             x[0:(NT - 1) * P, :].rearrange("(t p) f -> p t f", p=P)).then_inc(loaded, 16)
                sp.dma_start(C.X[0:N - (NT - 1) * P, NT - 1, :], x[(NT - 1) * P:N, :]).then_inc(loaded, 16)
                sp.wait_ge(loaded, 32)

            @block.vector
            def _(v):
                v.memset(C.X[:, NT - 1, :], 0.0).then_inc(filled, 1)
                v.memset(C.ones[:], 1.0)
                v.wait_ge(made, 9)
                v.tensor_copy(C.iota_row[:], iota_i[:])
                v.tensor_copy(C.iota_col[:], col_i[:])

            @block.gpsimd
            def _(pool):
                pool.memset(C.ident[:], 0.0).then_inc(made, 1)
                pool.memset(C.below[:], 1.0).then_inc(made, 1)
                pool.memset(C.above[:], 1.0).then_inc(made, 1)
                pool.wait_ge(made, 3)
                pool.affine_select(out=C.ident[:], in_=C.ident[:], compare_op=ALU.not_equal, fill=1.0,
                                   base=0, pattern=[[-1, P]], channel_multiplier=1).then_inc(made, 1)
                pool.affine_select(out=C.below[:], in_=C.below[:], compare_op=ALU.is_gt, fill=0.0,
                                   base=0, pattern=[[-1, P]], channel_multiplier=1).then_inc(made, 1)
                pool.affine_select(out=C.above[:], in_=C.above[:], compare_op=ALU.is_gt, fill=0.0,
                                   base=0, pattern=[[1, P]], channel_multiplier=-1).then_inc(made, 1)
                pool.iota(iota_i[:], pattern=[[1, P]], base=0, channel_multiplier=0).then_inc(made, 1)
                pool.iota(col_i[:], pattern=[[0, 1]], base=0, channel_multiplier=1).then_inc(made, 1)
                pool.iota(C.node_i[:], pattern=[[P, NT]], base=0, channel_multiplier=1).then_inc(made, 1)


class Graph:

    def __init__(self, nc, sb, name, tiles, rows, degrees):
        self.name, self.T, self.R = name, tiles, rows
        assert tiles * P + NP + NP * (SLOTS - 1) <= rows * P * SLOTS
        self.records = nc.dram_tensor(f"records_{name}", (P * rows * SLOTS, 4), I32, kind="Internal").ap()
        self.cont = sb(f"cont_{name}", [P, rows], F32)
        self.apart = sb(f"apart_{name}", [P, rows + 1], F32)
        self.in_first = sb(f"in_first_{name}", [P, rows], F32)
        self.in_last = sb(f"in_last_{name}", [P, rows], F32)
        self.carry = sb(f"carry_{name}", [P, P], F32)
        self.from_prev = sb(f"from_prev_{name}", [P, P], F32)
        self.from_next = sb(f"from_next_{name}", [P, P], F32)
        self.ends_here = sb(f"ends_here_{name}", [P, 1], F32)
        self.first_node = sb(f"first_node_{name}", [P, NT], F32)
        self.end_row = sb(f"end_row_{name}", [P, NT], I32)
        self.is_edge = sb(f"is_edge_{name}", [P, rows, SLOTS], F32)
        self.is_any = sb(f"is_any_{name}", [P, rows, SLOTS], F32)
        if degrees:
            self.weight = sb(f"weight_{name}", [P, rows, SLOTS], F32)
            self.norm_in = sb(f"norm_in_{name}", [P, NT], F32)
            self.norm_out = sb(f"norm_out_{name}", [P, NT], F32)
        self.degrees = degrees


def sort_edges(nc, C, g, dst_rows, dst_cols, src_cols, w_cols):
    T, R = g.T, g.R
    SUB = 4
    TURNS = T // (2 * SUB)
    with ExitStack() as outer:
        def keep(name, shape, dt=F32):
            return outer.enter_context(nc.sbuf_tensor(f"{name}_{g.name}", shape, dt))

        counts = keep("counts", [P, T, NT])
        offset = keep("offset", [P, T, NT])
        dst_i = keep("dst_i", [P, T], I32)
        src_i = keep("src_i", [P, T], I32)
        w_f = keep("w_f", [P, T])
        dst_f = keep("dst_f", [P, T])
        dst_lo = keep("dst_lo", [P, T])
        loop_slot = keep("loop_slot", [P, NT], I32)
        out_count = keep("out_count", [P, SUB * NT])

        with phase(nc) as ph:
            tmp_i = ph.sb("tmp_i", [P, T], I32)
            dst_hi = ph.sb("dst_hi", [P, T])
            src_hi = ph.sb("src_hi", [P, T])
            src_lo = ph.sb("src_lo", [P, T])
            blank = ph.sb("blank", [P, R * SLOTS, 4], I32)
            oh_hi = ph.sb("oh_hi", [P, 2, 2, SUB, P], BF16)
            oh_lo = ph.sb("oh_lo", [P, 2, 2, SUB, NT], BF16)
            psum = ph.ps("psum", [P, 2, 2, 512])
            loaded, blanked, blank_sent = ph.sem("loaded"), ph.sem("blanked"), ph.sem("blank_sent")
            hot_ready = ph.sem_ring("hot_ready", 2)
            counted, taken, added = ph.sem_ring("counted", 2), ph.sem_ring("taken", 2), ph.sem_ring("added", 2)
            pe_passed, act_passed, v_passed = ph.sem("pe_passed"), ph.sem("act_passed"), ph.sem("v_passed")
            both = [("dst", dst_hi, dst_lo)] + ([("src", src_hi, src_lo)] if g.degrees else [])
            with nc.Block() as block:
                @block.sync
                def _(sp):
                    sp.dma_start(dst_i[:], dst_cols).then_inc(loaded, 16)
                    sp.dma_start(src_i[:], src_cols).then_inc(loaded, 16)
                    if g.degrees:
                        sp.dma_start(w_f[:], w_cols).then_inc(loaded, 16)
                    sp.wait_ge(blanked, 1)
                    sp.dma_start(g.records.rearrange("(p s) c -> p s c", p=P), blank[:]).then_inc(blank_sent, 16)
                    sp.wait_ge(blank_sent, 16)

                @block.vector
                def _(v):
                    v.memset(blank[:], 0)
                    v.memset(out_count[:], 0.0)
                    if not g.degrees:
                        v.memset(w_f[:], 0.0)
                    v.drain()
                    v.memset(blank[:, :, 3], NP - 1).then_inc(blanked, 1)
                    v.wait_ge(loaded, 48 if g.degrees else 32)
                    v.tensor_copy(dst_f[:], dst_i[:])
                    for (_, hi, lo), ends in zip(both, (dst_i, src_i)):
                        v.drain()
                        v.tensor_scalar(tmp_i[:], ends[:], P - 1, None, ALU.bitwise_and)
                        v.drain()
                        v.tensor_copy(hi[:], tmp_i[:])
                        v.drain()
                        v.tensor_scalar(tmp_i[:], ends[:], P.bit_length() - 1, None, ALU.logical_shift_right)
                        v.drain()
                        v.tensor_copy(lo[:], tmp_i[:])
                    v.drain()
                    with v.Fori(0, TURNS) as i:
                        for s in range(2):
                            hold(v, counted[s], i + 1, v_passed)
                            for k, (_, hi, lo) in enumerate(both):
                                at = bass.ds(i * (2 * SUB) + s * SUB, SUB)
                                v.tensor_tensor(oh_hi[:, s, k], wide(C.iota_row[:], 1, SUB),
                                                wide(hi[:, at], 2, P), ALU.is_equal)
                                last = v.tensor_tensor(oh_lo[:, s, k], wide(C.iota_row[:, 0:NT], 1, SUB),
                                                       wide(lo[:, at], 2, NT), ALU.is_equal)
                            last.then_inc(hot_ready[s], 1)
                            if g.degrees:
                                v.wait_ge(counted[s], i + 2)
                                v.tensor_tensor(out_count[:], out_count[:], psum[:, s, 1, 0:SUB * NT],
                                                ALU.add).then_inc(added[s], 1)

                @block.tensor
                def _(pe):
                    for s in range(2):
                        pe.sem_inc(counted[s], 1)
                    with pe.Fori(0, TURNS) as i:
                        for s in range(2):
                            hold(pe, hot_ready[s], i + 1, pe_passed)
                            hold(pe, taken[s], i + 1, pe_passed)
                            if g.degrees:
                                hold(pe, added[s], i + 1, pe_passed)
                            for k in range(len(both)):
                                for j in range(SUB):
                                    last = pe.matmul(psum[:, s, k, j * NT:(j + 1) * NT], oh_hi[:, s, k, j],
                                                     oh_lo[:, s, k, j], start=True, stop=True)
                            last.then_inc(counted[s], 1)

                @block.scalar
                def _(act):
                    for s in range(2):
                        act.sem_inc(taken[s], 1)
                        act.sem_inc(added[s], 1)
                    with act.Fori(0, TURNS) as i:
                        for s in range(2):
                            hold(act, counted[s], i + 2, act_passed)
                            act.activation(counts[:, bass.ds(i * (2 * SUB) + s * SUB, SUB), :],
                                           psum[:, s, 0, 0:SUB * NT].rearrange("p (j l) -> p j l", j=SUB),
                                           ACT.Copy).then_inc(taken[s], 1)

        with phase(nc) as ph:
            deg = ph.sb("deg", [P, NT])
            rows_f = ph.sb("rows_f", [P, NT])
            inc = ph.sb("inc", [P, NT])
            start = ph.sb("start", [P, NT])
            tmp_i = ph.sb("tmp_i", [P, NT], I32)
            tmp_f = ph.sb("tmp_f", [P, NT])
            total = ph.sb("total", [P, 1])
            norm = ph.sb("norm", [P, 2, NT])
            psum = ph.ps("psum", [P, 512])
            have_total, have_base, clipped, rooted = (ph.sem(n) for n in ("have_total", "have_base", "clipped", "rooted"))
            with nc.Block() as block:
                @block.vector
                def _(v):
                    for lo in range(NT):
                        v.tensor_tensor_scan(offset[:, :, lo], C.ones[:, 0:1].broadcast_to([P, T]),
                                             counts[:, :, lo], 0.0, ALU.mult, ALU.add)
                    v.drain()
                    v.tensor_copy(deg[:], offset[:, T - 1, :])
                    v.drain()
                    v.tensor_tensor(offset[:], offset[:], counts[:], ALU.subtract)
                    v.tensor_scalar(tmp_f[:], deg[:], float(SLOTS), None, ALU.add)
                    v.drain()
                    v.tensor_copy(tmp_i[:], tmp_f[:])
                    v.drain()
                    v.tensor_scalar(tmp_i[:], tmp_i[:], SLOTS.bit_length() - 1, None, ALU.logical_shift_right)
                    v.drain()
                    v.tensor_copy(rows_f[:], tmp_i[:])
                    v.drain()
                    v.tensor_tensor_scan(inc[:], C.ones[:, 0:1].broadcast_to([P, NT]), rows_f[:], 0.0,
                                         ALU.mult, ALU.add)
                    v.drain()
                    v.tensor_copy(total[:], inc[:, NT - 1:NT]).then_inc(have_total, 1)
                    v.tensor_tensor(start[:], inc[:], rows_f[:], ALU.subtract)
                    v.drain()
                    v.wait_ge(have_base, 1)
                    v.tensor_scalar(start[:], start[:], psum[:, 0:1], None, ALU.add)
                    v.drain()
                    v.tensor_tensor(tmp_f[:], start[:], rows_f[:], ALU.add)
                    v.drain()
                    v.tensor_scalar(tmp_f[:], tmp_f[:], 1.0, None, ALU.subtract)
                    v.drain()
                    v.tensor_copy(g.end_row[:], tmp_f[:])
                    v.tensor_scalar(start[:], start[:], float(SLOTS), None, ALU.mult)
                    v.drain()
                    v.tensor_tensor(offset[:], offset[:], wide(start[:], 1, T), ALU.add)
                    v.tensor_tensor(tmp_f[:], start[:], deg[:], ALU.add)
                    v.drain()
                    v.tensor_copy(loop_slot[:], tmp_f[:])
                    if g.degrees:
                        v.tensor_scalar(norm[:, 0], deg[:], 1.0, None, ALU.max)
                        v.tensor_reduce(norm[:, 1], out_count[:].rearrange("p (j l) -> p l j", j=SUB), AX.X, ALU.add)
                        v.drain()
                        v.tensor_scalar(norm[:, 1], norm[:, 1], 1.0, None, ALU.max).then_inc(clipped, 1)
                        v.wait_ge(rooted, 1)
                        v.reciprocal(g.norm_in[:], norm[:, 0])
                        v.reciprocal(g.norm_out[:], norm[:, 1])

                @block.tensor
                def _(pe):
                    pe.wait_ge(have_total, 1)
                    pe.matmul(psum[:, 0:1], C.above[:], total[:], start=True, stop=True).then_inc(have_base, 1)

                @block.scalar
                def _(act):
                    if g.degrees:
                        act.wait_ge(clipped, 1)
                        act.activation(norm[:], norm[:], ACT.Sqrt).then_inc(rooted, 1)

        with phase(nc) as ph:
            rows_i = ph.sb("rows_i", [P, 2, SUB * P], I32)
            rows_f = ph.sb("rows_f", [P, 2, SUB * P])
            hi_i = ph.sb("hi_i", [P, 2, SUB * P], I32)
            hot_t = ph.sb("hot_t", [P, 2, SUB * P])
            oh_lo = ph.sb("oh_lo", [P, 2, SUB, NT])
            picked = ph.sb("picked", [P, 2, SUB, NT])
            junk = ph.sb("junk", [P, P])
            dst_s = ph.sb("dst_s", [P, 2, SUB])
            rank = ph.sb("rank", [P, 2, SUB])
            place_f = ph.sb("place_f", [P, 2, SUB])
            place = ph.sb("place", [P, 2, SUB], I32)
            rec = ph.sb("rec", [P, 2, SUB, 4], I32)
            loop_rec = ph.sb("loop_rec", [P, NT, 4], I32)
            psum = ph.ps("psum", [P, 2, 512])
            rows_in, rows_used = ph.sem_ring("rows_in", 2), ph.sem_ring("rows_used", 2)
            hot_ready, looked_up, rec_ready, rec_sent, rec_free = (ph.sem_ring(n, 2) for n in (
                "hot_ready", "looked_up", "rec_ready", "rec_sent", "rec_free"))
            loops_ready, loops_sent = ph.sem("loops_ready"), ph.sem("loops_sent")
            sp_passed, v_passed, pe_passed, pool_passed = (ph.sem(n) for n in (
                "sp_passed", "v_passed", "pe_passed", "pool_passed"))
            with nc.Block() as block:
                @block.sync
                def _(sp):
                    with sp.Fori(0, TURNS) as i:
                        for s in range(2):
                            hold(sp, rows_used[s], i + 1, sp_passed)
                            sp.dma_start(rows_i[:, s, :],
                                         dst_rows[bass.ds(i * (2 * SUB) + s * SUB, SUB), :]
                                         .rearrange("(o t) q -> o (t q)", o=1)
                                         .broadcast_to([P, SUB * P])).then_inc(rows_in[s], 16)

                @block.vector
                def _(v):
                    for s in range(2):
                        v.sem_inc(rows_used[s], 1)
                    v.memset(rec[:], 1)
                    v.memset(loop_rec[:], 0)
                    v.drain()
                    v.memset(loop_rec[:, :, 2], 2)
                    v.tensor_copy(loop_rec[:, :, 0], C.node_i[:])
                    v.tensor_copy(loop_rec[:, :, 3], C.node_i[:]).then_inc(loops_ready, 1)
                    with v.Fori(0, TURNS) as i:
                        for s in range(2):
                            at = bass.ds(i * (2 * SUB) + s * SUB, SUB)
                            hold(v, rows_in[s], i * 16 + 16, v_passed)
                            v.tensor_scalar(hi_i[:, s], rows_i[:, s], P - 1, None, ALU.bitwise_and)
                            v.tensor_copy(rows_f[:, s], rows_i[:, s]).then_inc(rows_used[s], 1)
                            v.tensor_copy(dst_s[:, s], dst_f[:, at])
                            v.drain()
                            v.tensor_scalar(hot_t[:, s], hi_i[:, s], C.iota_col[:, 0:1], None,
                                            ALU.is_equal).then_inc(hot_ready[s], 1)
                            v.tensor_tensor(oh_lo[:, s], wide(C.iota_row[:, 0:NT], 1, SUB),
                                            wide(dst_lo[:, at], 2, NT), ALU.is_equal)
                            for j in range(SUB):
                                v.scalar_tensor_tensor(junk[:], rows_f[:, s, j * P:(j + 1) * P],
                                                       dst_s[:, s, j:j + 1], C.below[:], ALU.is_equal, ALU.mult,
                                                       accum_out=rank[:, s, j:j + 1])
                                v.drain()
                            hold(v, looked_up[s], i + 1, v_passed)
                            v.tensor_tensor(picked[:, s], oh_lo[:, s],
                                            psum[:, s, 0:SUB * NT].rearrange("p (j l) -> p j l", j=SUB), ALU.mult)
                            v.drain()
                            v.tensor_reduce(place_f[:, s], picked[:, s], AX.X, ALU.add)
                            v.drain()
                            v.tensor_tensor(place_f[:, s], place_f[:, s], rank[:, s], ALU.add)
                            v.drain()
                            hold(v, rec_free[s], i + 1, v_passed)
                            v.tensor_copy(place[:, s], place_f[:, s])
                            v.tensor_copy(rec[:, s, :, 0], src_i[:, at])
                            v.tensor_copy(rec[:, s, :, 1].bitcast(F32), w_f[:, at])
                            v.tensor_copy(rec[:, s, :, 3], dst_i[:, at]).then_inc(rec_ready[s], 1)

                @block.tensor
                def _(pe):
                    with pe.Fori(0, TURNS) as i:
                        for s in range(2):
                            hold(pe, hot_ready[s], i + 1, pe_passed)
                            for j in range(SUB):
                                last = pe.matmul(psum[:, s, j * NT:(j + 1) * NT], hot_t[:, s, j * P:(j + 1) * P],
                                                 offset[:, bass.ds(i * (2 * SUB) + s * SUB + j, 1), :]
                                                 .rearrange("p o l -> p (o l)"), start=True, stop=True)
                            last.then_inc(looked_up[s], 1)

                @block.scalar
                def _(act):
                    for s in range(2):
                        act.sem_inc(rec_free[s], 1)
                    with act.Fori(0, TURNS) as i:
                        for s in range(2):
                            hold(act, rec_sent[s], i * (16 * SUB) + 16 * SUB, rec_free[s])

                @block.gpsimd
                def _(pool):
                    with pool.Fori(0, TURNS) as i:
                        for s in range(2):
                            hold(pool, rec_ready[s], i + 1, pool_passed)
                            for j in range(SUB):
                                pool.indirect_dma_start(
                                    out=g.records, out_offset=bass.IndirectOffsetOnAxis(ap=place[:, s, j:j + 1], axis=0),
                                    in_=rec[:, s, j, :], in_offset=None).then_inc(rec_sent[s], 16)
                    pool.wait_ge(loops_ready, 1)
                    for t in range(NT):
                        pool.indirect_dma_start(
                            out=g.records, out_offset=bass.IndirectOffsetOnAxis(ap=loop_slot[:, t:t + 1], axis=0),
                            in_=loop_rec[:, t, :], in_offset=None).then_inc(loops_sent, 16)
                    pool.wait_ge(loops_sent, 16 * NT)
                    for s in range(2):
                        pool.wait_ge(rec_sent[s], 16 * SUB * TURNS)

    with phase(nc) as ph:
        recs = ph.sb("recs", [P, R * SLOTS, 4], I32)
        row_dst = ph.sb("row_dst", [P, R])
        kind = ph.sb("kind", [P, R * SLOTS])
        ends = ph.sb("ends", [P, 2])
        hit = ph.sb("hit", [P, 2, P])
        has = ph.sb("has", [P, 2])
        same = ph.sb("same", [P, 1])
        psum = ph.ps("psum", [P, 2, P])
        loaded, have_ends, spread = ph.sem("loaded"), ph.sem("have_ends"), ph.sem("spread")
        with nc.Block() as block:
            @block.sync
            def _(sp):
                sp.dma_start(recs[:], g.records.rearrange("(p s) c -> p s c", p=P)).then_inc(loaded, 16)

            @block.tensor
            def _(pe):
                pe.wait_ge(have_ends, 1)
                for k in range(2):
                    last = pe.matmul(psum[:, k], ends[:, k:k + 1].broadcast_to([P, P]), C.ident[:],
                                     start=True, stop=True)
                last.then_inc(spread, 1)

            @block.vector
            def _(v):
                v.wait_ge(loaded, 16)
                v.tensor_copy(row_dst[:], recs[:].rearrange("p (r k) c -> p r k c", k=SLOTS)[:, :, 0, 3])
                v.tensor_copy(kind[:], recs[:, :, 2])
                if g.degrees:
                    v.tensor_copy(g.weight[:].rearrange("p r k -> p (r k)"), recs[:, :, 1].bitcast(F32))
                v.drain()
                v.tensor_copy(ends[:, 0:1], row_dst[:, 0:1])
                v.tensor_copy(ends[:, 1:2], row_dst[:, R - 1:R])
                v.drain()
                v.tensor_tensor(same[:], ends[:, 0:1], ends[:, 1:2], ALU.is_equal).then_inc(have_ends, 1)
                v.tensor_scalar(g.is_edge[:].rearrange("p r k -> p (r k)"), kind[:], 1.0, None, ALU.is_equal)
                v.tensor_scalar(g.is_any[:].rearrange("p r k -> p (r k)"), kind[:], 1.0, None, ALU.is_ge)
                v.memset(g.cont[:, 0:1], 0.0)
                v.tensor_tensor(g.cont[:, 1:R], row_dst[:, 1:R], row_dst[:, 0:R - 1], ALU.is_equal)
                v.memset(g.apart[:, R:R + 1], -APART)
                v.drain()
                v.tensor_scalar(g.apart[:, 0:R], g.cont[:], 1.0, APART, ALU.subtract, ALU.mult)
                for k, into in enumerate((g.in_first, g.in_last)):
                    v.tensor_scalar(into[:], row_dst[:], ends[:, k:k + 1], None, ALU.is_equal)
                    v.drain()
                    v.tensor_scalar(into[:], into[:], 1.0, APART, ALU.subtract, ALU.mult)
                v.wait_ge(spread, 1)
                v.tensor_scalar(hit[:, 0], psum[:, 1], ends[:, 0:1], None, ALU.is_equal)
                v.tensor_scalar(hit[:, 1], psum[:, 0], ends[:, 1:2], None, ALU.is_equal)
                v.drain()
                v.tensor_tensor(hit[:, 0], hit[:, 0], C.below[:], ALU.mult)
                v.tensor_tensor(hit[:, 1], hit[:, 1], C.above[:], ALU.mult)
                v.drain()
                v.tensor_copy(g.carry[:], hit[:, 1])
                v.tensor_scalar(g.from_prev[:], hit[:, 0], 1.0, APART, ALU.subtract, ALU.mult)
                v.tensor_scalar(g.from_next[:], hit[:, 1], 1.0, APART, ALU.subtract, ALU.mult)
                v.tensor_reduce(has[:], hit[:], AX.X, ALU.max)
                v.drain()
                v.tensor_tensor(same[:], same[:], has[:, 1:2], ALU.mult)
                v.drain()
                v.tensor_scalar(same[:], same[:], -1.0, 1.0, ALU.mult, ALU.add)
                v.drain()
                v.tensor_tensor(g.ends_here[:], same[:], has[:, 0:1], ALU.mult)
                for t in range(NT):
                    v.tensor_scalar(g.first_node[:, t:t + 1], ends[:, 0:1], float(P * t), None, ALU.subtract)


class Pass:

    def __init__(self, graph, source, target, feats, cols, heads, slope, score, inner, mask, dead=None):
        self.graph = graph
        self.source = source
        self.target = target
        self.feats = feats
        self.cols = cols
        self.heads = heads
        self.slope = slope
        self.score = score
        self.inner = inner
        self.mask = mask
        self.dead = dead

    def per_head(self, ap):
        if self.inner == "h":
            return ap.rearrange("p a (f h) -> p a f h", h=self.heads)
        return ap.rearrange("p a (h f) -> p a h f", h=self.heads)

    def spread(self, ap):
        each = self.feats // self.heads
        return wide(ap, 2, each) if self.inner == "h" else wide(ap, 3, each)


def edge_pass(nc, C, e, att, finish):
    g, F, H, K = e.graph, e.feats, e.heads, SLOTS
    R = g.R
    W = F + (H if e.score != "weight" else 0)
    RING = 4
    TURNS = R // RING
    assert R % RING == 0
    run_table = nc.dram_tensor(f"run_{Phase.count}", (P * R, W), F32, kind="Internal").ap()
    with ExitStack() as outer:
        n = Phase.count

        def keep(name, shape, dt=F32):
            return outer.enter_context(nc.sbuf_tensor(f"{name}_{n}", shape, dt))

        sums = keep("sums", [P, R, W])
        row_max = keep("row_max", [P, R, H])
        cin = keep("cin", [P, W])

        with phase(nc) as ph:
            stage = ph.sb("stage", [P, RING, K * 4], I32)
            G = ph.sb("G", [P, RING, K, e.cols])
            tcols = F if e.score == "att" else H
            T = ph.sb("T", [P, RING, tcols])
            s_e = ph.sb("s_e", [P, RING, K, H])
            s_x = ph.sb("s_x", [P, RING, K, H])
            prob = ph.sb("prob", [P, RING, K, H])
            lowered = ph.sb("lowered", [P, R, K])
            mixed = ph.sb("mixed", [P, K, F] if e.score == "att" else [P, 1, 1])
            idx_in, gathered, consumed = (ph.sem_ring(n, RING) for n in ("idx_in", "gathered", "consumed"))
            scored, powered = ph.sem_ring("scored", RING), ph.sem_ring("powered", RING)
            sp_passed, pool_passed, v_passed, act_passed = (ph.sem(n) for n in (
                "sp_passed", "pool_passed", "v_passed", "act_passed"))
            idx_view = g.records.rearrange("(p r k) c -> p r (k c)", p=P, k=K)
            per_turn = 16 * (K + (e.score != "weight"))
            with nc.Block() as block:
                @block.sync
                def _(sp):
                    for s in range(RING):
                        sp.dma_start(stage[:, s, :], idx_view[:, s, :]).then_inc(idx_in[s], 16)
                    with sp.Fori(0, TURNS - 1) as i:
                        for s in range(RING):
                            hold(sp, gathered[s], i * per_turn + per_turn, sp_passed)
                            sp.dma_start(stage[:, s, :], idx_view[:, bass.ds(i * RING + (RING + s), 1), :]
                                         .rearrange("p o c -> p (o c)")).then_inc(idx_in[s], 16)

                @block.gpsimd
                def _(pool):
                    with pool.Fori(0, TURNS) as i:
                        for s in range(RING):
                            hold(pool, idx_in[s], i * 16 + 16, pool_passed)
                            hold(pool, consumed[s], i + 1, pool_passed)
                            for k in range(K):
                                pool.indirect_dma_start(
                                    out=G[:, s, k, :], out_offset=None, in_=e.source,
                                    in_offset=bass.IndirectOffsetOnAxis(ap=stage[:, s, 4 * k:4 * k + 1], axis=0)
                                ).then_inc(gathered[s], 16)
                            if e.score != "weight":
                                pool.indirect_dma_start(
                                    out=T[:, s, :], out_offset=None, in_=e.target,
                                    in_offset=bass.IndirectOffsetOnAxis(ap=stage[:, s, 3:4], axis=0)
                                ).then_inc(gathered[s], 16)

                @block.scalar
                def _(act):
                    if e.score != "weight":
                        with act.Fori(0, TURNS) as i:
                            for s in range(RING):
                                hold(act, scored[s], i + 1, act_passed)
                                act.activation(prob[:, s], s_x[:, s], ACT.Exp).then_inc(powered[s], 1)

                @block.vector
                def _(v):
                    for s in range(RING):
                        v.sem_inc(consumed[s], 1)
                    mask = e.mask
                    if e.score != "weight":
                        v.tensor_scalar(lowered[:], mask[:], 1.0, MASKED, ALU.subtract, ALU.mult)
                    v.drain()

                    def score(i, s):
                        r = bass.ds(i * RING + s, 1)
                        hold(v, gathered[s], i * per_turn + per_turn, v_passed)
                        if e.score == "weight":
                            return
                        if e.score == "att":
                            v.tensor_tensor(mixed[:], G[:, s, :, 0:F], wide(T[:, s], 1, K), ALU.add)
                            v.drain()
                            v.scalar_tensor_tensor(mixed[:], mixed[:], e.slope, mixed[:], ALU.mult, ALU.max)
                            v.drain()
                            v.tensor_tensor(mixed[:], mixed[:], wide(att[:], 1, K), ALU.mult)
                            v.drain()
                            v.tensor_reduce(s_e[:, s], mixed[:].rearrange("p k (h f) -> p k h f", h=H), AX.X, ALU.add)
                            v.drain()
                        else:
                            v.tensor_tensor(s_e[:, s], G[:, s, :, F:F + H], wide(T[:, s], 1, K), ALU.add)
                            v.drain()
                            v.scalar_tensor_tensor(s_e[:, s], s_e[:, s], e.slope, s_e[:, s], ALU.mult, ALU.max)
                            v.drain()
                        if e.dead is not None:
                            v.tensor_scalar(s_x[:, s], s_e[:, s], 0.0, e.dead, ALU.is_equal, ALU.mult)
                            v.drain()
                            v.tensor_tensor(s_e[:, s], s_e[:, s], s_x[:, s], ALU.add)
                            v.drain()
                        v.tensor_tensor(s_e[:, s], s_e[:, s], wide(lowered[:, r, :].rearrange("p o k -> p (o k)"), 2, H),
                                        ALU.add)
                        v.drain()
                        v.tensor_reduce(row_max[:, r, :], s_e[:, s].rearrange("p k h -> p h k"), AX.X, ALU.max)
                        v.drain()
                        v.tensor_tensor(s_x[:, s], s_e[:, s],
                                        wide(row_max[:, r, :].rearrange("p o h -> p (o h)"), 1, K),
                                        ALU.subtract).then_inc(scored[s], 1)

                    def weigh(i, s):
                        r = bass.ds(i * RING + s, 1)
                        if e.score == "weight":
                            v.tensor_tensor(G[:, s], G[:, s],
                                            wide(g.weight[:, r, :].rearrange("p o k -> p (o k)"), 2, F), ALU.mult)
                        else:
                            hold(v, powered[s], i + 1, v_passed)
                            v.tensor_tensor(prob[:, s], prob[:, s],
                                            wide(mask[:, r, :].rearrange("p o k -> p (o k)"), 2, H), ALU.mult)
                            v.drain()
                            v.tensor_reduce(sums[:, r, F:W], prob[:, s].rearrange("p k h -> p h k"), AX.X, ALU.add)
                            v.tensor_tensor(e.per_head(G[:, s, :, 0:F]), e.per_head(G[:, s, :, 0:F]),
                                            e.spread(prob[:, s]), ALU.mult)
                        v.drain()
                        v.tensor_reduce(sums[:, r, 0:F], G[:, s, :, 0:F].rearrange("p k f -> p f k"), AX.X,
                                        ALU.add).then_inc(consumed[s], 1)

                    with v.Fori(0, TURNS) as i:
                        score(i, 0)
                        for s in range(1, RING):
                            score(i, s)
                            weigh(i, s - 1)
                        weigh(i, RING - 1)

        with phase(nc) as ph:
            fwd = ph.sb("fwd", [P, R, H])
            bwd = ph.sb("bwd", [P, R, H])
            passed_on = ph.sb("passed_on", [P, 2, H, P])
            edge_max = ph.sb("edge_max", [P, 2, H])
            psum = ph.ps("psum", [P, 2, 512])
            psum_c = ph.ps("psum_c", [P, 512])
            scanned, spread, read, shifted, powered, ran, carried, written = (ph.sem(n) for n in (
                "scanned", "spread", "read", "shifted", "powered", "ran", "carried", "written"))
            PIECES = 4
            with nc.Block() as block:
                @block.vector
                def _(v):
                    if e.score != "weight":
                        for h in range(H):
                            v.tensor_tensor_scan(fwd[:, :, h], g.apart[:, 0:R], row_max[:, :, h], 0.0,
                                                 ALU.add, ALU.max)
                            v.tensor_tensor_scan(bwd[:, R - 1::-1, h], g.apart[:, R:0:-1], row_max[:, R - 1::-1, h],
                                                 0.0, ALU.add, ALU.max)
                        v.drain()
                        v.tensor_copy(edge_max[:, 0], fwd[:, R - 1, :])
                        v.tensor_copy(edge_max[:, 1], bwd[:, 0, :]).then_inc(scanned, 1)
                        v.drain()
                        v.tensor_tensor(fwd[:], fwd[:], bwd[:], ALU.max)
                        v.drain()
                        for h in range(H):
                            v.wait_ge(spread, h + 1)
                            v.tensor_tensor(passed_on[:, 0, h], psum[:, h % 2, 0:P], g.from_prev[:], ALU.add)
                            v.tensor_tensor(passed_on[:, 1, h], psum[:, h % 2, P:2 * P], g.from_next[:],
                                            ALU.add).then_inc(read, 1)
                        v.drain()
                        v.tensor_reduce(edge_max[:], passed_on[:], AX.X, ALU.max)
                        v.drain()
                        for k, inside in enumerate((g.in_first, g.in_last)):
                            for h in range(H):
                                v.scalar_tensor_tensor(fwd[:, :, h], inside[:], edge_max[:, k, h:h + 1], fwd[:, :, h],
                                                       ALU.add, ALU.max)
                            v.drain()
                        v.tensor_tensor(row_max[:], row_max[:], fwd[:], ALU.subtract).then_inc(shifted, 1)
                        v.wait_ge(powered, 1)
                        v.tensor_tensor(sums[:, :, F:W], sums[:, :, F:W], row_max[:], ALU.mult)
                        for k in range(PIECES):
                            rows = slice(k * R // PIECES, (k + 1) * R // PIECES)
                            v.tensor_tensor(e.per_head(sums[:, rows, 0:F]), e.per_head(sums[:, rows, 0:F]),
                                            e.spread(row_max[:, rows, :]), ALU.mult)
                        v.drain()
                    steps = next(u for u in (3, 7, 1) if (R - 1) % u == 0)
                    with v.Fori(0, (R - 1) // steps) as i:
                        for u in range(steps):
                            r0, r1 = bass.ds(i * steps + u, 1), bass.ds(i * steps + u + 1, 1)
                            v.scalar_tensor_tensor(sums[:, r1, :], sums[:, r0, :], g.cont[:, r1], sums[:, r1, :],
                                                   ALU.mult, ALU.add)
                            v.drain()
                    v.sem_inc(ran, 2)
                    v.wait_ge(carried, 1)
                    v.tensor_scalar(cin[:], psum_c[:, 0:W], g.ends_here[:, 0:1], None, ALU.mult)

                @block.scalar
                def _(act):
                    if e.score != "weight":
                        act.wait_ge(shifted, 1)
                        act.activation(row_max[:], row_max[:], ACT.Exp).then_inc(powered, 1)

                @block.tensor
                def _(pe):
                    if e.score != "weight":
                        pe.wait_ge(scanned, 1)
                        for h in range(H):
                            if h >= 2:
                                pe.wait_ge(read, h - 1)
                            for k in range(2):
                                last = pe.matmul(psum[:, h % 2, k * P:(k + 1) * P],
                                                 edge_max[:, k, h:h + 1].broadcast_to([P, P]), C.ident[:],
                                                 start=True, stop=True)
                            last.then_inc(spread, 1)
                    pe.wait_ge(ran, 1)
                    pe.matmul(psum_c[:, 0:W], g.carry[:], sums[:, R - 1, :], start=True, stop=True).then_inc(carried, 1)

                @block.sync
                def _(sp):
                    sp.wait_ge(ran, 1)
                    sp.dma_start(run_table.rearrange("(p r) f -> p r f", p=P), sums[:]).then_inc(written, 16)
                    sp.wait_ge(written, 16)

        with phase(nc) as ph:
            picks = ph.sb("picks", [P, GRP], I32)
            got = ph.sb("got", [P, GRP, W])
            den = ph.sb("den", [P, GRP, max(H, 1)])
            den2 = ph.sb("den2", [P, GRP, max(H, 1)])
            onto = ph.sb("onto", [P, GRP, P])
            psum = ph.ps("psum", [P, GRP, 512])
            picked, landed, onto_ready, added, done = (ph.sem(n) for n in (
                "picked", "landed", "onto_ready", "added", "done"))
            written = ph.sem("written")
            pool_passed, pe_passed, v_passed, sp_passed = (ph.sem(n) for n in (
                "pool_passed", "pe_passed", "v_passed", "sp_passed"))
            free = ph.sem("free")
            with nc.Block() as block:
                @block.gpsimd
                def _(pool):
                    with pool.Fori(0, NG) as i:
                        hold(pool, picked, i + 1, pool_passed)
                        for s in range(GRP):
                            pool.indirect_dma_start(
                                out=got[:, s, :], out_offset=None, in_=run_table,
                                in_offset=bass.IndirectOffsetOnAxis(ap=picks[:, s:s + 1], axis=0)
                            ).then_inc(landed, 16)

                @block.tensor
                def _(pe):
                    with pe.Fori(0, NG) as i:
                        hold(pe, onto_ready, i + 1, pe_passed)
                        for s in range(GRP):
                            last = pe.matmul(psum[:, s, 0:W], onto[:, s], cin[:], start=True, stop=True)
                        last.then_inc(added, 1)

                @block.vector
                def _(v):
                    v.sem_inc(free, 1)
                    with v.Fori(0, NG) as i:
                        tiles = bass.ds(i * GRP, GRP)
                        hold(v, free, i + 1, v_passed)
                        v.tensor_copy(picks[:], g.end_row[:, tiles]).then_inc(picked, 1)
                        v.tensor_tensor(onto[:], wide(C.iota_row[:], 1, GRP), wide(g.first_node[:, tiles], 2, P),
                                        ALU.is_equal).then_inc(onto_ready, 1)
                        hold(v, added, i + 1, v_passed)
                        hold(v, landed, i * (16 * GRP) + 16 * GRP, v_passed)
                        v.tensor_tensor(got[:], got[:], psum[:, :, 0:W], ALU.add)
                        v.drain()
                        if e.score != "weight":
                            v.tensor_scalar(den2[:], got[:, :, F:W], 0.0, None, ALU.is_le)
                            v.drain()
                            v.tensor_tensor(den[:], got[:, :, F:W], den2[:], ALU.add)
                            v.drain()
                            v.reciprocal(den2[:], den[:])
                            v.drain()
                            v.tensor_tensor(e.per_head(got[:, :, 0:F]), e.per_head(got[:, :, 0:F]), e.spread(den2[:]),
                                            ALU.mult)
                            v.drain()
                        finish.vector(v, i, got)
                        v.drain()
                        v.sem_inc(done, 1)

                @block.sync
                def _(sp):
                    with sp.Fori(0, NG) as i:
                        hold(sp, done, i + 1, sp_passed)
                        if finish.store(sp, i, got, written):
                            hold(sp, written, i * 16 + 16, free)
                        else:
                            sp.sem_inc(free, 1)


def node_rows(table, i, cols):
    return table.rearrange("(g t p) f -> g p t f", g=NG, p=P)[bass.ds(i, 1), :, :, 0:cols] \
        .rearrange("o p t f -> (o p) t f")


class ToNodes:

    def __init__(self, C, bias=None):
        self.C, self.bias = C, bias

    def vector(self, v, i, got):
        tiles = bass.ds(i * GRP, GRP)
        if self.bias is not None:
            v.tensor_tensor(got[:, :, 0:D], got[:, :, 0:D], wide(self.bias[:], 1, GRP), ALU.add)
            v.drain()
        v.tensor_tensor(self.C.X[:, tiles, :], self.C.X[:, tiles, :], got[:, :, 0:D], ALU.add)

    def store(self, sp, i, got, written):
        return False


class ToTable:

    def __init__(self, table, cols, bias=None, scale=None, raw=False):
        self.table, self.cols, self.bias, self.scale, self.raw = table, cols, bias, scale, raw

    def vector(self, v, i, got):
        out = got[:, :, 0:self.cols]
        if self.scale is not None:
            v.tensor_tensor(out, out, wide(self.scale[:, bass.ds(i * GRP, GRP)], 2, self.cols), ALU.mult)
            v.drain()
        if self.bias is not None:
            v.tensor_tensor(out, out, wide(self.bias[:], 1, GRP), ALU.add)
            v.drain()
        if not self.raw:
            v.tensor_scalar(out, out, 0.0, None, ALU.max)

    def store(self, sp, i, got, written):
        sp.dma_start(node_rows(self.table, i, self.cols), got[:, :, 0:self.cols]).then_inc(written, 16)
        return True


def turn(nc, C, xT, table=None, cols=D, norm=True, keep_table=None, add=False):
    KB = cols // P
    with phase(nc) as ph:
        rows = ph.sb("rows", [P, GRP, cols])
        stats = ph.sb("stats", [P, GRP, 6])
        mean_var = ph.sb("mean_var", [P, GRP, 2])
        spread = ph.sb("spread", [P, GRP])
        inv = ph.sb("inv", [P, GRP])
        psum = ph.ps("psum", [P, GRP, 512])
        ready, turned, taken, have_var, rooted, stored, loaded = (ph.sem(n) for n in (
            "ready", "turned", "taken", "have_var", "rooted", "stored", "loaded"))
        v_passed, pe_passed, act_passed, sp_passed, free = (ph.sem(n) for n in (
            "v_passed", "pe_passed", "act_passed", "sp_passed", "free"))
        with nc.Block() as block:
            @block.sync
            def _(sp):
                if not norm:
                    with sp.Fori(0, NG) as i:
                        hold(sp, turned, i + 1, sp_passed)
                        sp.dma_start(rows[:], node_rows(table, i, cols)).then_inc(loaded, 16)
                if keep_table is not None:
                    with sp.Fori(0, NG) as i:
                        hold(sp, ready, i + 1, sp_passed)
                        sp.dma_start(node_rows(keep_table, i, cols), rows[:]).then_inc(stored, 16)
                        hold(sp, stored, i * 16 + 16, free)

            @block.vector
            def _(v):
                if keep_table is not None:
                    v.sem_inc(free, 1)
                if norm:
                    with v.Fori(0, NG) as i:
                        tiles = bass.ds(i * GRP, GRP)
                        for s in range(GRP):
                            v.bn_stats(stats[:, s], C.X[:, bass.ds(i * GRP + s, 1), :].rearrange("p o f -> p (o f)"))
                        v.drain()
                        for s in range(GRP):
                            v.bn_aggr(mean_var[:, s], stats[:, s])
                        v.drain()
                        v.tensor_scalar(spread[:], mean_var[:, :, 1], LN_EPS, None, ALU.add).then_inc(have_var, 1)
                        hold(v, rooted, i + 1, v_passed)
                        v.reciprocal(inv[:], spread[:])
                        hold(v, turned, i + 1, v_passed)
                        if keep_table is not None:
                            hold(v, free, i + 1, v_passed)
                        v.tensor_tensor(rows[:], C.X[:, tiles, :], wide(mean_var[:, :, 0], 2, D), ALU.subtract)
                        v.drain()
                        v.tensor_tensor(rows[:], rows[:], wide(inv[:], 2, D), ALU.mult).then_inc(ready, 1)
                        if add:
                            v.drain()
                            v.tensor_tensor(C.X[:, tiles, :], C.X[:, tiles, :], rows[:], ALU.add)
                        v.drain()

            @block.tensor
            def _(pe):
                pe.sem_inc(turned, 1)
                with pe.Fori(0, NG) as i:
                    if norm:
                        hold(pe, ready, i + 1, pe_passed)
                    else:
                        hold(pe, loaded, i * 16 + 16, pe_passed)
                    hold(pe, taken, i + 1, pe_passed)
                    for s in range(GRP):
                        for b in range(KB):
                            last = pe.transpose(psum[:, s, b * P:(b + 1) * P], rows[:, s, b * P:(b + 1) * P],
                                                C.ident[:])
                    last.then_inc(turned, 1)

            @block.scalar
            def _(act):
                act.sem_inc(taken, 1)
                with act.Fori(0, NG) as i:
                    if norm:
                        hold(act, have_var, i + 1, act_passed)
                        act.activation(spread[:], spread[:], ACT.Sqrt).then_inc(rooted, 1)
                    hold(act, turned, i + 2, act_passed)
                    for b in range(KB):
                        last = act.activation(xT[:, b, bass.ds(i * UNIT, UNIT)].rearrange("p (t q) -> p t q", q=P),
                                              psum[:, :, b * P:(b + 1) * P], ACT.Copy)
                    last.then_inc(taken, 1)


def project(nc, C, xT, weight, cols, outputs, K=D, bias=None, post=None, extra=0):
    KB = K // P
    with phase(nc) as ph:
        w = ph.sb("w", [P, KB, cols])
        rows = ph.sb("rows", [P, GRP, cols + extra])
        b = ph.sb("b", [P, cols]) if bias is not None else None
        scratch = ph.sb("scratch", [P, GRP, cols]) if extra else None
        x = ph.sb("x", [P, KB, UNIT])
        staged, act_passed = ph.sem("staged"), ph.sem("act_passed")
        psum = ph.ps("psum", [P, GRP, 512])
        loaded, made, taken, ready, stored = (ph.sem(n) for n in ("loaded", "made", "taken", "ready", "stored"))
        v_passed, pe_passed, sp_passed, free = (ph.sem(n) for n in ("v_passed", "pe_passed", "sp_passed", "free"))
        loads = 16 * (1 + (bias is not None))
        with nc.Block() as block:
            @block.sync
            def _(sp):
                sp.dma_start(w[:], weight.rearrange("(k p) c -> p k c", p=P)).then_inc(loaded, 16)
                if bias is not None:
                    sp.dma_start(b[:], bias.broadcast_to([P, cols])).then_inc(loaded, 16)
                with sp.Fori(0, NG) as i:
                    hold(sp, ready, i + 1, sp_passed)
                    for table, at, n in outputs:
                        sp.dma_start(node_rows(table, i, n), rows[:, :, at:at + n]).then_inc(stored, 16)
                    hold(sp, stored, i * (16 * len(outputs)) + 16 * len(outputs), free)

            @block.tensor
            def _(pe):
                pe.wait_ge(loaded, loads)
                with pe.Fori(0, NG) as i:
                    hold(pe, taken, i + 1, pe_passed)
                    hold(pe, staged, i + 1, pe_passed)
                    for s in range(GRP):
                        for k in range(KB):
                            last = pe.matmul(psum[:, s, 0:cols], x[:, k, s * P:(s + 1) * P], w[:, k, :],
                                             start=(k == 0), stop=(k == KB - 1))
                    last.then_inc(made, 1)

            @block.scalar
            def _(act):
                act.sem_inc(made, 1)
                with act.Fori(0, NG) as i:
                    hold(act, made, i + 1, act_passed)
                    act.activation(x[:], xT[:, :, bass.ds(i * UNIT, UNIT)], ACT.Copy).then_inc(staged, 1)

            @block.vector
            def _(v):
                v.sem_inc(taken, 1)
                v.sem_inc(free, 1)
                v.wait_ge(loaded, loads)
                with v.Fori(0, NG) as i:
                    hold(v, free, i + 1, v_passed)
                    hold(v, made, i + 2, v_passed)
                    if bias is not None:
                        v.tensor_tensor(rows[:, :, 0:cols], psum[:, :, 0:cols], wide(b[:], 1, GRP),
                                        ALU.add).then_inc(taken, 1)
                    else:
                        v.tensor_copy(rows[:, :, 0:cols], psum[:, :, 0:cols]).then_inc(taken, 1)
                    v.drain()
                    if post is not None:
                        post(v, rows, scratch, bass.ds(i * GRP, GRP))
                        v.drain()
                    v.sem_inc(ready, 1)


def load_rows(nc, pairs):
    with phase(nc) as ph:
        loaded = ph.sem("loaded")
        with nc.Block() as block:
            @block.sync
            def _(sp):
                for to, of in pairs:
                    sp.dma_start(to, of).then_inc(loaded, 16)
                sp.wait_ge(loaded, 16 * len(pairs))


def pick_top(v, scratch, score, chosen, E, K):
    before = scratch
    for x in range(E):
        me = score[:, :, x:x + 1]
        if x:
            v.tensor_tensor(before[:, :, 0:x], score[:, :, 0:x], me.broadcast_to([P, NT, x]), ALU.is_ge)
        if x < E - 1:
            v.tensor_tensor(before[:, :, x:E - 1], score[:, :, x + 1:E], me.broadcast_to([P, NT, E - 1 - x]), ALU.is_gt)
        v.drain()
        v.tensor_reduce(chosen[:, :, x], before[:, :, 0:E - 1], AX.X, ALU.add)
        v.drain()
    v.tensor_scalar(chosen[:], chosen[:], float(K), None, ALU.is_lt)
    v.drain()


def choose_experts(nc, C, logits, gates, E, K, among_chosen):
    with phase(nc) as ph:
        top = ph.sb("top", [P, NT])
        scratch = ph.sb("scratch", [P, NT, E])
        chosen = ph.sb("chosen", [P, NT, E])
        prob = ph.sb("prob", [P, NT, E])
        total = ph.sb("total", [P, NT])
        shifted, powered = ph.sem("shifted"), ph.sem("powered")
        with nc.Block() as block:
            @block.scalar
            def _(act):
                act.wait_ge(shifted, 1)
                act.activation(prob[:], prob[:], ACT.Exp).then_inc(powered, 1)

            @block.vector
            def _(v):
                v.tensor_reduce(top[:], logits[:], AX.X, ALU.max)
                v.drain()
                v.tensor_tensor(prob[:], logits[:], wide(top[:], 2, E), ALU.subtract).then_inc(shifted, 1)
                if among_chosen:
                    pick_top(v, scratch, logits, chosen, E, K)
                v.wait_ge(powered, 1)
                if among_chosen:
                    v.tensor_tensor(prob[:], prob[:], chosen[:], ALU.mult)
                    v.drain()
                v.tensor_reduce(total[:], prob[:], AX.X, ALU.add)
                v.drain()
                v.reciprocal(total[:], total[:])
                v.drain()
                v.tensor_tensor(prob[:], prob[:], wide(total[:], 2, E), ALU.mult)
                v.drain()
                if among_chosen:
                    v.tensor_copy(gates[:], prob[:])
                else:
                    pick_top(v, scratch, prob, chosen, E, K)
                    v.tensor_tensor(gates[:], prob[:], chosen[:], ALU.mult)


def logits_of(nc, C, xT, weight, bias, E, logits):
    with phase(nc) as ph:
        w = ph.sb("w", [P, DC, E])
        b = ph.sb("b", [P, E])
        psum = ph.ps("psum", [P, NT, E])
        loaded, made = ph.sem("loaded"), ph.sem("made")
        with nc.Block() as block:
            @block.sync
            def _(sp):
                sp.dma_start(w[:], weight).then_inc(loaded, 16)
                sp.dma_start(b[:], bias.broadcast_to([P, E])).then_inc(loaded, 16)

            @block.tensor
            def _(pe):
                pe.wait_ge(loaded, 32)
                for t in range(NT):
                    for k in range(DC):
                        last = pe.matmul(psum[:, t, :], xT[:, k, t * P:(t + 1) * P], w[:, k, :],
                                         start=(k == 0), stop=(k == DC - 1))
                last.then_inc(made, 1)

            @block.vector
            def _(v):
                v.wait_ge(made, 1)
                v.tensor_tensor(logits[:], psum[:], wide(b[:], 1, NT), ALU.add)


def experts(nc, C, xT, gates, E, H, func, w1, b1, w2, b2):
    HC = H // P
    EB = 2 if E > 1 else 1
    ET = E // EB
    with phase(nc) as ph:
        w1s = ph.sb("w1s", [P, EB, DC, H])
        w2s = ph.sb("w2s", [P, EB, HC, D])
        b1s = ph.sb("b1s", [P, EB, HC])
        b2s = ph.sb("b2s", [1, EB, D])
        hidden = ph.sb("hidden", [P, HC, UNIT])
        psum_h = ph.ps("psum_h", [P, 2, 2, 512])
        YB = 4
        psum_y = ph.ps("psum_y", [P, YB, 512])
        w_in = ph.sem_ring("w_in", EB)
        h_made, h_taken = ph.sem_ring("h_made", 2), ph.sem_ring("h_taken", 2)
        y_made, y_taken, w_used = ph.sem("y_made"), ph.sem("y_taken"), ph.sem_ring("w_used", EB)
        sp_passed, pe_passed, act_passed, v_passed = (ph.sem(n) for n in (
            "sp_passed", "pe_passed", "act_passed", "v_passed"))

        def each_expert(eng, expert):
            if ET > 1:
                with eng.Fori(0, ET) as i:
                    for b in range(EB):
                        expert(i, b)
            else:
                for b in range(EB):
                    expert(0, b)

        with nc.Block() as block:
            @block.sync
            def _(sp):
                def load(i, b):
                    if ET > 1:
                        hold(sp, w_used[b], i + 1, sp_passed)
                    e = i * EB + b
                    sp.dma_start(w1s[:, b], w1[bass.ds(e, 1), :, :].rearrange("o (k p) h -> p (o k) h", p=P)
                                 ).then_inc(w_in[b], 16)
                    sp.dma_start(w2s[:, b], w2[bass.ds(e, 1), :, :].rearrange("o (k p) h -> p (o k) h", p=P)
                                 ).then_inc(w_in[b], 16)
                    sp.dma_start(b1s[:, b], b1[:, bass.ds(e * HC, HC)]).then_inc(w_in[b], 16)
                    sp.dma_start(b2s[:, b], b2[bass.ds(e, 1), :]).then_inc(w_in[b], 16)

                each_expert(sp, load)

            @block.tensor
            def _(pe):
                for b in range(EB):
                    pe.sem_inc(w_used[b], 1)

                def expert(i, b):
                    hold(pe, w_in[b], i * 64 + 64, pe_passed)
                    with pe.Fori(0, NG) as c:
                        u = i * (EB * NG) + b * NG + c
                        for m in range(HC):
                            s = m % 2
                            hold(pe, h_taken[s], u * (HC // 2) + (m // 2 + 1), pe_passed)
                            for half in range(2):
                                for k in range(DC):
                                    last = pe.matmul(psum_h[:, s, half, 0:HALF], w1s[:, b, k, m * P:(m + 1) * P],
                                                     xT[:, k, bass.ds(c * UNIT + half * HALF, HALF)],
                                                     start=(k == 0), stop=(k == DC - 1))
                            last.then_inc(h_made[s], 1)
                        for s in range(2):
                            hold(pe, h_taken[s], u * (HC // 2) + (HC // 2 + 1), pe_passed)
                        for t in range(GRP):
                            before = t - YB if t >= YB else max(q for q in range(GRP) if q % YB == t) - GRP
                            hold(pe, y_taken, u * GRP + (before + 1 + GRP), pe_passed)
                            out = psum_y[:, t % YB, 0:D]
                            for m in range(HC):
                                pe.matmul(out, hidden[:, m, t * P:(t + 1) * P], w2s[:, b, m, :],
                                          start=(m == 0), stop=False)
                            last = pe.matmul(out, C.ones[0:1, :], b2s[0:1, b, :], start=False, stop=True)
                            last.then_inc(y_made, 1)
                    hold(pe, y_made, i * (EB * NT) + (b + 1) * NT, pe_passed)
                    pe.sem_inc(w_used[b], 1)

                each_expert(pe, expert)

            @block.scalar
            def _(act):
                for s in range(2):
                    act.sem_inc(h_taken[s], 1)

                def expert(i, b):
                    hold(act, w_in[b], i * 64 + 64, act_passed)
                    with act.Fori(0, NG) as c:
                        u = i * (EB * NG) + b * NG + c
                        for m in range(HC):
                            s = m % 2
                            hold(act, h_made[s], u * (HC // 2) + (m // 2 + 1), act_passed)
                            act.activation(hidden[:, m].rearrange("p (a n) -> p a n", a=2), psum_h[:, s, :, 0:HALF],
                                           func, bias=b1s[:, b, m:m + 1]).then_inc(h_taken[s], 1)

                each_expert(act, expert)

            @block.vector
            def _(v):
                v.sem_inc(y_taken, GRP)

                def expert(i, b):
                    with v.Fori(0, NG) as c:
                        u = i * (EB * NG) + b * NG + c
                        for t in range(GRP):
                            hold(v, y_made, u * GRP + (t + 1), v_passed)
                            tile = bass.ds(c * GRP + t, 1)
                            v.scalar_tensor_tensor(
                                C.X[:, tile, :], psum_y[:, t % YB:t % YB + 1, 0:D], gates[:, tile, bass.ds(i * EB + b, 1)],
                                C.X[:, tile, :], ALU.mult, ALU.add).then_inc(y_taken, 1)
                        v.drain()

                each_expert(v, expert)


def channel_mix(nc, C, xT, fc_w, fc_b, ch_w, scale, table):
    with phase(nc) as ph:
        w = ph.sb("w", [P, DC, D])
        b = ph.sb("b", [P, DC])
        mix = ph.sb("mix", [P, DC, P])
        hidden = ph.sb("hidden", [P, DC, UNIT])
        rows = ph.sb("rows", [P, GRP, D])
        psum_h = ph.ps("psum_h", [P, DC, 2, 512])
        psum_y = ph.ps("psum_y", [P, 3, 2, D])
        zeroed, loaded, made, hid, mixed, ready, stored = (ph.sem(n) for n in (
            "zeroed", "loaded", "made", "hid", "mixed", "ready", "stored"))
        sp_passed, pe_passed, act_passed, v_passed, free = (ph.sem(n) for n in (
            "sp_passed", "pe_passed", "act_passed", "v_passed", "free"))
        CH = D // 4
        with nc.Block() as block:
            @block.sync
            def _(sp):
                sp.wait_ge(zeroed, 1)
                sp.dma_start(w[:], fc_w.rearrange("(k p) c -> p k c", p=P)).then_inc(loaded, 16)
                sp.dma_start(b[:], fc_b).then_inc(loaded, 16)
                for m in range(DC):
                    for c in range(2):
                        sp.dma_start(mix[c * CH:(c + 1) * CH, m, c * CH:(c + 1) * CH], ch_w[2 * m + c]).then_inc(loaded, 16)
                with sp.Fori(0, NG) as i:
                    hold(sp, ready, i + 2, sp_passed)
                    sp.dma_start(node_rows(table, i, D), rows[:]).then_inc(stored, 16)
                    hold(sp, stored, i * 16 + 16, free)

            @block.tensor
            def _(pe):
                pe.wait_ge(loaded, 96)
                with pe.Fori(0, NG) as i:
                    hold(pe, hid, i + 1, pe_passed)
                    for m in range(DC):
                        for half in range(2):
                            for k in range(DC):
                                last = pe.matmul(psum_h[:, m, half, 0:HALF], w[:, k, m * P:(m + 1) * P],
                                                 xT[:, k, bass.ds(i * UNIT + half * HALF, HALF)],
                                                 start=(k == 0), stop=(k == DC - 1))
                    last.then_inc(made, 1)
                    hold(pe, hid, i + 2, pe_passed)
                    hold(pe, ready, i + 1, pe_passed)
                    for t in range(GRP):
                        for m in range(DC):
                            last = pe.matmul(psum_y[:, t // 2, t % 2, m * P:(m + 1) * P], hidden[:, m, t * P:(t + 1) * P],
                                             mix[:, m, :], start=True, stop=True)
                    last.then_inc(mixed, 1)

            @block.scalar
            def _(act):
                act.sem_inc(hid, 1)
                with act.Fori(0, NG) as i:
                    hold(act, made, i + 1, act_passed)
                    for m in range(DC):
                        last = act.activation(hidden[:, m].rearrange("p (a n) -> p a n", a=2), psum_h[:, m, :, 0:HALF],
                                              ACT.Identity, bias=b[:, m:m + 1])
                    last.then_inc(hid, 1)

            @block.vector
            def _(v):
                v.memset(mix[:], 0.0).then_inc(zeroed, 1)
                v.sem_inc(ready, 1)
                v.sem_inc(free, 1)
                with v.Fori(0, NG) as i:
                    hold(v, mixed, i + 1, v_passed)
                    hold(v, free, i + 1, v_passed)
                    flat = psum_y[:].rearrange("p a b f -> p (a b) f")[:, 0:GRP, :]
                    v.tensor_tensor(rows[:], flat, wide(scale[:, bass.ds(i * GRP, GRP)], 2, D), ALU.mult)
                    v.drain()
                    v.sem_inc(ready, 1)


def add_product(nc, C, xT, weight, bias=None):
    with phase(nc) as ph:
        w = ph.sb("w", [P, DC, D])
        b = ph.sb("b", [P, D])
        x = ph.sb("x", [P, DC, UNIT])
        staged, act_passed = ph.sem("staged"), ph.sem("act_passed")
        psum = ph.ps("psum", [P, GRP, 512])
        loaded, made, taken = ph.sem("loaded"), ph.sem("made"), ph.sem("taken")
        v_passed, pe_passed = ph.sem("v_passed"), ph.sem("pe_passed")
        loads = 16 * (1 + (bias is not None))
        with nc.Block() as block:
            @block.sync
            def _(sp):
                sp.dma_start(w[:], weight.rearrange("(k p) c -> p k c", p=P)).then_inc(loaded, 16)
                if bias is not None:
                    sp.dma_start(b[:], bias.broadcast_to([P, D])).then_inc(loaded, 16)

            @block.tensor
            def _(pe):
                pe.wait_ge(loaded, loads)
                with pe.Fori(0, NG) as i:
                    hold(pe, taken, i + 1, pe_passed)
                    hold(pe, staged, i + 1, pe_passed)
                    for s in range(GRP):
                        for k in range(DC):
                            last = pe.matmul(psum[:, s, 0:D], x[:, k, s * P:(s + 1) * P], w[:, k, :],
                                             start=(k == 0), stop=(k == DC - 1))
                    last.then_inc(made, 1)

            @block.scalar
            def _(act):
                act.sem_inc(made, 1)
                with act.Fori(0, NG) as i:
                    hold(act, made, i + 1, act_passed)
                    act.activation(x[:], xT[:, :, bass.ds(i * UNIT, UNIT)], ACT.Copy).then_inc(staged, 1)

            @block.vector
            def _(v):
                v.sem_inc(taken, 1)
                v.wait_ge(loaded, loads)
                with v.Fori(0, NG) as i:
                    tiles = bass.ds(i * GRP, GRP)
                    hold(v, made, i + 2, v_passed)
                    v.tensor_tensor(C.X[:, tiles, :], C.X[:, tiles, :], psum[:, :, 0:D], ALU.add).then_inc(taken, 1)
                    v.drain()
                    if bias is not None:
                        v.tensor_tensor(C.X[:, tiles, :], C.X[:, tiles, :], wide(b[:], 1, GRP), ALU.add)
                        v.drain()


def take_top_nodes(nc, C, weights, gates, K):
    table = nc.dram_tensor("router_weights", (NT, P), F32, kind="Internal").ap()
    with phase(nc) as ph:
        row = ph.sb("row", [P, NP])
        junk = ph.sb("junk", [P, NP])
        rank = ph.sb("rank", [P, 4, NT])
        total = ph.sb("total", [P, NT])
        turned = ph.sb("turned", [NT, P])
        psum = ph.ps("psum", [P, 512])
        turned_in, copied, stored, spread = (ph.sem(n) for n in ("turned_in", "copied", "stored", "spread"))
        with nc.Block() as block:
            @block.tensor
            def _(pe):
                pe.transpose(psum[0:NT, 0:P], weights[:, :, 0], C.ident[:]).then_inc(turned_in, 1)

            @block.sync
            def _(sp):
                sp.wait_ge(copied, 1)
                sp.dma_start(table, turned[:]).then_inc(stored, 16)
                sp.wait_ge(stored, 16)
                sp.dma_start(row[:], table.rearrange("(o t) q -> o (t q)", o=1).broadcast_to([P, NP])).then_inc(spread, 16)

            @block.vector
            def _(v):
                v.memset(rank[:], 0.0)
                v.wait_ge(turned_in, 1)
                v.tensor_copy(turned[:], psum[0:NT, 0:P]).then_inc(copied, 1)
                v.wait_ge(spread, 16)
                v.drain()

                def count(k, t, lo, hi, op, by):
                    v.scalar_tensor_tensor(junk[:, lo:hi], row[:, lo:hi], weights[:, t, 0:1], by, op, ALU.mult,
                                           accum_out=rank[:, k, t:t + 1])
                    v.drain()

                for t in range(NT):
                    at, end = t * P, min((t + 1) * P, N)
                    if at:
                        count(0, t, 0, at, ALU.is_ge, C.ones[:, 0:1].broadcast_to([P, at]))
                    if end < N:
                        count(1, t, end, N, ALU.is_gt, C.ones[:, 0:1].broadcast_to([P, N - end]))
                    count(2, t, at, end, ALU.is_gt, C.ones[:, 0:end - at])
                    count(3, t, at, end, ALU.is_equal, C.below[:, 0:end - at])
                v.tensor_reduce(total[:], rank[:].rearrange("p k t -> p t k"), AX.X, ALU.add)
                v.drain()
                v.scalar_tensor_tensor(gates[:, :, 0], total[:], float(K), weights[:, :, 0], ALU.is_lt, ALU.mult)


def score_experts(nc, C, table, b_gat, gamma, beta, logits):
    F, E = 16, 4
    with phase(nc) as ph:
        agg = ph.sb("agg", [P, NT, F])
        sq = ph.sb("sq", [P, NT, F])
        rows = ph.sb("rows", [P, 3, F])
        mean = ph.sb("mean", [P, NT])
        var = ph.sb("var", [P, NT])
        loaded, have_var, rooted = ph.sem("loaded"), ph.sem("have_var"), ph.sem("rooted")
        with nc.Block() as block:
            @block.sync
            def _(sp):
                sp.dma_start(agg[:], table.rearrange("(t p) f -> p t f", p=P)).then_inc(loaded, 16)
                for k, of in enumerate((b_gat, gamma, beta)):
                    sp.dma_start(rows[:, k, :], of.broadcast_to([P, F])).then_inc(loaded, 16)

            @block.scalar
            def _(act):
                act.wait_ge(have_var, 1)
                act.activation(var[:], var[:], ACT.Sqrt).then_inc(rooted, 1)

            @block.vector
            def _(v):
                v.wait_ge(loaded, 64)
                v.tensor_tensor(agg[:], agg[:], wide(rows[:, 0], 1, NT), ALU.add)
                v.drain()
                v.tensor_reduce(mean[:], agg[:], AX.X, ALU.add)
                v.drain()
                v.tensor_scalar(mean[:], mean[:], 1.0 / F, None, ALU.mult)
                v.drain()
                v.tensor_tensor(agg[:], agg[:], wide(mean[:], 2, F), ALU.subtract)
                v.drain()
                v.tensor_tensor(sq[:], agg[:], agg[:], ALU.mult)
                v.drain()
                v.tensor_reduce(var[:], sq[:], AX.X, ALU.add)
                v.drain()
                v.tensor_scalar(var[:], var[:], 1.0 / F, LN_EPS, ALU.mult, ALU.add).then_inc(have_var, 1)
                v.wait_ge(rooted, 1)
                v.reciprocal(mean[:], var[:])
                v.drain()
                v.tensor_tensor(agg[:], agg[:], wide(mean[:], 2, F), ALU.mult)
                v.drain()
                v.tensor_tensor(agg[:], agg[:], wide(rows[:, 1], 1, NT), ALU.mult)
                v.drain()
                v.tensor_tensor(agg[:], agg[:], wide(rows[:, 2], 1, NT), ALU.add)
                v.drain()
                v.tensor_reduce(logits[:], agg[:].rearrange("p t (h e) -> p t e h", e=E), AX.X, ALU.add)
                v.drain()
                v.tensor_scalar(logits[:], logits[:], E / F, None, ALU.mult)


def build(nc, a, out, layers=8):
    class C:
        pass

    with ExitStack() as ctx:
        def sb(name, shape, dt=F32):
            return ctx.enter_context(nc.sbuf_tensor(name, shape, dt))

        def dram(name, shape):
            return nc.dram_tensor(name, shape, F32, kind="Internal").ap()

        C.X = sb("node_features", [P, NT, D])
        C.ident, C.ones, C.below, C.above, C.iota_row = (
            sb(n, [P, P]) for n in ("ident", "ones", "below", "above", "iota_row"))
        C.iota_col = sb("iota_col", [P, 1])
        C.node_i = sb("node_i", [P, NT], I32)
        build_constants(nc, C, a["x"])
        main = Graph(nc, sb, "main", a["dst_rows"].shape[0], 124, True)
        sort_edges(nc, C, main, a["dst_rows"], a["dst_cols"], a["src_cols"], a["w_cols"])

        def store_and_stop():
            with phase(nc) as ph:
                sent = ph.sem("sent")
                with nc.Block() as block:
                    @block.sync
                    def _(sp):
                        sp.dma_start(out[0:(NT - 1) * P, :].rearrange("(t p) f -> p t f", p=P),
                                     C.X[:, 0:NT - 1, :]).then_inc(sent, 16)
                        sp.dma_start(out[(NT - 1) * P:N, :], C.X[0:N - (NT - 1) * P, NT - 1, :]).then_inc(sent, 16)
                        sp.wait_ge(sent, 32)

        @contextmanager
        def turned(cols=D, **kw):
            with nc.sbuf_tensor(f"xT_{Phase.count}", [P, cols // P, NP], F32) as xT:
                turn(nc, C, xT, cols=cols, **kw)
                yield xT

        @contextmanager
        def rows(*shapes):
            with ExitStack() as c:
                n = Phase.count
                yield [c.enter_context(nc.sbuf_tensor(f"row{k}_{n}", list(s), F32)) for k, s in enumerate(shapes)]

        def moe(xT, layer, gates, E, H, func):
            experts(nc, C, xT, gates, E, H, func, *(a[f"L{layer}_ffn_{n}"] for n in ("w1", "b1", "w2", "b2")))

        source, target = dram("l0_source", (NP, D + 4)), dram("l0_target", (NP, 4))
        with turned() as xT, rows((P, 2, D)) as (att,):
            load_rows(nc, [(att[:, k, :], a["L0_gnn_att"][k:k + 1, :].broadcast_to([P, D])) for k in range(2)])

            def scores(v, r, scratch, tiles):
                for k in range(2):
                    v.tensor_tensor(scratch[:], r[:, :, 0:D], wide(att[:, k], 1, GRP), ALU.mult)
                    v.drain()
                    v.tensor_reduce(r[:, :, D + 4 * k:D + 4 * k + 4],
                                    scratch[:].rearrange("p t (h f) -> p t h f", h=4), AX.X, ALU.add)
                    v.drain()

            project(nc, C, xT, a["L0_gnn_W"], D, [(source, 0, D + 4), (target, D + 4, 4)], post=scores, extra=8)
        edge_pass(nc, C, Pass(main, source, target, D, D + 4, 4, 0.01, "sum", "f", main.is_edge, dead=-1000.0),
                  None, ToNodes(C))
        if layers == 1:
            return store_and_stop()

        with turned() as xT, rows((P, NT, 8), (P, NT, 8)) as (logits, gates):
            logits_of(nc, C, xT, a["L0_ffn_gate_w"], a["L0_ffn_gate_b"], 8, logits)
            choose_experts(nc, C, logits, gates, 8, 2, False)
            moe(xT, 0, gates, 8, 512, ACT.Gelu)
        if layers == 2:
            return store_and_stop()

        source, target = dram("l1_source", (NP, D + 8)), dram("l1_target", (NP, 8))
        with turned(keep_table=source) as xT:
            project(nc, C, xT, a["L1_gnn_W"], 16, [(source[:, D:D + 8], 0, 8), (target, 8, 8)], bias=a["L1_gnn_b"])
        edge_pass(nc, C, Pass(main, source, target, D, D + 8, 8, 0.2, "sum", "h", main.is_edge), None, ToNodes(C))
        if layers == 3:
            return store_and_stop()

        with turned(add=True) as xT, rows((P, NT, 1), (P, NT, 1)) as (weights, gates):
            logits_of(nc, C, xT, a["L1_ffn_wr"], a["L1_ffn_br"], 1, weights)
            take_top_nodes(nc, C, weights, gates, max(1, N // 2) - 1)
            moe(xT, 1, gates, 1, 1024, ACT.Gelu_apprx_tanh)
        if layers == 4:
            return store_and_stop()

        mixed, conv = dram("l2_mixed", (NP, D)), dram("l2_conv", (NP, D))
        for step in range(3):
            with (turned() if step == 0 else turned(table=conv, norm=False)) as xT:
                if step:
                    add_product(nc, C, xT, a["L2_gnn_mlp_w"][(step - 1) * D:step * D, :])
                channel_mix(nc, C, xT, a["L2_gnn_fc_w"][step], a["L2_gnn_fc_b"][:, step * DC:(step + 1) * DC],
                            a["L2_gnn_ch_w"][step], main.norm_out, mixed)
            with rows((P, D)) as (bias,):
                load_rows(nc, [(bias[:], a["L2_gnn_ch_b"][step:step + 1, :].broadcast_to([P, D]))])
                edge_pass(nc, C, Pass(main, mixed, None, D, D, 1, None, "weight", "f", None), None,
                          ToTable(conv, D, bias=bias, scale=main.norm_in))
        with turned(table=conv, norm=False) as xT:
            add_product(nc, C, xT, a["L2_gnn_mlp_w"][2 * D:3 * D, :], bias=a["L2_gnn_mlp_b"])
        if layers == 5:
            return store_and_stop()

        source, target, agg = dram("l2_source", (NP, 20)), dram("l2_target", (NP, 4)), dram("l2_agg", (NP, 16))
        with turned() as xT, rows((P, NT, 4), (P, NT, 4)) as (logits, gates):
            with ExitStack() as gc:
                route = Graph(nc, lambda n, s, d: gc.enter_context(nc.sbuf_tensor(n, s, d)), "route",
                              a["route_dst_rows"].shape[0], 92, False)
                sort_edges(nc, C, route, a["route_dst_rows"], a["route_dst_cols"], a["route_src_cols"], None)
                with rows((P, 2, 16)) as (att,):
                    load_rows(nc, [(att[:, k, :], a["L2_ffn_att"][k:k + 1, :].broadcast_to([P, 16])) for k in range(2)])

                    def scores(v, r, scratch, tiles):
                        for k in range(2):
                            v.tensor_tensor(scratch[:], r[:, :, 0:16], wide(att[:, k], 1, GRP), ALU.mult)
                            v.drain()
                            v.tensor_reduce(r[:, :, 16 + 4 * k:20 + 4 * k],
                                            scratch[:].rearrange("p t (h f) -> p t h f", h=4), AX.X, ALU.add)
                            v.drain()

                    project(nc, C, xT, a["L2_ffn_W_gat"], 16, [(source, 0, 20), (target, 20, 4)], post=scores, extra=8)
                edge_pass(nc, C, Pass(route, source, target, 16, 20, 4, 0.2, "sum", "f", route.is_any), None,
                          ToTable(agg, 16, raw=True))
            score_experts(nc, C, agg, a["L2_ffn_b_gat"], a["L2_ffn_ln_gamma"], a["L2_ffn_ln_beta"], logits)
            choose_experts(nc, C, logits, gates, 4, 2, True)
            moe(xT, 2, gates, 4, 512, ACT.Gelu)
        if layers == 6:
            return store_and_stop()

        pairs = [[dram(f"l3_{side}{k}", (NP, D)) for k in range(2)] for side in ("left", "right")]
        hidden = dram("l3_hidden", (NP, 2 * D))
        with turned() as xT:
            for side, name in enumerate(("W1l", "W1r")):
                project(nc, C, xT, a[f"L3_gnn_{name}"], 2 * D, [(pairs[side][k], k * D, D) for k in range(2)])
        for k in range(2):
            with rows((P, D), (P, D)) as (att, bias):
                load_rows(nc, [(att[:], a["L3_gnn_a1"][k:k + 1, :].broadcast_to([P, D])),
                               (bias[:], a["L3_gnn_b1"][k:k + 1, :].broadcast_to([P, D]))])
                edge_pass(nc, C, Pass(main, pairs[0][k], pairs[1][k], D, D, 2, 0.2, "att", "f", main.is_any), att,
                          ToTable(hidden[:, k * D:(k + 1) * D], D, bias=bias))
        with turned(cols=2 * D, table=hidden, norm=False) as xT:
            for side, name in enumerate(("W2l", "W2r")):
                project(nc, C, xT, a[f"L3_gnn_{name}"], D, [(pairs[side][0], 0, D)], K=2 * D)
        with rows((P, D), (P, D)) as (att, bias):
            load_rows(nc, [(att[:], a["L3_gnn_a2"].broadcast_to([P, D])), (bias[:], a["L3_gnn_b2"].broadcast_to([P, D]))])
            edge_pass(nc, C, Pass(main, pairs[0][0], pairs[1][0], D, D, 1, 0.2, "att", "f", main.is_any), att,
                      ToNodes(C, bias))
        if layers == 7:
            return store_and_stop()

        with turned() as xT, rows((P, NT, 8), (P, NT, 8)) as (logits, gates):
            logits_of(nc, C, xT, a["L3_ffn_Wg"], a["L3_ffn_bg"], 8, logits)
            choose_experts(nc, C, logits, gates, 8, 2, True)
            moe(xT, 3, gates, 8, 1024, ACT.Relu)
        store_and_stop()


LAYERS = 8


def edge_lists(src, dst):
    tiles = -(-len(dst) // (8 * P)) * 8
    pad = (0, tiles * P - len(dst))
    src, dst = (np.pad(v, pad, constant_values=NP - 1).reshape(tiles, P) for v in (src, dst))
    return dst, np.ascontiguousarray(dst.T), np.ascontiguousarray(src.T)


def kernel(**inputs):
    import concourse.bacc as bacc
    from concourse.bass_utils import run_bass_kernel_spmd

    i = {k: np.asarray(v) for k, v in inputs.items()}

    def columns(b):
        return b.reshape(-1, P).T

    def blocks(w):
        return w.reshape(DC, P, -1).transpose(1, 0, 2)

    a = {"x": i["x"]}
    a["dst_rows"], a["dst_cols"], a["src_cols"] = edge_lists(i["src"], i["dst"])
    tiles = a["dst_rows"].shape[0]
    a["w_cols"] = np.pad(i["edge_weight"], (0, tiles * P - len(i["dst"]))).reshape(tiles, P).T
    a["route_dst_rows"], a["route_dst_cols"], a["route_src_cols"] = edge_lists(*i["L2_ffn_edge_index"])
    a["L0_gnn_W"] = i["L0_gnn_W"].transpose(1, 0, 2).reshape(D, D)
    a["L0_gnn_att"] = i["L0_gnn_att"].reshape(4, 2, 64).transpose(1, 0, 2).reshape(2, D)
    a["L0_ffn_gate_w"] = blocks(i["L0_ffn_gate_w"])
    a["L0_ffn_gate_b"] = i["L0_ffn_gate_b"].reshape(1, 8)
    for layer, names in ((0, ("W1", "b1", "W2", "b2")), (1, ("w1", "b1", "w2", "b2")),
                         (2, ("W1", "b1", "W2", "b2")), (3, ("W1", "b1", "W2", "b2"))):
        w1, b1, w2, b2 = (i[f"L{layer}_ffn_{n}"] for n in names)
        if layer == 1:
            w1, w2 = w1[None], w2[None]
        if layer == 3:
            w1, w2 = w1.transpose(0, 2, 1), w2.transpose(0, 2, 1)
        a[f"L{layer}_ffn_w1"], a[f"L{layer}_ffn_w2"] = w1, w2
        a[f"L{layer}_ffn_b1"], a[f"L{layer}_ffn_b2"] = columns(b1), b2.reshape(-1, D)
    a["L1_gnn_W"] = np.concatenate([i["L1_gnn_W_u"], i["L1_gnn_W_v"]]).T
    a["L1_gnn_b"] = np.pad(i["L1_gnn_b_u"], (0, 8)).reshape(1, 16)
    a["L1_ffn_wr"] = blocks(i["L1_ffn_wr"])
    a["L1_ffn_br"] = i["L1_ffn_br"].reshape(1, 1)
    a["L2_gnn_fc_w"] = i["L2_gnn_fc_w"].transpose(0, 2, 1)
    a["L2_gnn_fc_b"] = columns(i["L2_gnn_fc_b"])
    a["L2_gnn_ch_w"] = i["L2_gnn_ch_w"]
    a["L2_gnn_ch_b"] = i["L2_gnn_ch_b"].reshape(3, D)
    a["L2_gnn_mlp_w"] = i["L2_gnn_mlp_w"].T
    a["L2_gnn_mlp_b"] = i["L2_gnn_mlp_b"].reshape(1, D)
    a["L2_ffn_W_gat"] = i["L2_ffn_W_gat"]
    a["L2_ffn_att"] = np.stack([i["L2_ffn_att_src"].reshape(16), i["L2_ffn_att_dst"].reshape(16)])
    for n in ("b_gat", "ln_gamma", "ln_beta"):
        a[f"L2_ffn_{n}"] = i[f"L2_ffn_{n}"].reshape(1, 16)
    for n in ("W1l", "W1r", "W2l", "W2r"):
        a[f"L3_gnn_{n}"] = i[f"L3_gnn_{n}"]
    a["L3_gnn_a1"] = i["L3_gnn_a1"].reshape(2, D)
    a["L3_gnn_b1"] = i["L3_gnn_b1"].reshape(2, D)
    a["L3_gnn_a2"] = i["L3_gnn_a2"].reshape(1, D)
    a["L3_gnn_b2"] = i["L3_gnn_b2"].reshape(1, D)
    a["L3_ffn_Wg"] = blocks(i["L3_ffn_Wg"].T)
    a["L3_ffn_bg"] = i["L3_ffn_bg"].reshape(1, 8)

    nc = bacc.Bacc("TRN2", target_bir_lowering=False, num_devices=1)
    arrays = {f"in_{k}": np.ascontiguousarray(v) for k, v in a.items()}
    aps = {k: nc.dram_tensor(f"in_{k}", arrays[f"in_{k}"].shape, mybir.dt.from_np(arrays[f"in_{k}"].dtype),
                             kind="ExternalInput").ap() for k in a}
    out = nc.dram_tensor("out", (N, D), F32, kind="ExternalOutput").ap()
    build(nc, aps, out, LAYERS)
    result = run_bass_kernel_spmd(nc, [arrays], core_ids=[0])
    return result.results[0]["out"]
```

```python
from contextlib import ExitStack, contextmanager

import numpy as np

import concourse.bass as bass
from concourse import mybir

F32 = mybir.dt.float32
BF16 = mybir.dt.bfloat16
F32R = mybir.dt.float32r
I32 = mybir.dt.int32
ALU = mybir.AluOpType
ACT = mybir.ActivationFunctionType
AX = mybir.AxisListType

P = 128
D = 256
N = 3125
NT = -(-N // P)
NP = NT * P
GRP = 5
NG = NT // GRP
SLOTS = 4
DC = D // P
UNIT = GRP * P
HALF = UNIT // 2
LN_EPS = 1e-5
MASKED = 1e30
APART = 1e38
TAB = D + 8


class Phase:

    count = 0

    def __init__(self, nc, ctx):
        self.nc, self.ctx, self.sems = nc, ctx, []
        Phase.count += 1
        self.n = Phase.count

    def sb(self, name, shape, dt=F32):
        return self.ctx.enter_context(self.nc.sbuf_tensor(f"{name}_{self.n}", shape, dt))

    def ps(self, name, shape, dt=F32):
        return self.ctx.enter_context(self.nc.psum_tensor(f"{name}_{self.n}", shape, dt))

    def sem(self, name):
        self.sems.append(self.nc.alloc_semaphore(f"{name}_{self.n}"))
        return self.sems[-1]

    def sem_ring(self, name, n):
        return [self.sem(f"{name}{i}") for i in range(n)]


@contextmanager
def phase(nc):
    with ExitStack() as ctx:
        ph = Phase(nc, ctx)
        yield ph
        nc.clear_and_free_semaphores(ph.sems)
        nc.all_engine_barrier()


def hold(eng, sem, value, passed):
    eng.wait_ge(sem, value)
    eng.sem_inc(passed, 1)


def wide(ap, dim, n):
    ap = ap.unsqueeze(dim)
    shape = list(ap.shape)
    shape[dim] = n
    return ap.broadcast_to(shape)


def build_constants(nc, C, x):
    with phase(nc) as ph:
        loaded, filled, made = ph.sem("loaded"), ph.sem("filled"), ph.sem("made")
        iota_i = ph.sb("iota_i", [P, P], I32)
        col_i = ph.sb("col_i", [P, 1], I32)
        with nc.Block() as block:
            @block.sync
            def _(sp):
                sp.wait_ge(filled, 1)
                sp.dma_start(C.X[:, 0:NT - 1, :],
                             x[0:(NT - 1) * P, :].rearrange("(t p) f -> p t f", p=P)).then_inc(loaded, 16)
                sp.dma_start(C.X[0:N - (NT - 1) * P, NT - 1, :], x[(NT - 1) * P:N, :]).then_inc(loaded, 16)
                sp.wait_ge(loaded, 32)

            @block.vector
            def _(v):
                v.memset(C.X[:, NT - 1, :], 0.0).then_inc(filled, 1)
                v.memset(C.ones[:], 1.0)
                v.wait_ge(made, 9)
                v.tensor_copy(C.iota_row[:], iota_i[:])
                v.tensor_copy(C.iota_col[:], col_i[:])

            @block.gpsimd
            def _(pool):
                pool.memset(C.ident[:], 0.0).then_inc(made, 1)
                pool.memset(C.below[:], 1.0).then_inc(made, 1)
                pool.memset(C.above[:], 1.0).then_inc(made, 1)
                pool.wait_ge(made, 3)
                pool.affine_select(out=C.ident[:], in_=C.ident[:], compare_op=ALU.not_equal, fill=1.0,
                                   base=0, pattern=[[-1, P]], channel_multiplier=1).then_inc(made, 1)
                pool.affine_select(out=C.below[:], in_=C.below[:], compare_op=ALU.is_gt, fill=0.0,
                                   base=0, pattern=[[-1, P]], channel_multiplier=1).then_inc(made, 1)
                pool.affine_select(out=C.above[:], in_=C.above[:], compare_op=ALU.is_gt, fill=0.0,
                                   base=0, pattern=[[1, P]], channel_multiplier=-1).then_inc(made, 1)
                pool.iota(iota_i[:], pattern=[[1, P]], base=0, channel_multiplier=0).then_inc(made, 1)
                pool.iota(col_i[:], pattern=[[0, 1]], base=0, channel_multiplier=1).then_inc(made, 1)
                pool.iota(C.node_i[:], pattern=[[P, NT]], base=0, channel_multiplier=1).then_inc(made, 1)


class Graph:

    def __init__(self, nc, sb, name, tiles, degrees):
        rows = -(-(tiles * P + NP * SLOTS) // (P * SLOTS))
        self.name, self.T, self.R = name, tiles, rows
        self.records = nc.dram_tensor(f"records_{name}", (P * rows * SLOTS, 4), I32, kind="Internal").ap()
        self.cont = sb(f"cont_{name}", [P, rows], F32)
        self.apart = sb(f"apart_{name}", [P, rows + 1], F32)
        self.in_first = sb(f"in_first_{name}", [P, rows], F32)
        self.in_last = sb(f"in_last_{name}", [P, rows], F32)
        self.carry = sb(f"carry_{name}", [P, P], F32)
        self.from_prev = sb(f"from_prev_{name}", [P, P], F32)
        self.from_next = sb(f"from_next_{name}", [P, P], F32)
        self.ends_here = sb(f"ends_here_{name}", [P, 1], F32)
        self.first_node = sb(f"first_node_{name}", [P, NT], F32)
        self.end_row = sb(f"end_row_{name}", [P, NT], I32)
        self.is_edge = sb(f"is_edge_{name}", [P, rows, SLOTS], F32)
        self.is_any = sb(f"is_any_{name}", [P, rows, SLOTS], F32)
        if degrees:
            self.weight = sb(f"weight_{name}", [P, rows, SLOTS + 1], F32)
            self.norm_in = sb(f"norm_in_{name}", [P, NT], F32)
            self.norm_out = sb(f"norm_out_{name}", [P, NT], F32)
        self.degrees = degrees


def sort_edges(nc, C, g, dst_rows, dst_cols, src_cols, w_cols):
    T, R = g.T, g.R
    COUNT = max(s for s in range(1, 512 // NT + 1) if T % (2 * s) == 0)
    PLACE = max(s for s in range(1, 9) if T % (2 * s) == 0)
    with ExitStack() as outer:
        def keep(name, shape, dt=F32):
            return outer.enter_context(nc.sbuf_tensor(f"{name}_{g.name}", shape, dt))

        counts = keep("counts", [P, T, NT])
        offset = keep("offset", [P, T, NT])
        dst_i = keep("dst_i", [P, T], I32)
        src_i = keep("src_i", [P, T], I32)
        w_f = keep("w_f", [P, T])
        dst_f = keep("dst_f", [P, T])
        dst_lo = keep("dst_lo", [P, T])
        loop_slot = keep("loop_slot", [P, NT], I32)
        out_count = keep("out_count", [P, COUNT * NT])
        SUB, TURNS = COUNT, T // (2 * COUNT)

        with phase(nc) as ph:
            tmp_i = ph.sb("tmp_i", [P, T], I32)
            dst_hi = ph.sb("dst_hi", [P, T])
            src_hi = ph.sb("src_hi", [P, T])
            src_lo = ph.sb("src_lo", [P, T])
            blank = ph.sb("blank", [P, R * SLOTS, 4], I32)
            oh_hi = ph.sb("oh_hi", [P, 2, 2, SUB, P], BF16)
            oh_lo = ph.sb("oh_lo", [P, 2, 2, SUB, NT], BF16)
            psum = ph.ps("psum", [P, 2, 2, 512])
            loaded, blanked, blank_sent = ph.sem("loaded"), ph.sem("blanked"), ph.sem("blank_sent")
            hot_ready = ph.sem_ring("hot_ready", 2)
            counted, taken, added = ph.sem_ring("counted", 2), ph.sem_ring("taken", 2), ph.sem_ring("added", 2)
            pe_passed, act_passed, v_passed = ph.sem("pe_passed"), ph.sem("act_passed"), ph.sem("v_passed")
            both = [("dst", dst_hi, dst_lo)] + ([("src", src_hi, src_lo)] if g.degrees else [])
            with nc.Block() as block:
                @block.sync
                def _(sp):
                    sp.dma_start(dst_i[:], dst_cols).then_inc(loaded, 16)
                    sp.dma_start(src_i[:], src_cols).then_inc(loaded, 16)
                    if g.degrees:
                        sp.dma_start(w_f[:], w_cols).then_inc(loaded, 16)
                    sp.wait_ge(blanked, 1)
                    sp.dma_start(g.records.rearrange("(p s) c -> p s c", p=P), blank[:]).then_inc(blank_sent, 16)
                    sp.wait_ge(blank_sent, 16)

                @block.vector
                def _(v):
                    v.memset(blank[:], 0)
                    v.memset(out_count[:], 0.0)
                    if not g.degrees:
                        v.memset(w_f[:], 0.0)
                    v.drain()
                    v.memset(blank[:, :, 3], NP - 1).then_inc(blanked, 1)
                    v.wait_ge(loaded, 48 if g.degrees else 32)
                    v.tensor_copy(dst_f[:], dst_i[:])
                    for (_, hi, lo), ends in zip(both, (dst_i, src_i)):
                        v.drain()
                        v.tensor_scalar(tmp_i[:], ends[:], P - 1, None, ALU.bitwise_and)
                        v.drain()
                        v.tensor_copy(hi[:], tmp_i[:])
                        v.drain()
                        v.tensor_scalar(tmp_i[:], ends[:], P.bit_length() - 1, None, ALU.logical_shift_right)
                        v.drain()
                        v.tensor_copy(lo[:], tmp_i[:])
                    v.drain()
                    with v.Fori(0, TURNS) as i:
                        for s in range(2):
                            hold(v, counted[s], i + 1, v_passed)
                            for k, (_, hi, lo) in enumerate(both):
                                at = bass.ds(i * (2 * SUB) + s * SUB, SUB)
                                v.tensor_tensor(oh_hi[:, s, k], wide(C.iota_row[:], 1, SUB),
                                                wide(hi[:, at], 2, P), ALU.is_equal)
                                last = v.tensor_tensor(oh_lo[:, s, k], wide(C.iota_row[:, 0:NT], 1, SUB),
                                                       wide(lo[:, at], 2, NT), ALU.is_equal)
                            last.then_inc(hot_ready[s], 1)
                            if g.degrees:
                                v.wait_ge(counted[s], i + 2)
                                v.tensor_tensor(out_count[:], out_count[:], psum[:, s, 1, 0:SUB * NT],
                                                ALU.add).then_inc(added[s], 1)

                @block.tensor
                def _(pe):
                    for s in range(2):
                        pe.sem_inc(counted[s], 1)
                    with pe.Fori(0, TURNS) as i:
                        for s in range(2):
                            hold(pe, hot_ready[s], i + 1, pe_passed)
                            hold(pe, taken[s], i + 1, pe_passed)
                            if g.degrees:
                                hold(pe, added[s], i + 1, pe_passed)
                            for k in range(len(both)):
                                for j in range(SUB):
                                    last = pe.matmul(psum[:, s, k, j * NT:(j + 1) * NT], oh_hi[:, s, k, j],
                                                     oh_lo[:, s, k, j], start=True, stop=True)
                            last.then_inc(counted[s], 1)

                @block.scalar
                def _(act):
                    for s in range(2):
                        act.sem_inc(taken[s], 1)
                        act.sem_inc(added[s], 1)
                    with act.Fori(0, TURNS) as i:
                        for s in range(2):
                            hold(act, counted[s], i + 2, act_passed)
                            act.activation(counts[:, bass.ds(i * (2 * SUB) + s * SUB, SUB), :],
                                           psum[:, s, 0, 0:SUB * NT].rearrange("p (j l) -> p j l", j=SUB),
                                           ACT.Copy).then_inc(taken[s], 1)

        with phase(nc) as ph:
            deg = ph.sb("deg", [P, NT])
            rows_f = ph.sb("rows_f", [P, NT])
            inc = ph.sb("inc", [P, NT])
            start = ph.sb("start", [P, NT])
            tmp_i = ph.sb("tmp_i", [P, NT], I32)
            tmp_f = ph.sb("tmp_f", [P, NT])
            total = ph.sb("total", [P, 1])
            norm = ph.sb("norm", [P, 2, NT])
            psum = ph.ps("psum", [P, 512])
            have_total, have_base, clipped, rooted = (ph.sem(n) for n in ("have_total", "have_base", "clipped", "rooted"))
            with nc.Block() as block:
                @block.vector
                def _(v):
                    for lo in range(NT):
                        v.tensor_tensor_scan(offset[:, :, lo], C.ones[:, 0:1].broadcast_to([P, T]),
                                             counts[:, :, lo], 0.0, ALU.mult, ALU.add)
                    v.drain()
                    v.tensor_copy(deg[:], offset[:, T - 1, :])
                    v.drain()
                    v.tensor_tensor(offset[:], offset[:], counts[:], ALU.subtract)
                    v.tensor_scalar(tmp_f[:], deg[:], float(SLOTS), None, ALU.add)
                    v.drain()
                    v.tensor_copy(tmp_i[:], tmp_f[:])
                    v.drain()
                    v.tensor_scalar(tmp_i[:], tmp_i[:], SLOTS.bit_length() - 1, None, ALU.logical_shift_right)
                    v.drain()
                    v.tensor_copy(rows_f[:], tmp_i[:])
                    v.drain()
                    v.tensor_tensor_scan(inc[:], C.ones[:, 0:1].broadcast_to([P, NT]), rows_f[:], 0.0,
                                         ALU.mult, ALU.add)
                    v.drain()
                    v.tensor_copy(total[:], inc[:, NT - 1:NT]).then_inc(have_total, 1)
                    v.tensor_tensor(start[:], inc[:], rows_f[:], ALU.subtract)
                    v.drain()
                    v.wait_ge(have_base, 1)
                    v.tensor_scalar(start[:], start[:], psum[:, 0:1], None, ALU.add)
                    v.drain()
                    v.tensor_tensor(tmp_f[:], start[:], rows_f[:], ALU.add)
                    v.drain()
                    v.tensor_scalar(tmp_f[:], tmp_f[:], 1.0, None, ALU.subtract)
                    v.drain()
                    v.tensor_copy(g.end_row[:], tmp_f[:])
                    v.tensor_scalar(start[:], start[:], float(SLOTS), None, ALU.mult)
                    v.drain()
                    v.tensor_tensor(offset[:], offset[:], wide(start[:], 1, T), ALU.add)
                    v.tensor_tensor(tmp_f[:], start[:], deg[:], ALU.add)
                    v.drain()
                    v.tensor_copy(loop_slot[:], tmp_f[:])
                    if g.degrees:
                        v.tensor_scalar(norm[:, 0], deg[:], 1.0, None, ALU.max)
                        v.tensor_reduce(norm[:, 1], out_count[:].rearrange("p (j l) -> p l j", j=COUNT), AX.X, ALU.add)
                        v.drain()
                        v.tensor_scalar(norm[:, 1], norm[:, 1], 1.0, None, ALU.max).then_inc(clipped, 1)
                        v.wait_ge(rooted, 1)
                        v.reciprocal(g.norm_in[:], norm[:, 0])
                        v.reciprocal(g.norm_out[:], norm[:, 1])

                @block.tensor
                def _(pe):
                    pe.wait_ge(have_total, 1)
                    pe.matmul(psum[:, 0:1], C.above[:], total[:], start=True, stop=True).then_inc(have_base, 1)

                @block.scalar
                def _(act):
                    if g.degrees:
                        act.wait_ge(clipped, 1)
                        act.activation(norm[:], norm[:], ACT.Sqrt).then_inc(rooted, 1)

        SUB, TURNS = PLACE, T // (2 * PLACE)

        with phase(nc) as ph:
            rows_i = ph.sb("rows_i", [P, 2, SUB * P], I32)
            rows_f = ph.sb("rows_f", [P, 2, SUB * P])
            hi_i = ph.sb("hi_i", [P, 2, SUB * P], I32)
            hot_t = ph.sb("hot_t", [P, 2, SUB * P])
            oh_lo = ph.sb("oh_lo", [P, 2, SUB, NT])
            picked = ph.sb("picked", [P, 2, SUB, NT])
            junk = ph.sb("junk", [P, P])
            dst_s = ph.sb("dst_s", [P, 2, SUB])
            rank = ph.sb("rank", [P, 2, SUB])
            place_f = ph.sb("place_f", [P, 2, SUB])
            place = ph.sb("place", [P, 2, SUB], I32)
            rec = ph.sb("rec", [P, 2, SUB, 4], I32)
            loop_rec = ph.sb("loop_rec", [P, NT, 4], I32)
            psum = ph.ps("psum", [P, 2, 512])
            rows_in, rows_used = ph.sem_ring("rows_in", 2), ph.sem_ring("rows_used", 2)
            hot_ready, looked_up, rec_ready, rec_sent, rec_free = (ph.sem_ring(n, 2) for n in (
                "hot_ready", "looked_up", "rec_ready", "rec_sent", "rec_free"))
            loops_ready, loops_sent = ph.sem("loops_ready"), ph.sem("loops_sent")
            sp_passed, v_passed, pe_passed, pool_passed = (ph.sem(n) for n in (
                "sp_passed", "v_passed", "pe_passed", "pool_passed"))
            with nc.Block() as block:
                @block.sync
                def _(sp):
                    with sp.Fori(0, TURNS) as i:
                        for s in range(2):
                            hold(sp, rows_used[s], i + 1, sp_passed)
                            sp.dma_start(rows_i[:, s, :],
                                         dst_rows[bass.ds(i * (2 * SUB) + s * SUB, SUB), :]
                                         .rearrange("(o t) q -> o (t q)", o=1)
                                         .broadcast_to([P, SUB * P])).then_inc(rows_in[s], 16)

                @block.vector
                def _(v):
                    for s in range(2):
                        v.sem_inc(rows_used[s], 1)
                    v.memset(rec[:], 1)
                    v.memset(loop_rec[:], 0)
                    v.drain()
                    v.memset(loop_rec[:, :, 2], 2)
                    v.tensor_copy(loop_rec[:, :, 0], C.node_i[:])
                    v.tensor_copy(loop_rec[:, :, 3], C.node_i[:]).then_inc(loops_ready, 1)
                    with v.Fori(0, TURNS) as i:
                        for s in range(2):
                            at = bass.ds(i * (2 * SUB) + s * SUB, SUB)
                            hold(v, rows_in[s], i * 16 + 16, v_passed)
                            v.tensor_scalar(hi_i[:, s], rows_i[:, s], P - 1, None, ALU.bitwise_and)
                            v.tensor_copy(rows_f[:, s], rows_i[:, s]).then_inc(rows_used[s], 1)
                            v.tensor_copy(dst_s[:, s], dst_f[:, at])
                            v.drain()
                            v.tensor_scalar(hot_t[:, s], hi_i[:, s], C.iota_col[:, 0:1], None,
                                            ALU.is_equal).then_inc(hot_ready[s], 1)
                            v.tensor_tensor(oh_lo[:, s], wide(C.iota_row[:, 0:NT], 1, SUB),
                                            wide(dst_lo[:, at], 2, NT), ALU.is_equal)
                            for j in range(SUB):
                                v.scalar_tensor_tensor(junk[:], rows_f[:, s, j * P:(j + 1) * P],
                                                       dst_s[:, s, j:j + 1], C.below[:], ALU.is_equal, ALU.mult,
                                                       accum_out=rank[:, s, j:j + 1])
                                v.drain()
                            hold(v, looked_up[s], i + 1, v_passed)
                            v.tensor_tensor(picked[:, s], oh_lo[:, s],
                                            psum[:, s, 0:SUB * NT].rearrange("p (j l) -> p j l", j=SUB), ALU.mult)
                            v.drain()
                            v.tensor_reduce(place_f[:, s], picked[:, s], AX.X, ALU.add)
                            v.drain()
                            v.tensor_tensor(place_f[:, s], place_f[:, s], rank[:, s], ALU.add)
                            v.drain()
                            hold(v, rec_free[s], i + 1, v_passed)
                            v.tensor_copy(place[:, s], place_f[:, s])
                            v.tensor_copy(rec[:, s, :, 0], src_i[:, at])
                            v.tensor_copy(rec[:, s, :, 1].bitcast(F32), w_f[:, at])
                            v.tensor_copy(rec[:, s, :, 3], dst_i[:, at]).then_inc(rec_ready[s], 1)

                @block.tensor
                def _(pe):
                    with pe.Fori(0, TURNS) as i:
                        for s in range(2):
                            hold(pe, hot_ready[s], i + 1, pe_passed)
                            for j in range(SUB):
                                last = pe.matmul(psum[:, s, j * NT:(j + 1) * NT], hot_t[:, s, j * P:(j + 1) * P],
                                                 offset[:, bass.ds(i * (2 * SUB) + s * SUB + j, 1), :]
                                                 .rearrange("p o l -> p (o l)"), start=True, stop=True)
                            last.then_inc(looked_up[s], 1)

                @block.scalar
                def _(act):
                    for s in range(2):
                        act.sem_inc(rec_free[s], 1)
                    with act.Fori(0, TURNS) as i:
                        for s in range(2):
                            hold(act, rec_sent[s], i * (16 * SUB) + 16 * SUB, rec_free[s])

                @block.gpsimd
                def _(pool):
                    with pool.Fori(0, TURNS) as i:
                        for s in range(2):
                            hold(pool, rec_ready[s], i + 1, pool_passed)
                            for j in range(SUB):
                                pool.indirect_dma_start(
                                    out=g.records, out_offset=bass.IndirectOffsetOnAxis(ap=place[:, s, j:j + 1], axis=0),
                                    in_=rec[:, s, j, :], in_offset=None).then_inc(rec_sent[s], 16)
                    pool.wait_ge(loops_ready, 1)
                    for t in range(NT):
                        pool.indirect_dma_start(
                            out=g.records, out_offset=bass.IndirectOffsetOnAxis(ap=loop_slot[:, t:t + 1], axis=0),
                            in_=loop_rec[:, t, :], in_offset=None).then_inc(loops_sent, 16)
                    pool.wait_ge(loops_sent, 16 * NT)
                    for s in range(2):
                        pool.wait_ge(rec_sent[s], 16 * SUB * TURNS)

    with phase(nc) as ph:
        recs = ph.sb("recs", [P, R * SLOTS, 4], I32)
        row_dst = ph.sb("row_dst", [P, R])
        kind = ph.sb("kind", [P, R * SLOTS])
        ends = ph.sb("ends", [P, 2])
        hit = ph.sb("hit", [P, 2, P])
        has = ph.sb("has", [P, 2])
        same = ph.sb("same", [P, 1])
        psum = ph.ps("psum", [P, 2, P])
        loaded, have_ends, spread = ph.sem("loaded"), ph.sem("have_ends"), ph.sem("spread")
        with nc.Block() as block:
            @block.sync
            def _(sp):
                sp.dma_start(recs[:], g.records.rearrange("(p s) c -> p s c", p=P)).then_inc(loaded, 16)

            @block.tensor
            def _(pe):
                pe.wait_ge(have_ends, 1)
                for k in range(2):
                    last = pe.matmul(psum[:, k], ends[:, k:k + 1].broadcast_to([P, P]), C.ident[:],
                                     start=True, stop=True)
                last.then_inc(spread, 1)

            @block.vector
            def _(v):
                v.wait_ge(loaded, 16)
                v.tensor_copy(row_dst[:], recs[:].rearrange("p (r k) c -> p r k c", k=SLOTS)[:, :, 0, 3])
                v.tensor_copy(kind[:], recs[:, :, 2])
                if g.degrees:
                    v.tensor_copy(g.weight[:, :, 0:SLOTS],
                                  recs[:].bitcast(F32).rearrange("p (r k) c -> p r k c", k=SLOTS)[:, :, :, 1])
                v.drain()
                v.tensor_copy(ends[:, 0:1], row_dst[:, 0:1])
                v.tensor_copy(ends[:, 1:2], row_dst[:, R - 1:R])
                v.drain()
                v.tensor_tensor(same[:], ends[:, 0:1], ends[:, 1:2], ALU.is_equal).then_inc(have_ends, 1)
                v.tensor_scalar(g.is_edge[:].rearrange("p r k -> p (r k)"), kind[:], 1.0, None, ALU.is_equal)
                v.tensor_scalar(g.is_any[:].rearrange("p r k -> p (r k)"), kind[:], 1.0, None, ALU.is_ge)
                v.memset(g.cont[:, 0:1], 0.0)
                v.tensor_tensor(g.cont[:, 1:R], row_dst[:, 1:R], row_dst[:, 0:R - 1], ALU.is_equal)
                v.memset(g.apart[:, R:R + 1], -APART)
                v.drain()
                if g.degrees:
                    v.tensor_copy(g.weight[:, :, SLOTS], g.cont[:])
                v.tensor_scalar(g.apart[:, 0:R], g.cont[:], 1.0, APART, ALU.subtract, ALU.mult)
                for k, into in enumerate((g.in_first, g.in_last)):
                    v.tensor_scalar(into[:], row_dst[:], ends[:, k:k + 1], None, ALU.is_equal)
                    v.drain()
                    v.tensor_scalar(into[:], into[:], 1.0, APART, ALU.subtract, ALU.mult)
                v.wait_ge(spread, 1)
                v.tensor_scalar(hit[:, 0], psum[:, 1], ends[:, 0:1], None, ALU.is_equal)
                v.tensor_scalar(hit[:, 1], psum[:, 0], ends[:, 1:2], None, ALU.is_equal)
                v.drain()
                v.tensor_tensor(hit[:, 0], hit[:, 0], C.below[:], ALU.mult)
                v.tensor_tensor(hit[:, 1], hit[:, 1], C.above[:], ALU.mult)
                v.drain()
                v.tensor_copy(g.carry[:], hit[:, 1])
                v.tensor_scalar(g.from_prev[:], hit[:, 0], 1.0, APART, ALU.subtract, ALU.mult)
                v.tensor_scalar(g.from_next[:], hit[:, 1], 1.0, APART, ALU.subtract, ALU.mult)
                v.tensor_reduce(has[:], hit[:], AX.X, ALU.max)
                v.drain()
                v.tensor_tensor(same[:], same[:], has[:, 1:2], ALU.mult)
                v.drain()
                v.tensor_scalar(same[:], same[:], -1.0, 1.0, ALU.mult, ALU.add)
                v.drain()
                v.tensor_tensor(g.ends_here[:], same[:], has[:, 0:1], ALU.mult)
                for t in range(NT):
                    v.tensor_scalar(g.first_node[:, t:t + 1], ends[:, 0:1], float(P * t), None, ALU.subtract)


class Pass:

    def __init__(self, graph, source, target, feats, cols, heads, slope, score, inner, mask, dead=None):
        self.graph = graph
        self.source = source
        self.target = target
        self.feats = feats
        self.cols = cols
        self.heads = heads
        self.slope = slope
        self.score = score
        self.inner = inner
        self.mask = mask
        self.dead = dead

    def per_head(self, ap):
        if self.inner == "h":
            return ap.rearrange("p a (f h) -> p a f h", h=self.heads)
        return ap.rearrange("p a (h f) -> p a h f", h=self.heads)

    def spread(self, ap):
        each = self.feats // self.heads
        return wide(ap, 2, each) if self.inner == "h" else wide(ap, 3, each)


def edge_pass(nc, C, e, att, finish):
    g, F, H, K = e.graph, e.feats, e.heads, SLOTS
    R = g.R
    soft = e.score != "weight"
    W = F + (H if soft else 0)
    WC = W + (H if soft else 0)
    RING = 6
    TURNS, REST = divmod(R, RING)
    n = Phase.count
    run_table = nc.dram_tensor(f"run_{n}", (P * R, W), F32, kind="Internal").ap()
    run_rows = run_table.rearrange("(p r) f -> p r f", p=P)
    with ExitStack() as outer:
        def keep(name, shape, dt=F32):
            return outer.enter_context(nc.sbuf_tensor(f"{name}_{n}", shape, dt))

        last_state = keep("last_state", [P, W])
        top = keep("top", [P, R + 1, H])
        cin = keep("cin", [P, WC])

        with phase(nc) as ph:
            tcols = W if e.score == "att" else H
            stage = ph.sb("stage", [P, RING, K * 4], I32)
            G = ph.sb("G", [P, RING, K + 1, W])
            T = ph.sb("T", [P, RING, tcols])
            weighed = ph.sb("weighed", [P, K + 1, F])
            score_e = ph.sb("score_e", [P, RING, K + 1, H])
            score_x = ph.sb("score_x", [P, RING, K + 1, H])
            dead = ph.sb("dead", [P, K, H])
            best = ph.sb("best", [P, H])
            prob = ph.sb("prob", [P, RING, K + 2, H])
            lowered = ph.sb("lowered", [P, R, K])
            idx_in, gathered, consumed = (ph.sem_ring(n, RING) for n in ("idx_in", "gathered", "consumed"))
            scored, powered = ph.sem_ring("scored", RING), ph.sem_ring("powered", RING)
            state_ready, state_out, state_free = (ph.sem_ring(n, RING) for n in (
                "state_ready", "state_out", "state_free"))
            flipped, bent, attended, seen = (ph.sem_ring(n, 2) for n in ("flipped", "bent", "attended", "seen"))
            sp_passed, pool_passed, v_passed, act_passed, pe_passed = (ph.sem(n) for n in (
                "sp_passed", "pool_passed", "v_passed", "act_passed", "pe_passed"))
            if e.score == "att":
                bent_sb = ph.sb("bent_sb", [P, 2, DC, K, P])
                ident_k = ph.sb("ident_k", [P, K, P])
                have_ident = ph.sem("have_ident")
                psum_t = ph.ps("psum_t", [P, 2, DC, K, P])
                psum_e = ph.ps("psum_e", [P, 2, 512])
            idx_view = g.records.rearrange("(p r k) c -> p r (k c)", p=P, k=K)
            per_turn = 16 * (K + (1 if soft else 0))
            with nc.Block() as block:
                @block.sync
                def _(sp):
                    for s in range(RING):
                        sp.dma_start(stage[:, s, :], idx_view[:, s, :]).then_inc(idx_in[s], 16)

                    def store_state(i, s):
                        to = (s + 1) % RING
                        hold(sp, state_ready[to], i + 1, sp_passed)
                        sp.dma_start(run_rows[:, bass.ds(i * RING + s, 1), :].rearrange("p o f -> p (o f)"),
                                     G[:, to, K, :]).then_inc(state_out[to], 16)

                    def state_stored(i, s):
                        to = (s + 1) % RING
                        hold(sp, state_out[to], i * 16 + 16, state_free[to])

                    def next_indices(i, s):
                        hold(sp, gathered[s], i * per_turn + per_turn, sp_passed)
                        sp.dma_start(stage[:, s, :], idx_view[:, bass.ds(i * RING + (RING + s), 1), :]
                                     .rearrange("p o c -> p (o c)")).then_inc(idx_in[s], 16)

                    with sp.Fori(0, TURNS - 1) as i:
                        for s in range(RING):
                            next_indices(i, s)
                            store_state(i, s)
                            if s:
                                state_stored(i, s - 1)
                        state_stored(i, RING - 1)
                    for s in range(RING):
                        if s < REST:
                            next_indices(TURNS - 1, s)
                        store_state(TURNS - 1, s)
                        if s:
                            state_stored(TURNS - 1, s - 1)
                    state_stored(TURNS - 1, RING - 1)
                    for s in range(REST):
                        store_state(TURNS, s)
                        state_stored(TURNS, s)

                @block.gpsimd
                def _(pool):
                    def gather(i, s):
                        hold(pool, idx_in[s], i * 16 + 16, pool_passed)
                        hold(pool, consumed[s], i + 1, pool_passed)
                        for k in range(K):
                            pool.indirect_dma_start(
                                out=G[:, s, k, :], out_offset=None, in_=e.source,
                                in_offset=bass.IndirectOffsetOnAxis(ap=stage[:, s, 4 * k:4 * k + 1], axis=0)
                            ).then_inc(gathered[s], 16)
                        if soft:
                            pool.indirect_dma_start(
                                out=T[:, s, :], out_offset=None, in_=e.target,
                                in_offset=bass.IndirectOffsetOnAxis(ap=stage[:, s, 3:4], axis=0)
                            ).then_inc(gathered[s], 16)

                    with pool.Fori(0, TURNS) as i:
                        for s in range(RING):
                            gather(i, s)
                    for s in range(REST):
                        gather(TURNS, s)

                @block.tensor
                def _(pe):
                    if e.score != "att":
                        return
                    pe.wait_ge(have_ident, 1)

                    def flip(i, s):
                        q, use = s % 2, i * (RING // 2) + (s // 2 + 1)
                        hold(pe, gathered[s], i * per_turn + per_turn, pe_passed)
                        hold(pe, bent[q], use, pe_passed)
                        for b in range(DC):
                            pe.matmul(psum_t[:, q, b].rearrange("p k n -> p (k n)"), T[:, s, b * P:(b + 1) * P],
                                      ident_k[:].rearrange("p k n -> p (k n)"), start=True, stop=False)
                            for k in range(K):
                                last = pe.matmul(psum_t[:, q, b, k, :], G[:, s, k, b * P:(b + 1) * P], C.ident[:],
                                                 start=False, stop=(k == K - 1))
                        last.then_inc(flipped[q], 1)

                    def attend(i, s):
                        q, use = s % 2, i * (RING // 2) + (s // 2 + 1)
                        hold(pe, bent[q], use + 1, pe_passed)
                        hold(pe, seen[q], use, pe_passed)
                        for k in range(K):
                            for b in range(DC):
                                if H == 1:
                                    last = pe.matmul(psum_e[:, q, k:k + 1], bent_sb[:, q, b, k, :], att[:, b, 0:1],
                                                     start=(b == 0), stop=(b == DC - 1))
                                else:
                                    last = pe.matmul(psum_e[:, q, k * H + b:k * H + b + 1], bent_sb[:, q, b, k, :],
                                                     att[:, b, b:b + 1], start=True, stop=True)
                        last.then_inc(attended[q], 1)

                    def turn_of(i, steps):
                        for s in range(steps):
                            flip(i, s)
                            if s:
                                attend(i, s - 1)
                        attend(i, steps - 1)

                    with pe.Fori(0, TURNS) as i:
                        turn_of(i, RING)
                    if REST:
                        turn_of(TURNS, REST)

                @block.scalar
                def _(act):
                    if not soft:
                        return
                    for q in range(2):
                        act.sem_inc(bent[q], 1)

                    def bend(i, s):
                        if e.score == "att":
                            q, use = s % 2, i * (RING // 2) + (s // 2 + 1)
                            hold(act, flipped[q], use, act_passed)
                            act.activation(bent_sb[:, q], psum_t[:, q], ACT.Relu).then_inc(bent[q], 1)

                    def power(i, s):
                        hold(act, scored[s], i + 1, act_passed)
                        act.activation(prob[:, s, 1:K + 2], score_x[:, s], ACT.Exp).then_inc(powered[s], 1)

                    def turn_of(i, steps):
                        for s in range(steps):
                            bend(i, s)
                            if s:
                                power(i, s - 1)
                        power(i, steps - 1)

                    with act.Fori(0, TURNS) as i:
                        turn_of(i, RING)
                    if REST:
                        turn_of(TURNS, REST)

                @block.vector
                def _(v):
                    for s in range(RING):
                        v.sem_inc(consumed[s], 1)
                        v.sem_inc(state_free[s], 1)
                    v.memset(G[:, 0, K, :], 0.0)
                    if soft:
                        for q in range(2):
                            v.sem_inc(seen[q], 1)
                        v.tensor_scalar(lowered[:], e.mask[:], 1.0, MASKED, ALU.subtract, ALU.mult)
                        v.memset(score_e[:, :, K, :], -MASKED / 10)
                        v.memset(top[:, 0, :], -MASKED / 10)
                        if e.score == "att":
                            v.tensor_copy(ident_k[:], wide(C.ident[:], 1, K)).then_inc(have_ident, 1)
                    v.drain()

                    def score(i, s):
                        r, r1 = bass.ds(i * RING + s, 1), bass.ds(i * RING + s + 1, 1)
                        flat = "p o h -> p (o h)"
                        hold(v, gathered[s], i * per_turn + per_turn, v_passed)
                        if not soft:
                            return
                        now = score_e[:, s, 0:K]
                        v.tensor_tensor(now, G[:, s, 0:K, F:W], wide(T[:, s, tcols - H:tcols], 1, K), ALU.add)
                        v.drain()
                        if e.score == "att":
                            q, use = s % 2, i * (RING // 2) + (s // 2 + 1)
                            hold(v, attended[q], use, v_passed)
                            v.tensor_tensor(now, now, psum_e[:, q, 0:K * H].rearrange("p (k h) -> p k h", h=H),
                                            ALU.add).then_inc(seen[q], 1)
                        else:
                            v.scalar_tensor_tensor(now, now, e.slope, now, ALU.mult, ALU.max)
                        v.drain()
                        if e.dead is not None:
                            v.tensor_scalar(dead[:], now, 0.0, e.dead, ALU.is_equal, ALU.mult)
                            v.drain()
                            v.tensor_tensor(now, now, dead[:], ALU.add)
                            v.drain()
                        v.tensor_tensor(now, now, wide(lowered[:, r, :].rearrange("p o k -> p (o k)"), 2, H), ALU.add)
                        v.drain()
                        v.tensor_reduce(best[:], score_e[:, s].rearrange("p k h -> p h k"), AX.X, ALU.max)
                        v.drain()
                        v.scalar_tensor_tensor(top[:, r1, :].rearrange(flat), top[:, r, :].rearrange(flat),
                                               g.apart[:, r], best[:], ALU.add, ALU.max)
                        v.drain()
                        v.scalar_tensor_tensor(score_x[:, s, K], top[:, r, :].rearrange(flat), g.apart[:, r],
                                               top[:, r1, :].rearrange(flat), ALU.add, ALU.subtract)
                        v.tensor_tensor(score_x[:, s, 0:K], now, wide(top[:, r1, :].rearrange(flat), 1, K),
                                        ALU.subtract).then_inc(scored[s], 1)

                    def weigh(i, s):
                        r, to = bass.ds(i * RING + s, 1), (s + 1) % RING
                        if soft:
                            hold(v, powered[s], i + 1, v_passed)
                            v.tensor_tensor(prob[:, s, 0], prob[:, s, K + 1], G[:, s, K, F:W], ALU.mult)
                            v.tensor_tensor(e.per_head(weighed[:]), e.per_head(G[:, s, :, 0:F]),
                                            e.spread(prob[:, s, 1:K + 2]), ALU.mult).then_inc(consumed[s], 1)
                        else:
                            v.tensor_tensor(weighed[:], G[:, s],
                                            wide(g.weight[:, r, :].rearrange("p o k -> p (o k)"), 2, F),
                                            ALU.mult).then_inc(consumed[s], 1)
                        hold(v, state_free[to], i + 1, v_passed)
                        v.drain()
                        if soft:
                            v.tensor_reduce(G[:, to, K, F:W], prob[:, s, 0:K + 1].rearrange("p k h -> p h k"), AX.X,
                                            ALU.add)
                        v.tensor_reduce(G[:, to, K, 0:F], weighed[:].rearrange("p k f -> p f k"), AX.X,
                                        ALU.add).then_inc(state_ready[to], 1)
                        v.drain()

                    def turn_of(i, steps):
                        for s in range(steps):
                            score(i, s)
                            if s:
                                weigh(i, s - 1)
                        weigh(i, steps - 1)

                    with v.Fori(0, TURNS) as i:
                        turn_of(i, RING)
                    if REST:
                        turn_of(TURNS, REST)
                    v.tensor_copy(last_state[:], G[:, R % RING, K, :])

        with phase(nc) as ph:
            inside = ph.sb("inside", [P, H, R])
            first_top = ph.sb("first_top", [P, H])
            before_top = ph.sb("before_top", [P, H])
            both_top = ph.sb("both_top", [P, H])
            masked = ph.sb("masked", [P, H, P])
            factor = ph.sb("factor", [P, H])
            psum = ph.ps("psum", [P, 2, H, P])
            psum_c = ph.ps("psum_c", [P, 512])
            spread, topped, spread2, shifted, powered, carried, started = (ph.sem(n) for n in (
                "spread", "topped", "spread2", "shifted", "powered", "carried", "started"))
            last_top = top[:, R, :]
            with nc.Block() as block:
                @block.tensor
                def _(pe):
                    if soft:
                        for h in range(H):
                            last = pe.matmul(psum[:, 0, h], last_top[:, h:h + 1].broadcast_to([P, P]), C.ident[:],
                                             start=True, stop=True)
                        last.then_inc(spread, 1)
                        pe.wait_ge(topped, 1)
                        for h in range(H):
                            last = pe.matmul(psum[:, 1, h], both_top[:, h:h + 1].broadcast_to([P, P]), C.ident[:],
                                             start=True, stop=True)
                        last.then_inc(spread2, 1)
                        pe.wait_ge(powered, 1)
                        for h in range(H):
                            if e.inner == "h":
                                to, of = psum_c[:, h:F:H], last_state[:, h:F:H]
                            else:
                                to, of = (x[:, h * (F // H):(h + 1) * (F // H)] for x in (psum_c, last_state))
                            pe.matmul(to, masked[:, h], of, start=True, stop=True, skip_group_check=True)
                            last = pe.matmul(psum_c[:, F + h:F + h + 1], masked[:, h], last_state[:, F + h:F + h + 1],
                                             start=True, stop=True, skip_group_check=True)
                    else:
                        last = pe.matmul(psum_c[:, 0:W], g.carry[:], last_state[:], start=True, stop=True)
                    last.then_inc(carried, 1)

                @block.scalar
                def _(act):
                    if soft:
                        act.wait_ge(shifted, 1)
                        act.activation(masked[:], masked[:], ACT.Exp, scale=-1.0)
                        act.activation(factor[:], factor[:], ACT.Exp).then_inc(powered, 1)

                @block.vector
                def _(v):
                    if soft:
                        v.tensor_tensor(inside[:], top[:, 1:R + 1, :].rearrange("p r h -> p h r"),
                                        wide(g.in_first[:], 1, H), ALU.add)
                        v.drain()
                        v.tensor_reduce(first_top[:], inside[:], AX.X, ALU.max)
                        v.wait_ge(spread, 1)
                        v.tensor_tensor(masked[:], psum[:, 0], wide(g.from_prev[:], 1, H), ALU.add)
                        v.drain()
                        v.tensor_reduce(before_top[:], masked[:], AX.X, ALU.max)
                        v.drain()
                        v.tensor_tensor(both_top[:], first_top[:], before_top[:], ALU.max).then_inc(topped, 1)
                        v.drain()
                        v.tensor_tensor(factor[:], first_top[:], both_top[:], ALU.subtract)
                        v.wait_ge(spread2, 1)
                        for h in range(H):
                            last = v.scalar_tensor_tensor(masked[:, h], psum[:, 1, h], last_top[:, h:h + 1],
                                                          g.from_next[:], ALU.subtract, ALU.subtract)
                        last.then_inc(shifted, 1)
                        v.wait_ge(powered, 1)
                        v.tensor_scalar(cin[:, W:WC], factor[:], 1.0, g.ends_here[:, 0:1], ALU.subtract, ALU.mult)
                    v.wait_ge(carried, 1)
                    v.tensor_scalar(cin[:, 0:W], psum_c[:, 0:W], g.ends_here[:, 0:1], None, ALU.mult)

        with phase(nc) as ph:
            got = ph.sb("got", [P, NT, W])
            den = ph.sb("den", [P, GRP, max(H, 1)])
            den2 = ph.sb("den2", [P, GRP, max(H, 1)])
            onto = ph.sb("onto", [P, 2, GRP, P])
            psum = ph.ps("psum", [P, GRP, 512])
            landed = ph.sem_ring("landed", NG)
            onto_ready, added, read, done, stored = (ph.sem(n) for n in (
                "onto_ready", "added", "read", "done", "stored"))
            with nc.Block() as block:
                @block.gpsimd
                def _(pool):
                    for t in range(NT):
                        pool.indirect_dma_start(
                            out=got[:, t, :], out_offset=None, in_=run_table,
                            in_offset=bass.IndirectOffsetOnAxis(ap=g.end_row[:, t:t + 1], axis=0)
                        ).then_inc(landed[t // GRP], 16)

                @block.tensor
                def _(pe):
                    for i in range(NG):
                        pe.wait_ge(onto_ready, i + 1)
                        if i:
                            pe.wait_ge(read, i)
                        for s in range(GRP):
                            last = pe.matmul(psum[:, s, 0:WC], onto[:, i % 2, s], cin[:], start=True, stop=True)
                        last.then_inc(added, 1)

                @block.vector
                def _(v):
                    def select(i):
                        v.tensor_tensor(onto[:, i % 2], wide(C.iota_row[:], 1, GRP),
                                        wide(g.first_node[:, i * GRP:(i + 1) * GRP], 2, P),
                                        ALU.is_equal).then_inc(onto_ready, 1)

                    select(0)
                    for i in range(NG):
                        if i + 1 < NG:
                            if i:
                                v.wait_ge(added, i)
                            select(i + 1)
                        mine = got[:, i * GRP:(i + 1) * GRP, :]
                        v.wait_ge(added, i + 1)
                        v.wait_ge(landed[i], 16 * GRP)
                        if soft:
                            v.tensor_scalar(den[:], psum[:, :, W:WC], 1.0, None, ALU.add)
                            v.drain()
                            v.tensor_tensor(e.per_head(mine[:, :, 0:F]), e.per_head(mine[:, :, 0:F]), e.spread(den[:]),
                                            ALU.mult)
                            v.tensor_tensor(mine[:, :, F:W], mine[:, :, F:W], den[:], ALU.mult)
                            v.drain()
                        v.tensor_tensor(mine, mine, psum[:, :, 0:W], ALU.add).then_inc(read, 1)
                        v.drain()
                        if soft:
                            v.tensor_scalar(den2[:], mine[:, :, F:W], 0.0, None, ALU.is_le)
                            v.drain()
                            v.tensor_tensor(den[:], mine[:, :, F:W], den2[:], ALU.add)
                            v.drain()
                            v.reciprocal(den2[:], den[:])
                            v.drain()
                            v.tensor_tensor(e.per_head(mine[:, :, 0:F]), e.per_head(mine[:, :, 0:F]), e.spread(den2[:]),
                                            ALU.mult)
                            v.drain()
                        finish.vector(v, slice(i * GRP, (i + 1) * GRP), mine)
                        v.drain()
                        v.sem_inc(done, 1)

                @block.sync
                def _(sp):
                    if finish.table is not None:
                        for i in range(NG):
                            sp.wait_ge(done, i + 1)
                            sp.dma_start(node_rows(finish.table, i, F), got[:, i * GRP:(i + 1) * GRP, 0:F]
                                         ).then_inc(stored, 16)
                        sp.wait_ge(stored, 16 * NG)


def node_rows(table, i, cols):
    return table.rearrange("(g t p) f -> g p t f", g=NG, p=P)[bass.ds(i, 1), :, :, 0:cols] \
        .rearrange("o p t f -> (o p) t f")


class ToNodes:

    table = None

    def __init__(self, C, bias=None):
        self.C, self.bias = C, bias

    def vector(self, v, tiles, got):
        if self.bias is not None:
            v.tensor_tensor(got[:, :, 0:D], got[:, :, 0:D], wide(self.bias[:], 1, GRP), ALU.add)
            v.drain()
        v.tensor_tensor(self.C.X[:, tiles, :], self.C.X[:, tiles, :], got[:, :, 0:D], ALU.add)


class ToTable:

    def __init__(self, table, cols, bias=None, scale=None, raw=False):
        self.table, self.cols, self.bias, self.scale, self.raw = table, cols, bias, scale, raw

    def vector(self, v, tiles, got):
        out = got[:, :, 0:self.cols]
        if self.scale is not None:
            v.tensor_tensor(out, out, wide(self.scale[:, tiles], 2, self.cols), ALU.mult)
            v.drain()
        if self.bias is not None:
            v.tensor_tensor(out, out, wide(self.bias[:], 1, GRP), ALU.add)
            v.drain()
        if not self.raw:
            v.tensor_scalar(out, out, 0.0, None, ALU.max)



def turn(nc, C, xT, table=None, cols=D, norm=True, keep_table=None, add=False, parts=None):
    KB = cols // P
    with phase(nc) as ph:
        rows = ph.sb("rows", [P, GRP, cols])
        stats = ph.sb("stats", [P, GRP, 6])
        mean_var = ph.sb("mean_var", [P, GRP, 2])
        spread = ph.sb("spread", [P, GRP])
        inv = ph.sb("inv", [P, GRP])
        psum = ph.ps("psum", [P, GRP, 512])
        ready, turned, taken, have_var, rooted, stored, loaded = (ph.sem(n) for n in (
            "ready", "turned", "taken", "have_var", "rooted", "stored", "loaded"))
        v_passed, pe_passed, act_passed, sp_passed, free = (ph.sem(n) for n in (
            "v_passed", "pe_passed", "act_passed", "sp_passed", "free"))
        with nc.Block() as block:
            @block.sync
            def _(sp):
                if not norm:
                    with sp.Fori(0, NG) as i:
                        hold(sp, turned, i + 1, sp_passed)
                        sp.dma_start(rows[:], node_rows(table, i, cols)).then_inc(loaded, 16)
                if keep_table is not None:
                    with sp.Fori(0, NG) as i:
                        hold(sp, ready, i + 1, sp_passed)
                        sp.dma_start(node_rows(keep_table, i, cols), rows[:]).then_inc(stored, 16)
                        hold(sp, stored, i * 16 + 16, free)

            @block.vector
            def _(v):
                if keep_table is not None:
                    v.sem_inc(free, 1)
                if norm:
                    with v.Fori(0, NG) as i:
                        tiles = bass.ds(i * GRP, GRP)
                        for s in range(GRP):
                            v.bn_stats(stats[:, s], C.X[:, bass.ds(i * GRP + s, 1), :].rearrange("p o f -> p (o f)"))
                        v.drain()
                        for s in range(GRP):
                            v.bn_aggr(mean_var[:, s], stats[:, s])
                        v.drain()
                        v.tensor_scalar(spread[:], mean_var[:, :, 1], LN_EPS, None, ALU.add).then_inc(have_var, 1)
                        hold(v, rooted, i + 1, v_passed)
                        v.reciprocal(inv[:], spread[:])
                        hold(v, turned, i + 1, v_passed)
                        if keep_table is not None:
                            hold(v, free, i + 1, v_passed)
                        v.tensor_tensor(rows[:], C.X[:, tiles, :], wide(mean_var[:, :, 0], 2, D), ALU.subtract)
                        v.drain()
                        v.tensor_tensor(rows[:], rows[:], wide(inv[:], 2, D), ALU.mult).then_inc(ready, 1)
                        if add:
                            v.drain()
                            v.tensor_tensor(C.X[:, tiles, :], C.X[:, tiles, :], rows[:], ALU.add)
                        v.drain()
                if parts is not None:
                    v.wait_ge(taken, NG + 1)
                    v.tensor_tensor(parts[1][:], xT[:], parts[0][:], ALU.subtract)

            @block.tensor
            def _(pe):
                pe.sem_inc(turned, 1)
                with pe.Fori(0, NG) as i:
                    if norm:
                        hold(pe, ready, i + 1, pe_passed)
                    else:
                        hold(pe, loaded, i * 16 + 16, pe_passed)
                    hold(pe, taken, i + 1, pe_passed)
                    for s in range(GRP):
                        for b in range(KB):
                            last = pe.transpose(psum[:, s, b * P:(b + 1) * P], rows[:, s, b * P:(b + 1) * P],
                                                C.ident[:])
                    last.then_inc(turned, 1)

            @block.scalar
            def _(act):
                act.sem_inc(taken, 1)
                with act.Fori(0, NG) as i:
                    if norm:
                        hold(act, have_var, i + 1, act_passed)
                        act.activation(spread[:], spread[:], ACT.Sqrt).then_inc(rooted, 1)
                    hold(act, turned, i + 2, act_passed)
                    for b in range(KB):
                        last = act.activation(xT[:, b, bass.ds(i * UNIT, UNIT)].rearrange("p (t q) -> p t q", q=P),
                                              psum[:, :, b * P:(b + 1) * P], ACT.Copy)
                        if parts is not None:
                            last = act.activation(parts[0][:, b, bass.ds(i * UNIT, UNIT)].rearrange("p (t q) -> p t q", q=P),
                                                  psum[:, :, b * P:(b + 1) * P], ACT.Copy)
                    last.then_inc(taken, 1)


def project(nc, C, xT, weight, cols, outputs, K=D, bias=None, post=None, extra=0):
    KB = K // P
    with phase(nc) as ph:
        w = ph.sb("w", [P, KB, cols])
        rows = ph.sb("rows", [P, GRP, cols + extra])
        b = ph.sb("b", [P, cols]) if bias is not None else None
        scratch = ph.sb("scratch", [P, GRP, cols]) if extra else None
        x = ph.sb("x", [P, KB, UNIT])
        staged, act_passed = ph.sem("staged"), ph.sem("act_passed")
        psum = ph.ps("psum", [P, GRP, 512])
        loaded, made, taken, ready, stored = (ph.sem(n) for n in ("loaded", "made", "taken", "ready", "stored"))
        v_passed, pe_passed, sp_passed, free = (ph.sem(n) for n in ("v_passed", "pe_passed", "sp_passed", "free"))
        loads = 16 * (1 + (bias is not None))
        with nc.Block() as block:
            @block.sync
            def _(sp):
                sp.dma_start(w[:], weight.rearrange("(k p) c -> p k c", p=P)).then_inc(loaded, 16)
                if bias is not None:
                    sp.dma_start(b[:], bias.broadcast_to([P, cols])).then_inc(loaded, 16)
                with sp.Fori(0, NG) as i:
                    hold(sp, ready, i + 1, sp_passed)
                    for table, at, n in outputs:
                        sp.dma_start(node_rows(table, i, n), rows[:, :, at:at + n]).then_inc(stored, 16)
                    hold(sp, stored, i * (16 * len(outputs)) + 16 * len(outputs), free)

            @block.tensor
            def _(pe):
                pe.wait_ge(loaded, loads)
                with pe.Fori(0, NG) as i:
                    hold(pe, taken, i + 1, pe_passed)
                    hold(pe, staged, i + 1, pe_passed)
                    for s in range(GRP):
                        for k in range(KB):
                            last = pe.matmul(psum[:, s, 0:cols], x[:, k, s * P:(s + 1) * P], w[:, k, :],
                                             start=(k == 0), stop=(k == KB - 1))
                    last.then_inc(made, 1)

            @block.scalar
            def _(act):
                act.sem_inc(made, 1)
                with act.Fori(0, NG) as i:
                    hold(act, made, i + 1, act_passed)
                    act.activation(x[:], xT[:, :, bass.ds(i * UNIT, UNIT)], ACT.Copy).then_inc(staged, 1)

            @block.vector
            def _(v):
                v.sem_inc(taken, 1)
                v.sem_inc(free, 1)
                v.wait_ge(loaded, loads)
                with v.Fori(0, NG) as i:
                    hold(v, free, i + 1, v_passed)
                    hold(v, made, i + 2, v_passed)
                    if bias is not None:
                        v.tensor_tensor(rows[:, :, 0:cols], psum[:, :, 0:cols], wide(b[:], 1, GRP),
                                        ALU.add).then_inc(taken, 1)
                    else:
                        v.tensor_copy(rows[:, :, 0:cols], psum[:, :, 0:cols]).then_inc(taken, 1)
                    v.drain()
                    if post is not None:
                        post(v, rows, scratch, bass.ds(i * GRP, GRP))
                        v.drain()
                    v.sem_inc(ready, 1)


def load_rows(nc, pairs, scales=()):
    with phase(nc) as ph:
        loaded = ph.sem("loaded")
        with nc.Block() as block:
            @block.vector
            def _(v):
                if scales:
                    v.wait_ge(loaded, 16 * len(pairs))
                for row, factor in scales:
                    v.tensor_scalar(row, row, factor, None, ALU.mult)

            @block.sync
            def _(sp):
                for to, of in pairs:
                    sp.dma_start(to, of).then_inc(loaded, 16)
                sp.wait_ge(loaded, 16 * len(pairs))


def pick_top(v, scratch, score, chosen, E, K):
    before = scratch
    for x in range(E):
        me = score[:, :, x:x + 1]
        if x:
            v.tensor_tensor(before[:, :, 0:x], score[:, :, 0:x], me.broadcast_to([P, NT, x]), ALU.is_ge)
        if x < E - 1:
            v.tensor_tensor(before[:, :, x:E - 1], score[:, :, x + 1:E], me.broadcast_to([P, NT, E - 1 - x]), ALU.is_gt)
        v.drain()
        v.tensor_reduce(chosen[:, :, x], before[:, :, 0:E - 1], AX.X, ALU.add)
        v.drain()
    v.tensor_scalar(chosen[:], chosen[:], float(K), None, ALU.is_lt)
    v.drain()


def choose_experts(nc, C, logits, gates, E, K, among_chosen):
    with phase(nc) as ph:
        top = ph.sb("top", [P, NT])
        scratch = ph.sb("scratch", [P, NT, E])
        chosen = ph.sb("chosen", [P, NT, E])
        prob = ph.sb("prob", [P, NT, E])
        total = ph.sb("total", [P, NT])
        shifted, powered = ph.sem("shifted"), ph.sem("powered")
        with nc.Block() as block:
            @block.scalar
            def _(act):
                act.wait_ge(shifted, 1)
                act.activation(prob[:], prob[:], ACT.Exp).then_inc(powered, 1)

            @block.vector
            def _(v):
                v.tensor_reduce(top[:], logits[:], AX.X, ALU.max)
                v.drain()
                v.tensor_tensor(prob[:], logits[:], wide(top[:], 2, E), ALU.subtract).then_inc(shifted, 1)
                if among_chosen:
                    pick_top(v, scratch, logits, chosen, E, K)
                v.wait_ge(powered, 1)
                if among_chosen:
                    v.tensor_tensor(prob[:], prob[:], chosen[:], ALU.mult)
                    v.drain()
                v.tensor_reduce(total[:], prob[:], AX.X, ALU.add)
                v.drain()
                v.reciprocal(total[:], total[:])
                v.drain()
                v.tensor_tensor(prob[:], prob[:], wide(total[:], 2, E), ALU.mult)
                v.drain()
                if among_chosen:
                    v.tensor_copy(gates[:], prob[:])
                else:
                    pick_top(v, scratch, prob, chosen, E, K)
                    v.tensor_tensor(gates[:], prob[:], chosen[:], ALU.mult)


def logits_of(nc, C, xT, weight, bias, E, logits):
    with phase(nc) as ph:
        w = ph.sb("w", [P, DC, E])
        b = ph.sb("b", [P, E])
        psum = ph.ps("psum", [P, NT, E])
        loaded, made = ph.sem("loaded"), ph.sem("made")
        with nc.Block() as block:
            @block.sync
            def _(sp):
                sp.dma_start(w[:], weight).then_inc(loaded, 16)
                sp.dma_start(b[:], bias.broadcast_to([P, E])).then_inc(loaded, 16)

            @block.tensor
            def _(pe):
                pe.wait_ge(loaded, 32)
                for t in range(NT):
                    for k in range(DC):
                        last = pe.matmul(psum[:, t, :], xT[:, k, t * P:(t + 1) * P], w[:, k, :],
                                         start=(k == 0), stop=(k == DC - 1))
                last.then_inc(made, 1)

            @block.vector
            def _(v):
                v.wait_ge(made, 1)
                v.tensor_tensor(logits[:], psum[:], wide(b[:], 1, NT), ALU.add)


def experts(nc, C, parts, gates, E, H, func, w1, b1, w2, b2):
    HC = H // P
    with phase(nc) as ph:
        w1_raw = ph.sb("w1_raw", [P, DC, H])
        w2_raw = ph.sb("w2_raw", [P, HC, D])
        w1_high, w1_low = (ph.sb(n, [P, DC, H], F32R) for n in ("w1_high", "w1_low"))
        w2_high, w2_low = (ph.sb(n, [P, HC, D], F32R) for n in ("w2_high", "w2_low"))
        b1s = ph.sb("b1s", [P, E * HC])
        b2s = ph.sb("b2s", [P, E, D])
        x_high, x_low = parts
        hidden = ph.sb("hidden", [P, 2, UNIT])
        hid_high, hid_low = (ph.sb(n, [P, HC, UNIT], F32R) for n in ("hid_high", "hid_low"))
        psum_h = ph.ps("psum_h", [P, 2, 2, 512])
        YB = 4
        psum_y = ph.ps("psum_y", [P, YB, 512])
        w1_in, w2_in, b_in, w1_split, w2_split = (ph.sem(n) for n in (
            "w1_in", "w2_in", "b_in", "w1_split", "w2_split"))
        h_made, h_taken, h_split = (ph.sem_ring(n, 2) for n in ("h_made", "h_taken", "h_split"))
        y_made, y_taken = ph.sem("y_made"), ph.sem("y_taken")
        sp_passed, pool_passed, pe_passed, act_passed, v_passed = (ph.sem(n) for n in (
            "sp_passed", "pool_passed", "pe_passed", "act_passed", "v_passed"))
        H2 = HC // 2

        def each_expert(eng, expert):
            if E > 1:
                with eng.Fori(0, E) as e:
                    expert(e)
            else:
                expert(0)

        with nc.Block() as block:
            @block.sync
            def _(sp):
                sp.dma_start(b1s[:], b1).then_inc(b_in, 16)
                sp.dma_start(b2s[:], b2.rearrange("(o e) f -> o e f", o=1).broadcast_to([P, E, D])).then_inc(b_in, 16)

                def load(e):
                    for raw, w, arrived, split in ((w1_raw, w1, w1_in, w1_split), (w2_raw, w2, w2_in, w2_split)):
                        hold(sp, split, e + 1, sp_passed)
                        sp.dma_start(raw[:], w[bass.ds(e, 1), :, :].rearrange("o (k p) h -> p (o k) h", p=P)
                                     ).then_inc(arrived, 16)

                each_expert(sp, load)

            @block.gpsimd
            def _(pool):
                pool.sem_inc(w1_split, 1)
                pool.sem_inc(w2_split, 1)

                def split(raw, high, low, done):
                    pool.tensor_copy(high[:], raw[:])
                    pool.drain()
                    pool.tensor_tensor(low[:], raw[:], high[:], ALU.subtract)
                    pool.drain()
                    pool.sem_inc(done, 1)

                def expert(e):
                    hold(pool, w1_in, e * 16 + 16, pool_passed)
                    hold(pool, h_made[1], e * (NG * H2) + 1, pool_passed)
                    split(w1_raw, w1_high, w1_low, w1_split)
                    hold(pool, w2_in, e * 16 + 16, pool_passed)
                    hold(pool, y_made, e * NT + 1, pool_passed)
                    split(w2_raw, w2_high, w2_low, w2_split)

                each_expert(pool, expert)

            @block.tensor
            def _(pe):
                for made in (*h_made, y_made):
                    pe.sem_inc(made, 1)

                def product(out, parts, first, last):
                    (lh, ll), (rh, rl) = parts
                    pe.matmul(out, lh, rh, start=first, stop=False)
                    pe.matmul(out, lh, rl, start=False, stop=False)
                    return pe.matmul(out, ll, rh, start=False, stop=last)

                def expert(e):
                    hold(pe, w1_split, e + 2, pe_passed)
                    with pe.Fori(0, NG) as c:
                        u = e * NG + c
                        for m in range(HC):
                            s = m % 2
                            hold(pe, h_taken[s], u * H2 + (m // 2 + 1), pe_passed)
                            for half in range(2):
                                nodes = bass.ds(c * UNIT + half * HALF, HALF)
                                for k in range(DC):
                                    block_of = slice(m * P, (m + 1) * P)
                                    last = product(psum_h[:, s, half, 0:HALF],
                                                   ((w1_high[:, k, block_of], w1_low[:, k, block_of]),
                                                    (x_high[:, k, nodes], x_low[:, k, nodes])), k == 0, k == DC - 1)
                            last.then_inc(h_made[s], 1)
                        hold(pe, w2_split, e + 2, pe_passed)

                        def bank_free(t):
                            before = t - YB if t >= YB else max(q for q in range(GRP) if q % YB == t) - GRP
                            hold(pe, y_taken, u * GRP + (before + 1 + GRP), pe_passed)

                        def second(t, m):
                            tile = slice(t * P, (t + 1) * P)
                            return product(psum_y[:, t % YB, 0:D],
                                           ((hid_high[:, m, tile], hid_low[:, m, tile]),
                                            (w2_high[:, m, :], w2_low[:, m, :])), m == 0, m == HC - 1)

                        bank_free(0)
                        bank_free(1)
                        for m in range(HC):
                            hold(pe, h_split[m % 2], u * H2 + (m // 2 + 2), pe_passed)
                            for t in range(2):
                                last = second(t, m)
                                if m == HC - 1:
                                    last.then_inc(y_made, 1)
                        for t in range(2, GRP):
                            bank_free(t)
                            for m in range(HC):
                                last = second(t, m)
                            last.then_inc(y_made, 1)

                each_expert(pe, expert)

            @block.scalar
            def _(act):
                for s in range(2):
                    act.sem_inc(h_taken[s], 1)
                act.wait_ge(b_in, 32)

                def expert(e):
                    with act.Fori(0, NG) as c:
                        u = e * NG + c
                        for m in range(HC):
                            s = m % 2
                            hold(act, h_made[s], u * H2 + (m // 2 + 2), act_passed)
                            hold(act, h_split[s], u * H2 + (m // 2 + 1), act_passed)
                            of = psum_h[:, s, :, 0:HALF]
                            for to in (hidden[:, s], hid_high[:, m]):
                                last = act.activation(to.rearrange("p (a n) -> p a n", a=2), of, func,
                                                      bias=b1s[:, bass.ds(e * HC + m, 1)])
                            last.then_inc(h_taken[s], 1)

                each_expert(act, expert)

            @block.vector
            def _(v):
                v.sem_inc(y_taken, GRP)
                for s in range(2):
                    v.sem_inc(h_split[s], 1)
                v.wait_ge(b_in, 32)

                def expert(e):
                    with v.Fori(0, NG) as c:
                        u = e * NG + c
                        tile = [bass.ds(c * GRP + t, 1) for t in range(GRP)]
                        for m in range(HC):
                            s = m % 2
                            hold(v, h_taken[s], u * H2 + (m // 2 + 2), v_passed)
                            v.tensor_tensor(hid_low[:, m], hidden[:, s], hid_high[:, m],
                                            ALU.subtract).then_inc(h_split[s], 1)
                        for t in range(GRP):
                            v.scalar_tensor_tensor(C.X[:, tile[t], :], b2s[:, bass.ds(e, 1), :],
                                                   gates[:, tile[t], bass.ds(e, 1)], C.X[:, tile[t], :],
                                                   ALU.mult, ALU.add)
                        v.drain()
                        for t in range(GRP):
                            hold(v, y_made, u * GRP + (t + 2), v_passed)
                            v.scalar_tensor_tensor(
                                C.X[:, tile[t], :], psum_y[:, t % YB:t % YB + 1, 0:D],
                                gates[:, tile[t], bass.ds(e, 1)],
                                C.X[:, tile[t], :], ALU.mult, ALU.add).then_inc(y_taken, 1)
                        v.drain()

                each_expert(v, expert)


def channel_mix(nc, C, xT, fc_w, fc_b, ch_w, scale, table):
    with phase(nc) as ph:
        w = ph.sb("w", [P, DC, D])
        b = ph.sb("b", [P, DC])
        mix = ph.sb("mix", [P, DC, P])
        hidden = ph.sb("hidden", [P, DC, UNIT])
        rows = ph.sb("rows", [P, GRP, D])
        psum_h = ph.ps("psum_h", [P, DC, 2, 512])
        psum_y = ph.ps("psum_y", [P, 3, 2, D])
        zeroed, loaded, made, hid, mixed, ready, stored = (ph.sem(n) for n in (
            "zeroed", "loaded", "made", "hid", "mixed", "ready", "stored"))
        sp_passed, pe_passed, act_passed, v_passed, free = (ph.sem(n) for n in (
            "sp_passed", "pe_passed", "act_passed", "v_passed", "free"))
        CH = D // 4
        with nc.Block() as block:
            @block.sync
            def _(sp):
                sp.wait_ge(zeroed, 1)
                sp.dma_start(w[:], fc_w.rearrange("(k p) c -> p k c", p=P)).then_inc(loaded, 16)
                sp.dma_start(b[:], fc_b).then_inc(loaded, 16)
                for m in range(DC):
                    for c in range(2):
                        sp.dma_start(mix[c * CH:(c + 1) * CH, m, c * CH:(c + 1) * CH], ch_w[2 * m + c]).then_inc(loaded, 16)
                with sp.Fori(0, NG) as i:
                    hold(sp, ready, i + 2, sp_passed)
                    sp.dma_start(node_rows(table, i, D), rows[:]).then_inc(stored, 16)
                    hold(sp, stored, i * 16 + 16, free)

            @block.tensor
            def _(pe):
                pe.wait_ge(loaded, 96)
                with pe.Fori(0, NG) as i:
                    hold(pe, hid, i + 1, pe_passed)
                    for m in range(DC):
                        for half in range(2):
                            for k in range(DC):
                                last = pe.matmul(psum_h[:, m, half, 0:HALF], w[:, k, m * P:(m + 1) * P],
                                                 xT[:, k, bass.ds(i * UNIT + half * HALF, HALF)],
                                                 start=(k == 0), stop=(k == DC - 1))
                    last.then_inc(made, 1)
                    hold(pe, hid, i + 2, pe_passed)
                    hold(pe, ready, i + 1, pe_passed)
                    for t in range(GRP):
                        for m in range(DC):
                            last = pe.matmul(psum_y[:, t // 2, t % 2, m * P:(m + 1) * P], hidden[:, m, t * P:(t + 1) * P],
                                             mix[:, m, :], start=True, stop=True)
                    last.then_inc(mixed, 1)

            @block.scalar
            def _(act):
                act.sem_inc(hid, 1)
                with act.Fori(0, NG) as i:
                    hold(act, made, i + 1, act_passed)
                    for m in range(DC):
                        last = act.activation(hidden[:, m].rearrange("p (a n) -> p a n", a=2), psum_h[:, m, :, 0:HALF],
                                              ACT.Identity, bias=b[:, m:m + 1])
                    last.then_inc(hid, 1)

            @block.vector
            def _(v):
                v.memset(mix[:], 0.0).then_inc(zeroed, 1)
                v.sem_inc(ready, 1)
                v.sem_inc(free, 1)
                with v.Fori(0, NG) as i:
                    hold(v, mixed, i + 1, v_passed)
                    hold(v, free, i + 1, v_passed)
                    flat = psum_y[:].rearrange("p a b f -> p (a b) f")[:, 0:GRP, :]
                    v.tensor_tensor(rows[:], flat, wide(scale[:, bass.ds(i * GRP, GRP)], 2, D), ALU.mult)
                    v.drain()
                    v.sem_inc(ready, 1)


def add_product(nc, C, xT, weight, bias=None):
    with phase(nc) as ph:
        w = ph.sb("w", [P, DC, D])
        b = ph.sb("b", [P, D])
        x = ph.sb("x", [P, DC, UNIT])
        staged, act_passed = ph.sem("staged"), ph.sem("act_passed")
        psum = ph.ps("psum", [P, GRP, 512])
        loaded, made, taken = ph.sem("loaded"), ph.sem("made"), ph.sem("taken")
        v_passed, pe_passed = ph.sem("v_passed"), ph.sem("pe_passed")
        loads = 16 * (1 + (bias is not None))
        with nc.Block() as block:
            @block.sync
            def _(sp):
                sp.dma_start(w[:], weight.rearrange("(k p) c -> p k c", p=P)).then_inc(loaded, 16)
                if bias is not None:
                    sp.dma_start(b[:], bias.broadcast_to([P, D])).then_inc(loaded, 16)

            @block.tensor
            def _(pe):
                pe.wait_ge(loaded, loads)
                with pe.Fori(0, NG) as i:
                    hold(pe, taken, i + 1, pe_passed)
                    hold(pe, staged, i + 1, pe_passed)
                    for s in range(GRP):
                        for k in range(DC):
                            last = pe.matmul(psum[:, s, 0:D], x[:, k, s * P:(s + 1) * P], w[:, k, :],
                                             start=(k == 0), stop=(k == DC - 1))
                    last.then_inc(made, 1)

            @block.scalar
            def _(act):
                act.sem_inc(made, 1)
                with act.Fori(0, NG) as i:
                    hold(act, made, i + 1, act_passed)
                    act.activation(x[:], xT[:, :, bass.ds(i * UNIT, UNIT)], ACT.Copy).then_inc(staged, 1)

            @block.vector
            def _(v):
                v.sem_inc(taken, 1)
                v.wait_ge(loaded, loads)
                with v.Fori(0, NG) as i:
                    tiles = bass.ds(i * GRP, GRP)
                    hold(v, made, i + 2, v_passed)
                    v.tensor_tensor(C.X[:, tiles, :], C.X[:, tiles, :], psum[:, :, 0:D], ALU.add).then_inc(taken, 1)
                    v.drain()
                    if bias is not None:
                        v.tensor_tensor(C.X[:, tiles, :], C.X[:, tiles, :], wide(b[:], 1, GRP), ALU.add)
                        v.drain()


def take_top_nodes(nc, C, weights, gates, K):
    table = nc.dram_tensor("router_weights", (NT, P), F32, kind="Internal").ap()
    with phase(nc) as ph:
        row = ph.sb("row", [P, NP])
        junk = ph.sb("junk", [P, NP])
        rank = ph.sb("rank", [P, 4, NT])
        total = ph.sb("total", [P, NT])
        turned = ph.sb("turned", [NT, P])
        psum = ph.ps("psum", [P, 512])
        turned_in, copied, stored, spread = (ph.sem(n) for n in ("turned_in", "copied", "stored", "spread"))
        with nc.Block() as block:
            @block.tensor
            def _(pe):
                pe.transpose(psum[0:NT, 0:P], weights[:, :, 0], C.ident[:]).then_inc(turned_in, 1)

            @block.sync
            def _(sp):
                sp.wait_ge(copied, 1)
                sp.dma_start(table, turned[:]).then_inc(stored, 16)
                sp.wait_ge(stored, 16)
                sp.dma_start(row[:], table.rearrange("(o t) q -> o (t q)", o=1).broadcast_to([P, NP])).then_inc(spread, 16)

            @block.vector
            def _(v):
                v.memset(rank[:], 0.0)
                v.wait_ge(turned_in, 1)
                v.tensor_copy(turned[:], psum[0:NT, 0:P]).then_inc(copied, 1)
                v.wait_ge(spread, 16)
                v.drain()

                def count(k, t, lo, hi, op, by):
                    v.scalar_tensor_tensor(junk[:, lo:hi], row[:, lo:hi], weights[:, t, 0:1], by, op, ALU.mult,
                                           accum_out=rank[:, k, t:t + 1])
                    v.drain()

                for t in range(NT):
                    at, end = t * P, min((t + 1) * P, N)
                    if at:
                        count(0, t, 0, at, ALU.is_ge, C.ones[:, 0:1].broadcast_to([P, at]))
                    if end < N:
                        count(1, t, end, N, ALU.is_gt, C.ones[:, 0:1].broadcast_to([P, N - end]))
                    count(2, t, at, end, ALU.is_gt, C.ones[:, 0:end - at])
                    count(3, t, at, end, ALU.is_equal, C.below[:, 0:end - at])
                v.tensor_reduce(total[:], rank[:].rearrange("p k t -> p t k"), AX.X, ALU.add)
                v.drain()
                v.scalar_tensor_tensor(gates[:, :, 0], total[:], float(K), weights[:, :, 0], ALU.is_lt, ALU.mult)


def score_experts(nc, C, table, b_gat, gamma, beta, logits):
    F, E = 16, 4
    with phase(nc) as ph:
        agg = ph.sb("agg", [P, NT, F])
        sq = ph.sb("sq", [P, NT, F])
        rows = ph.sb("rows", [P, 3, F])
        mean = ph.sb("mean", [P, NT])
        var = ph.sb("var", [P, NT])
        loaded, have_var, rooted = ph.sem("loaded"), ph.sem("have_var"), ph.sem("rooted")
        with nc.Block() as block:
            @block.sync
            def _(sp):
                sp.dma_start(agg[:], table.rearrange("(t p) f -> p t f", p=P)).then_inc(loaded, 16)
                for k, of in enumerate((b_gat, gamma, beta)):
                    sp.dma_start(rows[:, k, :], of.broadcast_to([P, F])).then_inc(loaded, 16)

            @block.scalar
            def _(act):
                act.wait_ge(have_var, 1)
                act.activation(var[:], var[:], ACT.Sqrt).then_inc(rooted, 1)

            @block.vector
            def _(v):
                v.wait_ge(loaded, 64)
                v.tensor_tensor(agg[:], agg[:], wide(rows[:, 0], 1, NT), ALU.add)
                v.drain()
                v.tensor_reduce(mean[:], agg[:], AX.X, ALU.add)
                v.drain()
                v.tensor_scalar(mean[:], mean[:], 1.0 / F, None, ALU.mult)
                v.drain()
                v.tensor_tensor(agg[:], agg[:], wide(mean[:], 2, F), ALU.subtract)
                v.drain()
                v.tensor_tensor(sq[:], agg[:], agg[:], ALU.mult)
                v.drain()
                v.tensor_reduce(var[:], sq[:], AX.X, ALU.add)
                v.drain()
                v.tensor_scalar(var[:], var[:], 1.0 / F, LN_EPS, ALU.mult, ALU.add).then_inc(have_var, 1)
                v.wait_ge(rooted, 1)
                v.reciprocal(mean[:], var[:])
                v.drain()
                v.tensor_tensor(agg[:], agg[:], wide(mean[:], 2, F), ALU.mult)
                v.drain()
                v.tensor_tensor(agg[:], agg[:], wide(rows[:, 1], 1, NT), ALU.mult)
                v.drain()
                v.tensor_tensor(agg[:], agg[:], wide(rows[:, 2], 1, NT), ALU.add)
                v.drain()
                v.tensor_reduce(logits[:], agg[:].rearrange("p t (h e) -> p t e h", e=E), AX.X, ALU.add)
                v.drain()
                v.tensor_scalar(logits[:], logits[:], E / F, None, ALU.mult)


def build(nc, a, out, layers=8):
    class C:
        pass

    with ExitStack() as ctx:
        def sb(name, shape, dt=F32):
            return ctx.enter_context(nc.sbuf_tensor(name, shape, dt))

        def dram(name, shape):
            return nc.dram_tensor(name, shape, F32, kind="Internal").ap()

        C.X = sb("node_features", [P, NT, D])
        C.ident, C.ones, C.below, C.above, C.iota_row = (
            sb(n, [P, P]) for n in ("ident", "ones", "below", "above", "iota_row"))
        C.iota_col = sb("iota_col", [P, 1])
        C.node_i = sb("node_i", [P, NT], I32)
        build_constants(nc, C, a["x"])
        main = Graph(nc, sb, "main", a["dst_rows"].shape[0], True)
        sort_edges(nc, C, main, a["dst_rows"], a["dst_cols"], a["src_cols"], a["w_cols"])

        def store_and_stop():
            with phase(nc) as ph:
                sent = ph.sem("sent")
                with nc.Block() as block:
                    @block.sync
                    def _(sp):
                        sp.dma_start(out[0:(NT - 1) * P, :].rearrange("(t p) f -> p t f", p=P),
                                     C.X[:, 0:NT - 1, :]).then_inc(sent, 16)
                        sp.dma_start(out[(NT - 1) * P:N, :], C.X[0:N - (NT - 1) * P, NT - 1, :]).then_inc(sent, 16)
                        sp.wait_ge(sent, 32)

        @contextmanager
        def turned(cols=D, **kw):
            with nc.sbuf_tensor(f"xT_{Phase.count}", [P, cols // P, NP], F32) as xT:
                turn(nc, C, xT, cols=cols, **kw)
                yield xT

        @contextmanager
        def rows(*shapes):
            with ExitStack() as c:
                n = Phase.count
                yield [c.enter_context(nc.sbuf_tensor(f"row{k}_{n}", list(s), F32)) for k, s in enumerate(shapes)]

        @contextmanager
        def split_features():
            n = Phase.count
            with nc.sbuf_tensor(f"x_high_{n}", [P, DC, NP], F32R) as high:
                with nc.sbuf_tensor(f"x_low_{n}", [P, DC, NP], F32R) as low:
                    yield high, low

        def moe(parts, layer, gates, E, H, func):
            experts(nc, C, parts, gates, E, H, func, *(a[f"L{layer}_ffn_{n}"] for n in ("w1", "b1", "w2", "b2")))

        source, target = dram("l0_source", (NP, D + 4)), dram("l0_target", (NP, 4))
        with turned() as xT, rows((P, 2, D)) as (att,):
            load_rows(nc, [(att[:, k, :], a["L0_gnn_att"][k:k + 1, :].broadcast_to([P, D])) for k in range(2)])

            def scores(v, r, scratch, tiles):
                for k in range(2):
                    v.tensor_tensor(scratch[:], r[:, :, 0:D], wide(att[:, k], 1, GRP), ALU.mult)
                    v.drain()
                    v.tensor_reduce(r[:, :, D + 4 * k:D + 4 * k + 4],
                                    scratch[:].rearrange("p t (h f) -> p t h f", h=4), AX.X, ALU.add)
                    v.drain()

            project(nc, C, xT, a["L0_gnn_W"], D, [(source, 0, D + 4), (target, D + 4, 4)], post=scores, extra=8)
        edge_pass(nc, C, Pass(main, source, target, D, D + 4, 4, 0.01, "sum", "f", main.is_edge, dead=-1000.0),
                  None, ToNodes(C))
        if layers == 1:
            return store_and_stop()

        with rows((P, NT, 8)) as (gates,), split_features() as parts:
            with turned(parts=parts) as xT, rows((P, NT, 8)) as (logits,):
                logits_of(nc, C, xT, a["L0_ffn_gate_w"], a["L0_ffn_gate_b"], 8, logits)
                choose_experts(nc, C, logits, gates, 8, 2, False)
            moe(parts, 0, gates, 8, 512, ACT.Gelu)
        if layers == 2:
            return store_and_stop()

        source, target = dram("l1_source", (NP, D + 8)), dram("l1_target", (NP, 8))
        with turned(keep_table=source) as xT:
            project(nc, C, xT, a["L1_gnn_W"], 16, [(source[:, D:D + 8], 0, 8), (target, 8, 8)], bias=a["L1_gnn_b"])
        edge_pass(nc, C, Pass(main, source, target, D, D + 8, 8, 0.2, "sum", "h", main.is_edge), None, ToNodes(C))
        if layers == 3:
            return store_and_stop()

        with rows((P, NT, 1)) as (gates,), split_features() as parts:
            with turned(add=True, parts=parts) as xT, rows((P, NT, 1)) as (weights,):
                logits_of(nc, C, xT, a["L1_ffn_wr"], a["L1_ffn_br"], 1, weights)
                take_top_nodes(nc, C, weights, gates, max(1, N // 2) - 1)
            moe(parts, 1, gates, 1, 1024, ACT.Gelu_apprx_tanh)
        if layers == 4:
            return store_and_stop()

        mixed, conv = dram("l2_mixed", (NP, D)), dram("l2_conv", (NP, D))
        for step in range(3):
            with (turned() if step == 0 else turned(table=conv, norm=False)) as xT:
                if step:
                    add_product(nc, C, xT, a["L2_gnn_mlp_w"][(step - 1) * D:step * D, :])
                channel_mix(nc, C, xT, a["L2_gnn_fc_w"][step], a["L2_gnn_fc_b"][:, step * DC:(step + 1) * DC],
                            a["L2_gnn_ch_w"][step], main.norm_out, mixed)
            with rows((P, D)) as (bias,):
                load_rows(nc, [(bias[:], a["L2_gnn_ch_b"][step:step + 1, :].broadcast_to([P, D]))])
                edge_pass(nc, C, Pass(main, mixed, None, D, D, 1, None, "weight", "f", None), None,
                          ToTable(conv, D, bias=bias, scale=main.norm_in))
        with turned(table=conv, norm=False) as xT:
            add_product(nc, C, xT, a["L2_gnn_mlp_w"][2 * D:3 * D, :], bias=a["L2_gnn_mlp_b"])
        if layers == 5:
            return store_and_stop()

        source, target, agg = dram("l2_source", (NP, 20)), dram("l2_target", (NP, 4)), dram("l2_agg", (NP, 16))
        with rows((P, NT, 4)) as (gates,), ExitStack() as gc:
            route = Graph(nc, lambda n, s, d: gc.enter_context(nc.sbuf_tensor(n, s, d)), "route",
                          a["route_dst_rows"].shape[0], False)
            sort_edges(nc, C, route, a["route_dst_rows"], a["route_dst_cols"], a["route_src_cols"], None)
            with split_features() as parts:
                with turned(parts=parts) as xT, rows((P, 2, 16)) as (att,):
                    load_rows(nc, [(att[:, k, :], a["L2_ffn_att"][k:k + 1, :].broadcast_to([P, 16])) for k in range(2)])

                    def scores(v, r, scratch, tiles):
                        for k in range(2):
                            v.tensor_tensor(scratch[:], r[:, :, 0:16], wide(att[:, k], 1, GRP), ALU.mult)
                            v.drain()
                            v.tensor_reduce(r[:, :, 16 + 4 * k:20 + 4 * k],
                                            scratch[:].rearrange("p t (h f) -> p t h f", h=4), AX.X, ALU.add)
                            v.drain()

                    project(nc, C, xT, a["L2_ffn_W_gat"], 16, [(source, 0, 20), (target, 20, 4)], post=scores, extra=8)
                edge_pass(nc, C, Pass(route, source, target, 16, 20, 4, 0.2, "sum", "f", route.is_any), None,
                          ToTable(agg, 16, raw=True))
                with rows((P, NT, 4)) as (logits,):
                    score_experts(nc, C, agg, a["L2_ffn_b_gat"], a["L2_ffn_ln_gamma"], a["L2_ffn_ln_beta"], logits)
                    choose_experts(nc, C, logits, gates, 4, 2, True)
                moe(parts, 2, gates, 4, 512, ACT.Gelu)
        if layers == 6:
            return store_and_stop()

        pairs = [[dram(f"l3_{side}{k}", (NP, D + 2)) for k in range(2)] for side in ("left", "right")]
        singles = [dram(f"l3_{side}", (NP, D + 1)) for side in ("left", "right")]
        hidden = dram("l3_hidden", (NP, 2 * D))
        slope = 0.2

        def linear_part(att, H):
            def scores(v, r, scratch, tiles):
                v.tensor_tensor(scratch[:], r[:, :, 0:D], wide(att[:], 1, GRP), ALU.mult)
                v.drain()
                v.tensor_reduce(r[:, :, D:D + H], scratch[:].rearrange("p t (h f) -> p t h f", h=H), AX.X, ALU.add)
            return scores

        with rows((P, D), (P, D), (P, DC), (P, D), (P, D), (P, DC), (P, D), (P, D), (P, DC)) as kept:
            att, bias, att_col = kept[0::3], kept[1::3], kept[2::3]
            of = [(a["L3_gnn_a1"][0:1], a["L3_gnn_b1"][0:1], a["L3_gnn_a1_cols"][:, 0:2]),
                  (a["L3_gnn_a1"][1:2], a["L3_gnn_b1"][1:2], a["L3_gnn_a1_cols"][:, 2:4]),
                  (a["L3_gnn_a2"], a["L3_gnn_b2"], a["L3_gnn_a2_cols"])]
            load_rows(nc, [(att[k][:], of[k][0].broadcast_to([P, D])) for k in range(3)]
                      + [(bias[k][:], of[k][1].broadcast_to([P, D])) for k in range(3)]
                      + [(att_col[k][:], of[k][2]) for k in range(3)],
                      scales=[(att[k][:], slope) for k in range(3)] + [(att_col[k][:], 1 - slope) for k in range(3)])

            def att_of(k):
                return wide(att_col[k][:], 2, 2)

            with turned() as xT:
                for side, name in enumerate(("W1l", "W1r")):
                    for k in range(2):
                        project(nc, C, xT, a[f"L3_gnn_{name}"][:, k * D:(k + 1) * D], D, [(pairs[side][k], 0, D + 2)],
                                post=linear_part(att[k], 2), extra=2)
            for k in range(2):
                edge_pass(nc, C, Pass(main, pairs[0][k], pairs[1][k], D, D + 2, 2, slope, "att", "f", main.is_any),
                          att_of(k), ToTable(hidden[:, k * D:(k + 1) * D], D, bias=bias[k]))
            with turned(cols=2 * D, table=hidden, norm=False) as xT:
                for side, name in enumerate(("W2l", "W2r")):
                    project(nc, C, xT, a[f"L3_gnn_{name}"], D, [(singles[side], 0, D + 1)], K=2 * D,
                            post=linear_part(att[2], 1), extra=1)
            edge_pass(nc, C, Pass(main, singles[0], singles[1], D, D + 1, 1, slope, "att", "f", main.is_any),
                      att_of(2), ToNodes(C, bias[2]))
        if layers == 7:
            return store_and_stop()

        with rows((P, NT, 8)) as (gates,), split_features() as parts:
            with turned(parts=parts) as xT, rows((P, NT, 8)) as (logits,):
                logits_of(nc, C, xT, a["L3_ffn_Wg"], a["L3_ffn_bg"], 8, logits)
                choose_experts(nc, C, logits, gates, 8, 2, True)
            moe(parts, 3, gates, 8, 1024, ACT.Relu)
        store_and_stop()


LAYERS = 8


def edge_lists(src, dst):
    tiles = -(-len(dst) // (8 * P)) * 8
    pad = (0, tiles * P - len(dst))
    src, dst = (np.pad(v, pad, constant_values=NP - 1).reshape(tiles, P) for v in (src, dst))
    return dst, np.ascontiguousarray(dst.T), np.ascontiguousarray(src.T)


def kernel(**inputs):
    import concourse.bacc as bacc
    from concourse.bass_utils import run_bass_kernel_spmd

    i = {k: np.asarray(v) for k, v in inputs.items()}

    def columns(b):
        return b.reshape(-1, P).T

    def blocks(w):
        return w.reshape(DC, P, -1).transpose(1, 0, 2)

    a = {"x": i["x"]}
    a["dst_rows"], a["dst_cols"], a["src_cols"] = edge_lists(i["src"], i["dst"])
    tiles = a["dst_rows"].shape[0]
    a["w_cols"] = np.pad(i["edge_weight"], (0, tiles * P - len(i["dst"]))).reshape(tiles, P).T
    a["route_dst_rows"], a["route_dst_cols"], a["route_src_cols"] = edge_lists(*i["L2_ffn_edge_index"])
    a["L0_gnn_W"] = i["L0_gnn_W"].transpose(1, 0, 2).reshape(D, D)
    a["L0_gnn_att"] = i["L0_gnn_att"].reshape(4, 2, 64).transpose(1, 0, 2).reshape(2, D)
    a["L0_ffn_gate_w"] = blocks(i["L0_ffn_gate_w"])
    a["L0_ffn_gate_b"] = i["L0_ffn_gate_b"].reshape(1, 8)
    for layer, names in ((0, ("W1", "b1", "W2", "b2")), (1, ("w1", "b1", "w2", "b2")),
                         (2, ("W1", "b1", "W2", "b2")), (3, ("W1", "b1", "W2", "b2"))):
        w1, b1, w2, b2 = (i[f"L{layer}_ffn_{n}"] for n in names)
        if layer == 1:
            w1, w2 = w1[None], w2[None]
        if layer == 3:
            w1, w2 = w1.transpose(0, 2, 1), w2.transpose(0, 2, 1)
        a[f"L{layer}_ffn_w1"], a[f"L{layer}_ffn_w2"] = w1, w2
        a[f"L{layer}_ffn_b1"], a[f"L{layer}_ffn_b2"] = columns(b1), b2.reshape(-1, D)
    a["L1_gnn_W"] = np.concatenate([i["L1_gnn_W_u"], i["L1_gnn_W_v"]]).T
    a["L1_gnn_b"] = np.pad(i["L1_gnn_b_u"], (0, 8)).reshape(1, 16)
    a["L1_ffn_wr"] = blocks(i["L1_ffn_wr"])
    a["L1_ffn_br"] = i["L1_ffn_br"].reshape(1, 1)
    a["L2_gnn_fc_w"] = i["L2_gnn_fc_w"].transpose(0, 2, 1)
    a["L2_gnn_fc_b"] = columns(i["L2_gnn_fc_b"])
    a["L2_gnn_ch_w"] = i["L2_gnn_ch_w"]
    a["L2_gnn_ch_b"] = i["L2_gnn_ch_b"].reshape(3, D)
    a["L2_gnn_mlp_w"] = i["L2_gnn_mlp_w"].T
    a["L2_gnn_mlp_b"] = i["L2_gnn_mlp_b"].reshape(1, D)
    a["L2_ffn_W_gat"] = i["L2_ffn_W_gat"]
    a["L2_ffn_att"] = np.stack([i["L2_ffn_att_src"].reshape(16), i["L2_ffn_att_dst"].reshape(16)])
    for n in ("b_gat", "ln_gamma", "ln_beta"):
        a[f"L2_ffn_{n}"] = i[f"L2_ffn_{n}"].reshape(1, 16)
    for n in ("W1l", "W1r", "W2l", "W2r"):
        a[f"L3_gnn_{n}"] = i[f"L3_gnn_{n}"]
    a["L3_gnn_a1"] = i["L3_gnn_a1"].reshape(2, D)
    a["L3_gnn_a1_cols"] = columns(i["L3_gnn_a1"])
    a["L3_gnn_a2_cols"] = columns(i["L3_gnn_a2"])
    a["L3_gnn_b1"] = i["L3_gnn_b1"].reshape(2, D)
    a["L3_gnn_a2"] = i["L3_gnn_a2"].reshape(1, D)
    a["L3_gnn_b2"] = i["L3_gnn_b2"].reshape(1, D)
    a["L3_ffn_Wg"] = blocks(i["L3_ffn_Wg"].T)
    a["L3_ffn_bg"] = i["L3_ffn_bg"].reshape(1, 8)

    nc = bacc.Bacc("TRN2", target_bir_lowering=False, num_devices=1)
    arrays = {f"in_{k}": np.ascontiguousarray(v) for k, v in a.items()}
    aps = {k: nc.dram_tensor(f"in_{k}", arrays[f"in_{k}"].shape, mybir.dt.from_np(arrays[f"in_{k}"].dtype),
                             kind="ExternalInput").ap() for k in a}
    out = nc.dram_tensor("out", (N, D), F32, kind="ExternalOutput").ap()
    build(nc, aps, out, LAYERS)
    result = run_bass_kernel_spmd(nc, [arrays], core_ids=[0])
    return result.results[0]["out"]
```

```python
from contextlib import ExitStack, contextmanager

import numpy as np

import concourse.bass as bass
from concourse import mybir

F32 = mybir.dt.float32
BF16 = mybir.dt.bfloat16
F32R = mybir.dt.float32r
I32 = mybir.dt.int32
ALU = mybir.AluOpType
ACT = mybir.ActivationFunctionType
AX = mybir.AxisListType

P = 128
D = 256
N = 3125
NT = -(-N // P)
NP = NT * P
GRP = 5
NG = NT // GRP
SLOTS = 4
DC = D // P
UNIT = GRP * P
HALF = UNIT // 2
LN_EPS = 1e-5
MASKED = 1e30
APART = 1e38
TAB = D + 8


class Phase:

    count = 0

    def __init__(self, nc, ctx):
        self.nc, self.ctx, self.sems = nc, ctx, []
        Phase.count += 1
        self.n = Phase.count

    def sb(self, name, shape, dt=F32):
        return self.ctx.enter_context(self.nc.sbuf_tensor(f"{name}_{self.n}", shape, dt))

    def ps(self, name, shape, dt=F32):
        return self.ctx.enter_context(self.nc.psum_tensor(f"{name}_{self.n}", shape, dt))

    def sem(self, name):
        self.sems.append(self.nc.alloc_semaphore(f"{name}_{self.n}"))
        return self.sems[-1]

    def sem_ring(self, name, n):
        return [self.sem(f"{name}{i}") for i in range(n)]


@contextmanager
def phase(nc):
    with ExitStack() as ctx:
        ph = Phase(nc, ctx)
        yield ph
        nc.clear_and_free_semaphores(ph.sems)
        nc.all_engine_barrier()


def hold(eng, sem, value, passed):
    eng.wait_ge(sem, value)
    eng.sem_inc(passed, 1)


def wide(ap, dim, n):
    ap = ap.unsqueeze(dim)
    shape = list(ap.shape)
    shape[dim] = n
    return ap.broadcast_to(shape)


def build_constants(nc, C, x):
    with phase(nc) as ph:
        loaded, filled, made = ph.sem("loaded"), ph.sem("filled"), ph.sem("made")
        iota_i = ph.sb("iota_i", [P, P], I32)
        col_i = ph.sb("col_i", [P, 1], I32)
        with nc.Block() as block:
            @block.sync
            def _(sp):
                sp.wait_ge(filled, 1)
                sp.dma_start(C.X[:, 0:NT - 1, :],
                             x[0:(NT - 1) * P, :].rearrange("(t p) f -> p t f", p=P)).then_inc(loaded, 16)
                sp.dma_start(C.X[0:N - (NT - 1) * P, NT - 1, :], x[(NT - 1) * P:N, :]).then_inc(loaded, 16)
                sp.wait_ge(loaded, 32)

            @block.vector
            def _(v):
                v.memset(C.X[:, NT - 1, :], 0.0).then_inc(filled, 1)
                v.memset(C.ones[:], 1.0)
                v.wait_ge(made, 9)
                v.tensor_copy(C.iota_row[:], iota_i[:])
                v.tensor_copy(C.iota_col[:], col_i[:])

            @block.gpsimd
            def _(pool):
                pool.memset(C.ident[:], 0.0).then_inc(made, 1)
                pool.memset(C.below[:], 1.0).then_inc(made, 1)
                pool.memset(C.above[:], 1.0).then_inc(made, 1)
                pool.wait_ge(made, 3)
                pool.affine_select(out=C.ident[:], in_=C.ident[:], compare_op=ALU.not_equal, fill=1.0,
                                   base=0, pattern=[[-1, P]], channel_multiplier=1).then_inc(made, 1)
                pool.affine_select(out=C.below[:], in_=C.below[:], compare_op=ALU.is_gt, fill=0.0,
                                   base=0, pattern=[[-1, P]], channel_multiplier=1).then_inc(made, 1)
                pool.affine_select(out=C.above[:], in_=C.above[:], compare_op=ALU.is_gt, fill=0.0,
                                   base=0, pattern=[[1, P]], channel_multiplier=-1).then_inc(made, 1)
                pool.iota(iota_i[:], pattern=[[1, P]], base=0, channel_multiplier=0).then_inc(made, 1)
                pool.iota(col_i[:], pattern=[[0, 1]], base=0, channel_multiplier=1).then_inc(made, 1)
                pool.iota(C.node_i[:], pattern=[[P, NT]], base=0, channel_multiplier=1).then_inc(made, 1)


class Graph:

    def __init__(self, nc, sb, name, tiles, degrees):
        rows = -(-(tiles * P + NP * SLOTS) // (P * SLOTS))
        self.name, self.T, self.R = name, tiles, rows
        self.records = nc.dram_tensor(f"records_{name}", (P * rows * SLOTS, 4), I32, kind="Internal").ap()
        self.cont = sb(f"cont_{name}", [P, rows + 1], F32)
        self.apart = sb(f"apart_{name}", [P, rows + 1], F32)
        self.in_first = sb(f"in_first_{name}", [P, rows], F32)
        self.in_last = sb(f"in_last_{name}", [P, rows], F32)
        self.carry = sb(f"carry_{name}", [P, P], F32)
        self.from_prev = sb(f"from_prev_{name}", [P, P], F32)
        self.from_next = sb(f"from_next_{name}", [P, P], F32)
        self.ends_here = sb(f"ends_here_{name}", [P, 1], F32)
        self.first_node = sb(f"first_node_{name}", [P, NT], F32)
        self.end_row = sb(f"end_row_{name}", [P, NT], I32)
        self.last_node = sb(f"last_node_{name}", [P, 1], I32)
        self.is_edge = sb(f"is_edge_{name}", [P, rows, SLOTS], F32)
        self.is_any = sb(f"is_any_{name}", [P, rows, SLOTS], F32)
        if degrees:
            self.weight = sb(f"weight_{name}", [P, rows, SLOTS + 1], F32)
            self.norm_in = sb(f"norm_in_{name}", [P, NT], F32)
            self.norm_out = sb(f"norm_out_{name}", [P, NT], F32)
        self.degrees = degrees


def sort_edges(nc, C, g, dst_rows, dst_cols, src_cols, w_cols):
    T, R = g.T, g.R
    COUNT = max(s for s in range(1, 512 // NT + 1) if T % (2 * s) == 0)
    PLACE = max(s for s in range(1, 9) if T % (2 * s) == 0)
    with ExitStack() as outer:
        def keep(name, shape, dt=F32):
            return outer.enter_context(nc.sbuf_tensor(f"{name}_{g.name}", shape, dt))

        counts = keep("counts", [P, T, NT])
        offset = keep("offset", [P, T, NT])
        dst_i = keep("dst_i", [P, T], I32)
        src_i = keep("src_i", [P, T], I32)
        w_f = keep("w_f", [P, T])
        dst_f = keep("dst_f", [P, T])
        dst_lo = keep("dst_lo", [P, T])
        loop_slot = keep("loop_slot", [P, NT], I32)
        out_count = keep("out_count", [P, COUNT * NT])
        SUB, TURNS = COUNT, T // (2 * COUNT)

        with phase(nc) as ph:
            tmp_i = ph.sb("tmp_i", [P, T], I32)
            dst_hi = ph.sb("dst_hi", [P, T])
            src_hi = ph.sb("src_hi", [P, T])
            src_lo = ph.sb("src_lo", [P, T])
            blank = ph.sb("blank", [P, R * SLOTS, 4], I32)
            oh_hi = ph.sb("oh_hi", [P, 2, 2, SUB, P], BF16)
            oh_lo = ph.sb("oh_lo", [P, 2, 2, SUB, NT], BF16)
            psum = ph.ps("psum", [P, 2, 2, 512])
            loaded, blanked, blank_sent = ph.sem("loaded"), ph.sem("blanked"), ph.sem("blank_sent")
            hot_ready = ph.sem_ring("hot_ready", 2)
            counted, taken, added = ph.sem_ring("counted", 2), ph.sem_ring("taken", 2), ph.sem_ring("added", 2)
            pe_passed, act_passed, v_passed = ph.sem("pe_passed"), ph.sem("act_passed"), ph.sem("v_passed")
            both = [("dst", dst_hi, dst_lo)] + ([("src", src_hi, src_lo)] if g.degrees else [])
            with nc.Block() as block:
                @block.sync
                def _(sp):
                    sp.dma_start(dst_i[:], dst_cols).then_inc(loaded, 16)
                    sp.dma_start(src_i[:], src_cols).then_inc(loaded, 16)
                    if g.degrees:
                        sp.dma_start(w_f[:], w_cols).then_inc(loaded, 16)
                    sp.wait_ge(blanked, 1)
                    sp.dma_start(g.records.rearrange("(p s) c -> p s c", p=P), blank[:]).then_inc(blank_sent, 16)
                    sp.wait_ge(blank_sent, 16)

                @block.vector
                def _(v):
                    v.memset(blank[:], 0)
                    v.memset(out_count[:], 0.0)
                    if not g.degrees:
                        v.memset(w_f[:], 0.0)
                    v.drain()
                    v.memset(blank[:, :, 3], NP - 1).then_inc(blanked, 1)
                    v.wait_ge(loaded, 48 if g.degrees else 32)
                    v.tensor_copy(dst_f[:], dst_i[:])
                    for (_, hi, lo), ends in zip(both, (dst_i, src_i)):
                        v.drain()
                        v.tensor_scalar(tmp_i[:], ends[:], P - 1, None, ALU.bitwise_and)
                        v.drain()
                        v.tensor_copy(hi[:], tmp_i[:])
                        v.drain()
                        v.tensor_scalar(tmp_i[:], ends[:], P.bit_length() - 1, None, ALU.logical_shift_right)
                        v.drain()
                        v.tensor_copy(lo[:], tmp_i[:])
                    v.drain()
                    with v.Fori(0, TURNS) as i:
                        for s in range(2):
                            hold(v, counted[s], i + 1, v_passed)
                            for k, (_, hi, lo) in enumerate(both):
                                at = bass.ds(i * (2 * SUB) + s * SUB, SUB)
                                v.tensor_tensor(oh_hi[:, s, k], wide(C.iota_row[:], 1, SUB),
                                                wide(hi[:, at], 2, P), ALU.is_equal)
                                last = v.tensor_tensor(oh_lo[:, s, k], wide(C.iota_row[:, 0:NT], 1, SUB),
                                                       wide(lo[:, at], 2, NT), ALU.is_equal)
                            last.then_inc(hot_ready[s], 1)
                        for s in range(2 if g.degrees else 0):
                            v.drain()
                            v.wait_ge(counted[s], i + 2)
                            v.tensor_tensor(out_count[:], out_count[:], psum[:, s, 1, 0:SUB * NT],
                                            ALU.add).then_inc(added[s], 1)

                @block.tensor
                def _(pe):
                    for s in range(2):
                        pe.sem_inc(counted[s], 1)
                    with pe.Fori(0, TURNS) as i:
                        for s in range(2):
                            hold(pe, hot_ready[s], i + 1, pe_passed)
                            hold(pe, taken[s], i + 1, pe_passed)
                            if g.degrees:
                                hold(pe, added[s], i + 1, pe_passed)
                            for k in range(len(both)):
                                for j in range(SUB):
                                    last = pe.matmul(psum[:, s, k, j * NT:(j + 1) * NT], oh_hi[:, s, k, j],
                                                     oh_lo[:, s, k, j], start=True, stop=True)
                            last.then_inc(counted[s], 1)

                @block.scalar
                def _(act):
                    for s in range(2):
                        act.sem_inc(taken[s], 1)
                        act.sem_inc(added[s], 1)
                    with act.Fori(0, TURNS) as i:
                        for s in range(2):
                            hold(act, counted[s], i + 2, act_passed)
                            act.activation(counts[:, bass.ds(i * (2 * SUB) + s * SUB, SUB), :],
                                           psum[:, s, 0, 0:SUB * NT].rearrange("p (j l) -> p j l", j=SUB),
                                           ACT.Copy).then_inc(taken[s], 1)

        with phase(nc) as ph:
            deg = ph.sb("deg", [P, NT])
            rows_f = ph.sb("rows_f", [P, NT])
            inc = ph.sb("inc", [P, NT])
            start = ph.sb("start", [P, NT])
            tmp_i = ph.sb("tmp_i", [P, NT], I32)
            tmp_f = ph.sb("tmp_f", [P, NT])
            total = ph.sb("total", [P, 1])
            norm = ph.sb("norm", [P, 2, NT])
            psum = ph.ps("psum", [P, 512])
            have_total, have_base, clipped, rooted = (ph.sem(n) for n in ("have_total", "have_base", "clipped", "rooted"))
            with nc.Block() as block:
                @block.vector
                def _(v):
                    for lo in range(NT):
                        v.tensor_tensor_scan(offset[:, :, lo], C.ones[:, 0:1].broadcast_to([P, T]),
                                             counts[:, :, lo], 0.0, ALU.mult, ALU.add)
                    v.drain()
                    v.tensor_copy(deg[:], offset[:, T - 1, :])
                    v.drain()
                    v.tensor_tensor(offset[:], offset[:], counts[:], ALU.subtract)
                    v.tensor_scalar(tmp_f[:], deg[:], float(SLOTS), None, ALU.add)
                    v.drain()
                    v.tensor_copy(tmp_i[:], tmp_f[:])
                    v.drain()
                    v.tensor_scalar(tmp_i[:], tmp_i[:], SLOTS.bit_length() - 1, None, ALU.logical_shift_right)
                    v.drain()
                    v.tensor_copy(rows_f[:], tmp_i[:])
                    v.drain()
                    v.tensor_tensor_scan(inc[:], C.ones[:, 0:1].broadcast_to([P, NT]), rows_f[:], 0.0,
                                         ALU.mult, ALU.add)
                    v.drain()
                    v.tensor_copy(total[:], inc[:, NT - 1:NT]).then_inc(have_total, 1)
                    v.tensor_tensor(start[:], inc[:], rows_f[:], ALU.subtract)
                    v.drain()
                    v.wait_ge(have_base, 1)
                    v.tensor_scalar(start[:], start[:], psum[:, 0:1], None, ALU.add)
                    v.drain()
                    v.tensor_tensor(tmp_f[:], start[:], rows_f[:], ALU.add)
                    v.drain()
                    v.tensor_scalar(tmp_f[:], tmp_f[:], 1.0, None, ALU.subtract)
                    v.drain()
                    v.tensor_copy(g.end_row[:], tmp_f[:])
                    v.tensor_scalar(start[:], start[:], float(SLOTS), None, ALU.mult)
                    v.drain()
                    v.tensor_tensor(offset[:], offset[:], wide(start[:], 1, T), ALU.add)
                    v.tensor_tensor(tmp_f[:], start[:], deg[:], ALU.add)
                    v.drain()
                    v.tensor_copy(loop_slot[:], tmp_f[:])
                    if g.degrees:
                        v.tensor_scalar(norm[:, 0], deg[:], 1.0, None, ALU.max)
                        v.tensor_reduce(norm[:, 1], out_count[:].rearrange("p (j l) -> p l j", j=COUNT), AX.X, ALU.add)
                        v.drain()
                        v.tensor_scalar(norm[:, 1], norm[:, 1], 1.0, None, ALU.max).then_inc(clipped, 1)
                        v.wait_ge(rooted, 1)
                        v.reciprocal(g.norm_in[:], norm[:, 0])
                        v.reciprocal(g.norm_out[:], norm[:, 1])

                @block.tensor
                def _(pe):
                    pe.wait_ge(have_total, 1)
                    pe.matmul(psum[:, 0:1], C.above[:], total[:], start=True, stop=True).then_inc(have_base, 1)

                @block.scalar
                def _(act):
                    if g.degrees:
                        act.wait_ge(clipped, 1)
                        act.activation(norm[:], norm[:], ACT.Sqrt).then_inc(rooted, 1)

        SUB, TURNS = PLACE, T // (2 * PLACE)

        with phase(nc) as ph:
            rows_i = ph.sb("rows_i", [P, 2, SUB * P], I32)
            rows_f = ph.sb("rows_f", [P, 2, SUB * P])
            hi_i = ph.sb("hi_i", [P, 2, SUB * P], I32)
            hot_t = ph.sb("hot_t", [P, 2, SUB * P])
            oh_lo = ph.sb("oh_lo", [P, 2, SUB, NT])
            picked = ph.sb("picked", [P, 2, SUB, NT])
            junk = ph.sb("junk", [P, P])
            dst_s = ph.sb("dst_s", [P, 2, SUB])
            rank = ph.sb("rank", [P, 2, SUB])
            place_f = ph.sb("place_f", [P, 2, SUB])
            place = ph.sb("place", [P, 2, SUB], I32)
            rec = ph.sb("rec", [P, 2, SUB, 4], I32)
            loop_rec = ph.sb("loop_rec", [P, NT, 4], I32)
            psum = ph.ps("psum", [P, 2, 512])
            rows_in, rows_used = ph.sem_ring("rows_in", 2), ph.sem_ring("rows_used", 2)
            hot_ready, looked_up, rec_ready, rec_sent, rec_free = (ph.sem_ring(n, 2) for n in (
                "hot_ready", "looked_up", "rec_ready", "rec_sent", "rec_free"))
            loops_ready, loops_sent = ph.sem("loops_ready"), ph.sem("loops_sent")
            sp_passed, v_passed, pe_passed, pool_passed = (ph.sem(n) for n in (
                "sp_passed", "v_passed", "pe_passed", "pool_passed"))
            with nc.Block() as block:
                @block.sync
                def _(sp):
                    with sp.Fori(0, TURNS) as i:
                        for s in range(2):
                            hold(sp, rows_used[s], i + 1, sp_passed)
                            sp.dma_start(rows_i[:, s, :],
                                         dst_rows[bass.ds(i * (2 * SUB) + s * SUB, SUB), :]
                                         .rearrange("(o t) q -> o (t q)", o=1)
                                         .broadcast_to([P, SUB * P])).then_inc(rows_in[s], 16)

                @block.vector
                def _(v):
                    for s in range(2):
                        v.sem_inc(rows_used[s], 1)
                    v.memset(rec[:], 1)
                    v.memset(loop_rec[:], 0)
                    v.drain()
                    v.memset(loop_rec[:, :, 2], 2)
                    v.tensor_copy(loop_rec[:, :, 0], C.node_i[:])
                    v.tensor_copy(loop_rec[:, :, 3], C.node_i[:]).then_inc(loops_ready, 1)
                    with v.Fori(0, TURNS) as i:
                        for s in range(2):
                            at = bass.ds(i * (2 * SUB) + s * SUB, SUB)
                            hold(v, rows_in[s], i * 16 + 16, v_passed)
                            v.tensor_scalar(hi_i[:, s], rows_i[:, s], P - 1, None, ALU.bitwise_and)
                            v.tensor_copy(rows_f[:, s], rows_i[:, s]).then_inc(rows_used[s], 1)
                            v.tensor_copy(dst_s[:, s], dst_f[:, at])
                            v.drain()
                            v.tensor_scalar(hot_t[:, s], hi_i[:, s], C.iota_col[:, 0:1], None,
                                            ALU.is_equal).then_inc(hot_ready[s], 1)
                            v.tensor_tensor(oh_lo[:, s], wide(C.iota_row[:, 0:NT], 1, SUB),
                                            wide(dst_lo[:, at], 2, NT), ALU.is_equal)
                            for j in range(SUB):
                                v.scalar_tensor_tensor(junk[:], rows_f[:, s, j * P:(j + 1) * P],
                                                       dst_s[:, s, j:j + 1], C.below[:], ALU.is_equal, ALU.mult,
                                                       accum_out=rank[:, s, j:j + 1])
                                v.drain()
                            hold(v, looked_up[s], i + 1, v_passed)
                            v.tensor_tensor(picked[:, s], oh_lo[:, s],
                                            psum[:, s, 0:SUB * NT].rearrange("p (j l) -> p j l", j=SUB), ALU.mult)
                            v.drain()
                            v.tensor_reduce(place_f[:, s], picked[:, s], AX.X, ALU.add)
                            v.drain()
                            v.tensor_tensor(place_f[:, s], place_f[:, s], rank[:, s], ALU.add)
                            v.drain()
                            hold(v, rec_free[s], i + 1, v_passed)
                            v.tensor_copy(place[:, s], place_f[:, s])
                            v.tensor_copy(rec[:, s, :, 0], src_i[:, at])
                            v.tensor_copy(rec[:, s, :, 1].bitcast(F32), w_f[:, at])
                            v.tensor_copy(rec[:, s, :, 3], dst_i[:, at]).then_inc(rec_ready[s], 1)

                @block.tensor
                def _(pe):
                    with pe.Fori(0, TURNS) as i:
                        for s in range(2):
                            hold(pe, hot_ready[s], i + 1, pe_passed)
                            for j in range(SUB):
                                last = pe.matmul(psum[:, s, j * NT:(j + 1) * NT], hot_t[:, s, j * P:(j + 1) * P],
                                                 offset[:, bass.ds(i * (2 * SUB) + s * SUB + j, 1), :]
                                                 .rearrange("p o l -> p (o l)"), start=True, stop=True)
                            last.then_inc(looked_up[s], 1)

                @block.scalar
                def _(act):
                    for s in range(2):
                        act.sem_inc(rec_free[s], 1)
                    with act.Fori(0, TURNS) as i:
                        for s in range(2):
                            hold(act, rec_sent[s], i * (16 * SUB) + 16 * SUB, rec_free[s])

                @block.gpsimd
                def _(pool):
                    with pool.Fori(0, TURNS) as i:
                        for s in range(2):
                            hold(pool, rec_ready[s], i + 1, pool_passed)
                            for j in range(SUB):
                                pool.indirect_dma_start(
                                    out=g.records, out_offset=bass.IndirectOffsetOnAxis(ap=place[:, s, j:j + 1], axis=0),
                                    in_=rec[:, s, j, :], in_offset=None).then_inc(rec_sent[s], 16)
                    pool.wait_ge(loops_ready, 1)
                    for t in range(NT):
                        pool.indirect_dma_start(
                            out=g.records, out_offset=bass.IndirectOffsetOnAxis(ap=loop_slot[:, t:t + 1], axis=0),
                            in_=loop_rec[:, t, :], in_offset=None).then_inc(loops_sent, 16)
                    pool.wait_ge(loops_sent, 16 * NT)
                    for s in range(2):
                        pool.wait_ge(rec_sent[s], 16 * SUB * TURNS)

    with phase(nc) as ph:
        recs = ph.sb("recs", [P, R * SLOTS, 4], I32)
        row_dst = ph.sb("row_dst", [P, R])
        kind = ph.sb("kind", [P, R * SLOTS])
        ends = ph.sb("ends", [P, 2])
        hit = ph.sb("hit", [P, 2, P])
        has = ph.sb("has", [P, 2])
        same = ph.sb("same", [P, 1])
        psum = ph.ps("psum", [P, 2, P])
        loaded, have_ends, spread = ph.sem("loaded"), ph.sem("have_ends"), ph.sem("spread")
        with nc.Block() as block:
            @block.sync
            def _(sp):
                sp.dma_start(recs[:], g.records.rearrange("(p s) c -> p s c", p=P)).then_inc(loaded, 16)

            @block.tensor
            def _(pe):
                pe.wait_ge(have_ends, 1)
                for k in range(2):
                    last = pe.matmul(psum[:, k], ends[:, k:k + 1].broadcast_to([P, P]), C.ident[:],
                                     start=True, stop=True)
                last.then_inc(spread, 1)

            @block.vector
            def _(v):
                v.wait_ge(loaded, 16)
                v.tensor_copy(row_dst[:], recs[:].rearrange("p (r k) c -> p r k c", k=SLOTS)[:, :, 0, 3])
                v.tensor_copy(kind[:], recs[:, :, 2])
                if g.degrees:
                    v.tensor_copy(g.weight[:, :, 0:SLOTS],
                                  recs[:].bitcast(F32).rearrange("p (r k) c -> p r k c", k=SLOTS)[:, :, :, 1])
                v.drain()
                v.tensor_copy(ends[:, 0:1], row_dst[:, 0:1])
                v.tensor_copy(ends[:, 1:2], row_dst[:, R - 1:R])
                v.drain()
                v.tensor_tensor(same[:], ends[:, 0:1], ends[:, 1:2], ALU.is_equal).then_inc(have_ends, 1)
                v.tensor_scalar(g.is_edge[:].rearrange("p r k -> p (r k)"), kind[:], 1.0, None, ALU.is_equal)
                v.tensor_scalar(g.is_any[:].rearrange("p r k -> p (r k)"), kind[:], 1.0, None, ALU.is_ge)
                v.memset(g.cont[:, 0:1], 0.0)
                v.memset(g.cont[:, R:R + 1], 0.0)
                v.tensor_copy(g.last_node[:], row_dst[:, R - 1:R])
                v.tensor_tensor(g.cont[:, 1:R], row_dst[:, 1:R], row_dst[:, 0:R - 1], ALU.is_equal)
                v.memset(g.apart[:, R:R + 1], -APART)
                v.drain()
                if g.degrees:
                    v.tensor_copy(g.weight[:, :, SLOTS], g.cont[:, 0:R])
                v.tensor_scalar(g.apart[:, 0:R], g.cont[:, 0:R], 1.0, APART, ALU.subtract, ALU.mult)
                for k, into in enumerate((g.in_first, g.in_last)):
                    v.tensor_scalar(into[:], row_dst[:], ends[:, k:k + 1], None, ALU.is_equal)
                    v.drain()
                    v.tensor_scalar(into[:], into[:], 1.0, APART, ALU.subtract, ALU.mult)
                v.wait_ge(spread, 1)
                v.tensor_scalar(hit[:, 0], psum[:, 1], ends[:, 0:1], None, ALU.is_equal)
                v.tensor_scalar(hit[:, 1], psum[:, 0], ends[:, 1:2], None, ALU.is_equal)
                v.drain()
                v.tensor_tensor(hit[:, 0], hit[:, 0], C.below[:], ALU.mult)
                v.tensor_tensor(hit[:, 1], hit[:, 1], C.above[:], ALU.mult)
                v.drain()
                v.tensor_copy(g.carry[:], hit[:, 1])
                v.tensor_scalar(g.from_prev[:], hit[:, 0], 1.0, APART, ALU.subtract, ALU.mult)
                v.tensor_scalar(g.from_next[:], hit[:, 1], 1.0, APART, ALU.subtract, ALU.mult)
                v.tensor_reduce(has[:], hit[:], AX.X, ALU.max)
                v.drain()
                v.tensor_tensor(same[:], same[:], has[:, 1:2], ALU.mult)
                v.drain()
                v.tensor_scalar(same[:], same[:], -1.0, 1.0, ALU.mult, ALU.add)
                v.drain()
                v.tensor_tensor(g.ends_here[:], same[:], has[:, 0:1], ALU.mult)
                for t in range(NT):
                    v.tensor_scalar(g.first_node[:, t:t + 1], ends[:, 0:1], float(P * t), None, ALU.subtract)


class Pass:

    def __init__(self, graph, source, target, feats, cols, heads, slope, score, inner, mask, dead=None,
                 target_ends=None):
        self.graph = graph
        self.source = source
        self.target = target
        self.feats = feats
        self.cols = cols
        self.heads = heads
        self.slope = slope
        self.score = score
        self.inner = inner
        self.mask = mask
        self.target_ends = target_ends
        self.dead = dead

    def per_head(self, ap):
        if self.inner == "h":
            return ap.rearrange("p a (f h) -> p a f h", h=self.heads)
        return ap.rearrange("p a (h f) -> p a h f", h=self.heads)

    def spread(self, ap):
        each = self.feats // self.heads
        return wide(ap, 2, each) if self.inner == "h" else wide(ap, 3, each)


def edge_pass(nc, C, e, att, finish):
    g, F, H, K = e.graph, e.feats, e.heads, SLOTS
    R = g.R
    soft = e.score != "weight"
    W = F + (H if soft else 0)
    WC = W + (H if soft else 0)
    RING = 9 if e.score == "sum" else 6
    TURNS, REST = divmod(R, RING)
    CHUNK = 3 if e.score == "sum" else 1

    def chunks(steps):
        return [(s, min(CHUNK, steps - s)) for s in range(0, steps, CHUNK)]

    n = Phase.count
    run_table = nc.dram_tensor(f"run_{n}", (P * R, W), F32, kind="Internal").ap()
    run_rows = run_table.rearrange("(p r) f -> p r f", p=P)
    with ExitStack() as outer:
        def keep(name, shape, dt=F32):
            return outer.enter_context(nc.sbuf_tensor(f"{name}_{n}", shape, dt))

        last_state = keep("last_state", [P, W])
        top = keep("top", [P, R + 1, H])
        cin = keep("cin", [P, WC])

        with phase(nc) as ph:
            att_rows, sum_rows = e.score == "att", e.score == "sum"
            stage = ph.sb("stage", [P, RING, K * 4], I32)
            G = ph.sb("G", [P, RING, K + 1, W])
            if att_rows:
                T = ph.sb("T", [P, RING, W])
            if sum_rows:
                at_end = ph.sb("at_end", [P, R, H])
                target = ph.sb("target", [P, R, H])
                last_target = ph.sb("last_target", [P, H])
                ends_in, last_in = ph.sem("ends_in"), ph.sem("last_in")
            weighed = ph.sb("weighed", [P, K + 1, F])
            score_e = ph.sb("score_e", [P, RING, K + 1, H])
            score_x = ph.sb("score_x", [P, RING, K + 1, H])
            dead = ph.sb("dead", [P, CHUNK, K, H])
            best = ph.sb("best", [P, CHUNK, H])
            prob = ph.sb("prob", [P, RING, K + 2, H])
            lowered = ph.sb("lowered", [P, R, K])
            idx_in, gathered, consumed = (ph.sem_ring(n, RING) for n in ("idx_in", "gathered", "consumed"))
            scored, powered = ph.sem_ring("scored", RING), ph.sem_ring("powered", RING)
            state_ready, state_out, state_free = (ph.sem_ring(n, RING) for n in (
                "state_ready", "state_out", "state_free"))
            flipped, bent, attended, seen = (ph.sem_ring(n, 2) for n in ("flipped", "bent", "attended", "seen"))
            sp_passed, pool_passed, v_passed, act_passed, pe_passed = (ph.sem(n) for n in (
                "sp_passed", "pool_passed", "v_passed", "act_passed", "pe_passed"))
            if e.score == "att":
                bent_sb = ph.sb("bent_sb", [P, 2, DC, K, P])
                ident_k = ph.sb("ident_k", [P, K, P])
                have_ident = ph.sem("have_ident")
                psum_t = ph.ps("psum_t", [P, 2, DC, K, P])
                psum_e = ph.ps("psum_e", [P, 2, 512])
            idx_view = g.records.rearrange("(p r k) c -> p r (k c)", p=P, k=K)
            per_turn = 16 * (K + (1 if att_rows else 0))
            with nc.Block() as block:
                @block.sync
                def _(sp):
                    if sum_rows:
                        sp.dma_start(at_end[:], e.target_ends.rearrange("(p r) h -> p r h", p=P)).then_inc(ends_in, 16)
                    for s in range(RING):
                        sp.dma_start(stage[:, s, :], idx_view[:, s, :]).then_inc(idx_in[s], 16)

                    def store_state(i, s):
                        to = (s + 1) % RING
                        hold(sp, state_ready[to], i + 1, sp_passed)
                        sp.dma_start(run_rows[:, bass.ds(i * RING + s, 1), :].rearrange("p o f -> p (o f)"),
                                     G[:, to, K, :]).then_inc(state_out[to], 16)

                    def state_stored(i, s):
                        to = (s + 1) % RING
                        hold(sp, state_out[to], i * 16 + 16, state_free[to])

                    def next_indices(i, s):
                        hold(sp, gathered[s], i * per_turn + per_turn, sp_passed)
                        sp.dma_start(stage[:, s, :], idx_view[:, bass.ds(i * RING + (RING + s), 1), :]
                                     .rearrange("p o c -> p (o c)")).then_inc(idx_in[s], 16)

                    with sp.Fori(0, TURNS - 1) as i:
                        for s in range(RING):
                            next_indices(i, s)
                            store_state(i, s)
                            if s:
                                state_stored(i, s - 1)
                        state_stored(i, RING - 1)
                    for s in range(RING):
                        if s < REST:
                            next_indices(TURNS - 1, s)
                        store_state(TURNS - 1, s)
                        if s:
                            state_stored(TURNS - 1, s - 1)
                    state_stored(TURNS - 1, RING - 1)
                    for s in range(REST):
                        store_state(TURNS, s)
                        state_stored(TURNS, s)

                @block.gpsimd
                def _(pool):
                    def gather(i, s):
                        hold(pool, idx_in[s], i * 16 + 16, pool_passed)
                        hold(pool, consumed[s], i + 1, pool_passed)
                        for k in range(K):
                            pool.indirect_dma_start(
                                out=G[:, s, k, :], out_offset=None, in_=e.source,
                                in_offset=bass.IndirectOffsetOnAxis(ap=stage[:, s, 4 * k:4 * k + 1], axis=0)
                            ).then_inc(gathered[s], 16)
                        if att_rows:
                            pool.indirect_dma_start(
                                out=T[:, s, :], out_offset=None, in_=e.target,
                                in_offset=bass.IndirectOffsetOnAxis(ap=stage[:, s, 3:4], axis=0)
                            ).then_inc(gathered[s], 16)

                    if sum_rows:
                        pool.indirect_dma_start(
                            out=last_target[:], out_offset=None, in_=e.target,
                            in_offset=bass.IndirectOffsetOnAxis(ap=g.last_node[:, 0:1], axis=0)).then_inc(last_in, 16)
                    with pool.Fori(0, TURNS) as i:
                        for s in range(RING):
                            gather(i, s)
                    for s in range(REST):
                        gather(TURNS, s)

                @block.tensor
                def _(pe):
                    if e.score != "att":
                        return
                    pe.wait_ge(have_ident, 1)

                    def flip(i, s):
                        q, use = s % 2, i * (RING // 2) + (s // 2 + 1)
                        hold(pe, gathered[s], i * per_turn + per_turn, pe_passed)
                        hold(pe, bent[q], use, pe_passed)
                        for b in range(DC):
                            pe.matmul(psum_t[:, q, b].rearrange("p k n -> p (k n)"), T[:, s, b * P:(b + 1) * P],
                                      ident_k[:].rearrange("p k n -> p (k n)"), start=True, stop=False)
                            for k in range(K):
                                last = pe.matmul(psum_t[:, q, b, k, :], G[:, s, k, b * P:(b + 1) * P], C.ident[:],
                                                 start=False, stop=(k == K - 1))
                        last.then_inc(flipped[q], 1)

                    def attend(i, s):
                        q, use = s % 2, i * (RING // 2) + (s // 2 + 1)
                        hold(pe, bent[q], use + 1, pe_passed)
                        hold(pe, seen[q], use, pe_passed)
                        for k in range(K):
                            for b in range(DC):
                                if H == 1:
                                    last = pe.matmul(psum_e[:, q, k:k + 1], bent_sb[:, q, b, k, :], att[:, b, 0:1],
                                                     start=(b == 0), stop=(b == DC - 1))
                                else:
                                    last = pe.matmul(psum_e[:, q, k * H + b:k * H + b + 1], bent_sb[:, q, b, k, :],
                                                     att[:, b, b:b + 1], start=True, stop=True)
                        last.then_inc(attended[q], 1)

                    def turn_of(i, steps):
                        for s in range(steps):
                            flip(i, s)
                            if s:
                                attend(i, s - 1)
                        attend(i, steps - 1)

                    with pe.Fori(0, TURNS) as i:
                        turn_of(i, RING)
                    if REST:
                        turn_of(TURNS, REST)

                @block.scalar
                def _(act):
                    if not soft:
                        return
                    for q in range(2):
                        act.sem_inc(bent[q], 1)

                    def bend(i, s):
                        if e.score == "att":
                            q, use = s % 2, i * (RING // 2) + (s // 2 + 1)
                            hold(act, flipped[q], use, act_passed)
                            act.activation(bent_sb[:, q], psum_t[:, q], ACT.Relu).then_inc(bent[q], 1)

                    def power(i, s, n):
                        hold(act, scored[s], i + 1, act_passed)
                        act.activation(prob[:, s:s + n, 1:K + 2], score_x[:, s:s + n], ACT.Exp).then_inc(powered[s], 1)

                    def turn_of(i, steps):
                        if sum_rows:
                            for s, chunk in chunks(steps):
                                power(i, s, chunk)
                            return
                        for s in range(steps):
                            bend(i, s)
                            if s:
                                power(i, s - 1, 1)
                        power(i, steps - 1, 1)

                    with act.Fori(0, TURNS) as i:
                        turn_of(i, RING)
                    if REST:
                        turn_of(TURNS, REST)

                @block.vector
                def _(v):
                    for s in range(RING):
                        v.sem_inc(consumed[s], 1)
                        v.sem_inc(state_free[s], 1)
                    v.memset(G[:, 0, K, :], 0.0)
                    if soft:
                        for q in range(2):
                            v.sem_inc(seen[q], 1)
                        v.tensor_scalar(lowered[:], e.mask[:], 1.0, MASKED, ALU.subtract, ALU.mult)
                        v.memset(score_e[:, :, K, :], -MASKED / 10)
                        v.memset(top[:, 0, :], -MASKED / 10)
                        if e.score == "att":
                            v.tensor_copy(ident_k[:], wide(C.ident[:], 1, K)).then_inc(have_ident, 1)
                    if sum_rows:
                        v.wait_ge(ends_in, 16)
                        v.wait_ge(last_in, 16)
                        v.tensor_copy(at_end[:, R - 1, :], last_target[:])
                        v.drain()
                        for h in range(H):
                            v.tensor_tensor_scan(target[:, R - 1::-1, h], g.cont[:, R:0:-1], at_end[:, R - 1::-1, h],
                                                 0.0, ALU.mult, ALU.add)
                    v.drain()

                    def score(i, s, n):
                        r, r1 = bass.ds(i * RING + s, n), bass.ds(i * RING + s + 1, n)
                        flat = "p o h -> p (o h)"
                        for j in range(n):
                            hold(v, gathered[s + j], i * per_turn + per_turn, v_passed)
                        if not soft:
                            return
                        now = score_e[:, s:s + n, 0:K]
                        to = T[:, s:s + n, F:W] if att_rows else target[:, r, :]
                        v.tensor_tensor(now, G[:, s:s + n, 0:K, F:W], wide(to, 2, K), ALU.add)
                        v.drain()
                        if att_rows:
                            q, use = s % 2, i * (RING // 2) + (s // 2 + 1)
                            hold(v, attended[q], use, v_passed)
                            v.tensor_tensor(now, now, psum_e[:, q:q + 1, 0:K * H].rearrange("p o (k h) -> p o k h", h=H),
                                            ALU.add).then_inc(seen[q], 1)
                        else:
                            v.scalar_tensor_tensor(now, now, e.slope, now, ALU.mult, ALU.max)
                        v.drain()
                        if e.dead is not None:
                            v.tensor_scalar(dead[:, 0:n], now, 0.0, e.dead, ALU.is_equal, ALU.mult)
                            v.drain()
                            v.tensor_tensor(now, now, dead[:, 0:n], ALU.add)
                            v.drain()
                        v.tensor_tensor(now, now, wide(lowered[:, r, :], 3, H), ALU.add)
                        v.drain()
                        v.tensor_reduce(best[:, 0:n], score_e[:, s:s + n].rearrange("p s k h -> p s h k"), AX.X, ALU.max)
                        v.drain()
                        ahead = [bass.ds(i * RING + s + j, 1) for j in range(n + 1)]
                        for j in range(n):
                            v.scalar_tensor_tensor(top[:, ahead[j + 1], :].rearrange(flat), top[:, ahead[j], :].rearrange(flat),
                                                   g.apart[:, ahead[j]], best[:, j], ALU.add, ALU.max)
                            v.drain()
                        for j in range(n):
                            v.scalar_tensor_tensor(score_x[:, s + j, K], top[:, ahead[j], :].rearrange(flat),
                                                   g.apart[:, ahead[j]], top[:, ahead[j + 1], :].rearrange(flat),
                                                   ALU.add, ALU.subtract)
                        v.tensor_tensor(score_x[:, s:s + n, 0:K], now, wide(top[:, r1, :], 2, K),
                                        ALU.subtract).then_inc(scored[s], 1)

                    def weigh(i, s):
                        r, to = bass.ds(i * RING + s, 1), (s + 1) % RING
                        if soft:
                            if s % CHUNK == 0:
                                hold(v, powered[s], i + 1, v_passed)
                            v.tensor_tensor(prob[:, s, 0], prob[:, s, K + 1], G[:, s, K, F:W], ALU.mult)
                            v.tensor_tensor(e.per_head(weighed[:]), e.per_head(G[:, s, :, 0:F]),
                                            e.spread(prob[:, s, 1:K + 2]), ALU.mult).then_inc(consumed[s], 1)
                        else:
                            v.tensor_tensor(weighed[:], G[:, s],
                                            wide(g.weight[:, r, :].rearrange("p o k -> p (o k)"), 2, F),
                                            ALU.mult).then_inc(consumed[s], 1)
                        hold(v, state_free[to], i + 1, v_passed)
                        v.drain()
                        if soft:
                            v.tensor_reduce(G[:, to, K, F:W], prob[:, s, 0:K + 1].rearrange("p k h -> p h k"), AX.X,
                                            ALU.add)
                        v.tensor_reduce(G[:, to, K, 0:F], weighed[:].rearrange("p k f -> p f k"), AX.X,
                                        ALU.add).then_inc(state_ready[to], 1)
                        v.drain()

                    def turn_of(i, steps):
                        if sum_rows:
                            weighed_to = 0
                            for s0, chunk in chunks(steps):
                                score(i, s0, chunk)
                                ready_to = steps if s0 + chunk == steps else s0 + chunk - 1
                                for s in range(weighed_to, ready_to):
                                    weigh(i, s)
                                weighed_to = ready_to
                            return
                        for s in range(steps):
                            score(i, s, 1)
                            if s:
                                weigh(i, s - 1)
                        weigh(i, steps - 1)

                    with v.Fori(0, TURNS) as i:
                        turn_of(i, RING)
                    if REST:
                        turn_of(TURNS, REST)
                    v.tensor_copy(last_state[:], G[:, R % RING, K, :])

        with phase(nc) as ph:
            got = ph.sb("got", [P, NT, W])
            den = ph.sb("den", [P, GRP, max(H, 1)])
            den2 = ph.sb("den2", [P, GRP, max(H, 1)])
            onto = ph.sb("onto", [P, 2, GRP, P])
            landed = ph.sem_ring("landed", NG)
            onto_ready, added, read, done, stored, have_cin = (ph.sem(n) for n in (
                "onto_ready", "added", "read", "done", "stored", "have_cin"))
            inside = ph.sb("inside", [P, H, R])
            first_top = ph.sb("first_top", [P, H])
            before_top = ph.sb("before_top", [P, H])
            both_top = ph.sb("both_top", [P, H])
            masked = ph.sb("masked", [P, H, P])
            factor = ph.sb("factor", [P, H])
            banks = ph.ps("banks", [P, 8, 512])
            psum = banks[:, 0:4, :].rearrange("p a b -> p (a b)")[:, 0:2 * H * P].rearrange("p (a h q) -> p a h q", a=2, h=H)
            psum_n, psum_c = banks[:, 0:GRP, :], banks[:, 7, :]
            spread, topped, spread2, shifted, powered, carried = (ph.sem(n) for n in (
                "spread", "topped", "spread2", "shifted", "powered", "carried"))
            last_top = top[:, R, :]
            with nc.Block() as block:
                @block.gpsimd
                def _(pool):
                    for t in range(NT):
                        pool.indirect_dma_start(
                            out=got[:, t, :], out_offset=None, in_=run_table,
                            in_offset=bass.IndirectOffsetOnAxis(ap=g.end_row[:, t:t + 1], axis=0)).then_inc(landed[t // GRP], 16)

                @block.tensor
                def _(pe):
                    if soft:
                        for h in range(H):
                            last = pe.matmul(psum[:, 0, h], last_top[:, h:h + 1].broadcast_to([P, P]), C.ident[:],
                                             start=True, stop=True)
                        last.then_inc(spread, 1)
                        pe.wait_ge(topped, 1)
                        for h in range(H):
                            last = pe.matmul(psum[:, 1, h], both_top[:, h:h + 1].broadcast_to([P, P]), C.ident[:],
                                             start=True, stop=True)
                        last.then_inc(spread2, 1)
                        pe.wait_ge(powered, 1)
                        for h in range(H):
                            if e.inner == "h":
                                to, of = psum_c[:, h:F:H], last_state[:, h:F:H]
                            else:
                                to, of = (x[:, h * (F // H):(h + 1) * (F // H)] for x in (psum_c, last_state))
                            pe.matmul(to, masked[:, h], of, start=True, stop=True, skip_group_check=True)
                            last = pe.matmul(psum_c[:, F + h:F + h + 1], masked[:, h], last_state[:, F + h:F + h + 1],
                                             start=True, stop=True, skip_group_check=True)
                    else:
                        last = pe.matmul(psum_c[:, 0:W], g.carry[:], last_state[:], start=True, stop=True)
                    last.then_inc(carried, 1)
                    pe.wait_ge(have_cin, 1)
                    for i in range(NG):
                        pe.wait_ge(onto_ready, i + 1)
                        if i:
                            pe.wait_ge(read, i)
                        for s in range(GRP):
                            last = pe.matmul(psum_n[:, s, 0:WC], onto[:, i % 2, s], cin[:], start=True, stop=True)
                        last.then_inc(added, 1)

                @block.scalar
                def _(act):
                    if soft:
                        act.wait_ge(shifted, 1)
                        act.activation(masked[:], masked[:], ACT.Exp, scale=-1.0)
                        act.activation(factor[:], factor[:], ACT.Exp).then_inc(powered, 1)

                @block.vector
                def _(v):
                    def select(i):
                        v.tensor_tensor(onto[:, i % 2], wide(C.iota_row[:], 1, GRP),
                                        wide(g.first_node[:, i * GRP:(i + 1) * GRP], 2, P),
                                        ALU.is_equal).then_inc(onto_ready, 1)

                    if soft:
                        v.tensor_tensor(inside[:], top[:, 1:R + 1, :].rearrange("p r h -> p h r"),
                                        wide(g.in_first[:], 1, H), ALU.add)
                        v.drain()
                        v.tensor_reduce(first_top[:], inside[:], AX.X, ALU.max)
                        v.wait_ge(spread, 1)
                        v.tensor_tensor(masked[:], psum[:, 0], wide(g.from_prev[:], 1, H), ALU.add)
                        v.drain()
                        v.tensor_reduce(before_top[:], masked[:], AX.X, ALU.max)
                        v.drain()
                        v.tensor_tensor(both_top[:], first_top[:], before_top[:], ALU.max).then_inc(topped, 1)
                        v.drain()
                        v.tensor_tensor(factor[:], first_top[:], both_top[:], ALU.subtract)
                        v.wait_ge(spread2, 1)
                        for h in range(H):
                            last = v.scalar_tensor_tensor(masked[:, h], psum[:, 1, h], last_top[:, h:h + 1],
                                                          g.from_next[:], ALU.subtract, ALU.subtract)
                        last.then_inc(shifted, 1)
                        v.wait_ge(powered, 1)
                        v.tensor_scalar(cin[:, W:WC], factor[:], 1.0, g.ends_here[:, 0:1], ALU.subtract, ALU.mult)
                    v.wait_ge(carried, 1)
                    v.tensor_scalar(cin[:, 0:W], psum_c[:, 0:W], g.ends_here[:, 0:1], None, ALU.mult)
                    v.drain()
                    v.sem_inc(have_cin, 1)
                    select(0)
                    for i in range(NG):
                        if i + 1 < NG:
                            if i:
                                v.wait_ge(added, i)
                            select(i + 1)
                        mine = got[:, i * GRP:(i + 1) * GRP, :]
                        v.wait_ge(added, i + 1)
                        v.wait_ge(landed[i], 16 * GRP)
                        if soft:
                            v.tensor_scalar(den[:], psum_n[:, :, W:WC], 1.0, None, ALU.add)
                            v.drain()
                            v.tensor_tensor(e.per_head(mine[:, :, 0:F]), e.per_head(mine[:, :, 0:F]), e.spread(den[:]),
                                            ALU.mult)
                            v.tensor_tensor(mine[:, :, F:W], mine[:, :, F:W], den[:], ALU.mult)
                            v.drain()
                        v.tensor_tensor(mine, mine, psum_n[:, :, 0:W], ALU.add).then_inc(read, 1)
                        v.drain()
                        if soft:
                            v.tensor_scalar(den2[:], mine[:, :, F:W], 0.0, None, ALU.is_le)
                            v.drain()
                            v.tensor_tensor(den[:], mine[:, :, F:W], den2[:], ALU.add)
                            v.drain()
                            v.reciprocal(den2[:], den[:])
                            v.drain()
                            v.tensor_tensor(e.per_head(mine[:, :, 0:F]), e.per_head(mine[:, :, 0:F]), e.spread(den2[:]),
                                            ALU.mult)
                            v.drain()
                        finish.vector(v, slice(i * GRP, (i + 1) * GRP), mine)
                        v.drain()
                        v.sem_inc(done, 1)

                @block.sync
                def _(sp):
                    if finish.table is not None:
                        for i in range(NG):
                            sp.wait_ge(done, i + 1)
                            sp.dma_start(node_rows(finish.table, i, F), got[:, i * GRP:(i + 1) * GRP, 0:F]
                                         ).then_inc(stored, 16)
                        sp.wait_ge(stored, 16 * NG)


def node_rows(table, i, cols):
    return table.rearrange("(g t p) f -> g p t f", g=NG, p=P)[bass.ds(i, 1), :, :, 0:cols] \
        .rearrange("o p t f -> (o p) t f")


class ToNodes:

    table = None

    def __init__(self, C, bias=None):
        self.C, self.bias = C, bias

    def vector(self, v, tiles, got):
        if self.bias is not None:
            v.tensor_tensor(got[:, :, 0:D], got[:, :, 0:D], wide(self.bias[:], 1, GRP), ALU.add)
            v.drain()
        v.tensor_tensor(self.C.X[:, tiles, :], self.C.X[:, tiles, :], got[:, :, 0:D], ALU.add)


class ToTable:

    def __init__(self, table, cols, bias=None, scale=None, raw=False):
        self.table, self.cols, self.bias, self.scale, self.raw = table, cols, bias, scale, raw

    def vector(self, v, tiles, got):
        out = got[:, :, 0:self.cols]
        if self.scale is not None:
            v.tensor_tensor(out, out, wide(self.scale[:, tiles], 2, self.cols), ALU.mult)
            v.drain()
        if self.bias is not None:
            v.tensor_tensor(out, out, wide(self.bias[:], 1, GRP), ALU.add)
            v.drain()
        if not self.raw:
            v.tensor_scalar(out, out, 0.0, None, ALU.max)



def turn(nc, C, xT, table=None, cols=D, norm=True, keep_table=None, add=False, parts=None):
    KB = cols // P
    with phase(nc) as ph:
        rows = ph.sb("rows", [P, NT, cols])
        stats = ph.sb("stats", [P, GRP, 6])
        mean_var = ph.sb("mean_var", [P, GRP, 2])
        mean = ph.sb("mean", [P, NT])
        spread = ph.sb("spread", [P, NT])
        inv = ph.sb("inv", [P, NT])
        psum = ph.ps("psum", [P, GRP, 512])
        ready, turned, taken, have_var, rooted, stored, present = (ph.sem(n) for n in (
            "ready", "turned", "taken", "have_var", "rooted", "stored", "present"))
        loaded = ph.sem_ring("loaded", 0 if norm else NG)
        act_passed, sp_passed = ph.sem("act_passed"), ph.sem("sp_passed")
        with nc.Block() as block:
            @block.sync
            def _(sp):
                if not norm:
                    for g in range(NG):
                        sp.dma_start(rows[:, g * GRP:(g + 1) * GRP, :], node_rows(table, g, cols)).then_inc(loaded[g], 16)
                    for g in range(NG):
                        sp.wait_ge(loaded[g], 16)
                        sp.sem_inc(present, 1)
                if keep_table is not None:
                    with sp.Fori(0, NG) as i:
                        hold(sp, ready, i * GRP + GRP, sp_passed)
                        sp.dma_start(node_rows(keep_table, i, cols), rows[:, bass.ds(i * GRP, GRP), :]).then_inc(stored, 16)
                    sp.wait_ge(stored, NG * 16)

            @block.vector
            def _(v):
                if norm:
                    with v.Fori(0, NG) as i:
                        for s in range(GRP):
                            v.bn_stats(stats[:, s], C.X[:, bass.ds(i * GRP + s, 1), :].rearrange("p o f -> p (o f)"))
                        v.drain()
                        for s in range(GRP):
                            v.bn_aggr(mean_var[:, s], stats[:, s])
                        v.drain()
                        v.tensor_scalar(spread[:, bass.ds(i * GRP, GRP)], mean_var[:, :, 1], LN_EPS, None, ALU.add)
                        v.tensor_copy(mean[:, bass.ds(i * GRP, GRP)], mean_var[:, :, 0])
                        v.drain()
                    v.sem_inc(have_var, 1)
                    v.wait_ge(rooted, 1)
                    v.reciprocal(inv[:], spread[:])
                    v.drain()
                    with v.Fori(0, NG) as i:
                        for s in range(GRP):
                            tile = bass.ds(i * GRP + s, 1)
                            v.tensor_scalar(rows[:, tile, :], C.X[:, tile, :], mean[:, tile], inv[:, tile],
                                            ALU.subtract, ALU.mult).then_inc(ready, 1)
                    if add:
                        v.drain()
                        v.tensor_tensor(C.X[:], C.X[:], rows[:], ALU.add)
                if parts is not None:
                    v.wait_ge(taken, NT)
                    v.tensor_tensor(parts[1][:], xT[:], parts[0][:], ALU.subtract)

            @block.tensor
            def _(pe):
                for t in range(NT):
                    if norm:
                        pe.wait_ge(ready, t + 1)
                    elif t % GRP == 0:
                        pe.wait_ge(present, t // GRP + 1)
                    if t >= GRP:
                        pe.wait_ge(taken, t - GRP + 1)
                    for b in range(KB):
                        last = pe.transpose(psum[:, t % GRP, b * P:(b + 1) * P], rows[:, t, b * P:(b + 1) * P], C.ident[:])
                    last.then_inc(turned, 1)

            @block.scalar
            def _(act):
                if norm:
                    act.wait_ge(have_var, 1)
                    act.activation(spread[:], spread[:], ACT.Sqrt).then_inc(rooted, 1)
                with act.Fori(0, NG) as i:
                    for s in range(GRP):
                        hold(act, turned, i * GRP + (s + 1), act_passed)
                        for to in (xT,) if parts is None else (parts[0], xT):
                            last = act.activation(to[:, :, bass.ds(i * UNIT + s * P, P)],
                                                  psum[:, s, 0:cols].rearrange("p (b q) -> p b q", q=P), ACT.Copy)
                        last.then_inc(taken, 1)


def project(nc, C, xT, jobs, cols, K=D, extra=0, at_ends=None):
    KB, J = K // P, len(jobs)
    with phase(nc) as ph:
        w = ph.sb("w", [P, J, KB, cols])
        spots = 2 if J > 1 else NG
        rows = ph.sb("rows", [P, spots * GRP, cols + extra])
        b = ph.sb("b", [P, J, cols])
        scratch = ph.sb("scratch", [P, GRP, cols]) if extra else None
        x = ph.sb("x", [P, GRP, KB, P])
        psum = ph.ps("psum", [P, GRP, 512])
        loaded, staged, made, taken, ready, stored = (ph.sem(n) for n in (
            "loaded", "staged", "made", "taken", "ready", "stored"))
        v_passed, pe_passed, sp_passed, act_passed, free = (ph.sem(n) for n in (
            "v_passed", "pe_passed", "sp_passed", "act_passed", "free"))
        if at_ends is not None:
            graph, ends_table, ends_at, ends_n = at_ends
            zeros = ph.sb("zeros", [P, graph.R * ends_n])
            zero_made, zero_sent, ends_sent = ph.sem("zero_made"), ph.sem("zero_sent"), ph.sem("ends_sent")
        loads = sum(16 * (1 + (job[1] is not None)) for job in jobs)

        def spot(i, j):
            return slice((j % 2) * GRP, (j % 2 + 1) * GRP) if J > 1 else bass.ds(i * GRP, GRP)

        def one(i, j, s):
            return slice((j % 2) * GRP + s, (j % 2) * GRP + s + 1) if J > 1 else bass.ds(i * GRP + s, 1)

        with nc.Block() as block:
            @block.sync
            def _(sp):
                for j, (weight, bias, _, _) in enumerate(jobs):
                    sp.dma_start(w[:, j], weight.rearrange("(k p) c -> p k c", p=P)).then_inc(loaded, 16)
                    if bias is not None:
                        sp.dma_start(b[:, j], bias.broadcast_to([P, cols])).then_inc(loaded, 16)
                if at_ends is not None:
                    sp.wait_ge(zero_made, 1)
                    sp.dma_start(ends_table.rearrange("(p r) h -> p (r h)", p=P), zeros[:]).then_inc(zero_sent, 16)
                per_group = 16 * sum(len(job[3]) for job in jobs)
                with sp.Fori(0, NG) as i:
                    sent = 0
                    for j, (_, _, _, outputs) in enumerate(jobs):
                        hold(sp, ready, i * J + (j + 1), sp_passed)
                        for table, at, n in outputs:
                            sp.dma_start(node_rows(table, i, n), rows[:, spot(i, j), at:at + n]).then_inc(stored, 16)
                            sent += 16
                        hold(sp, stored, i * per_group + sent, free)

            @block.gpsimd
            def _(pool):
                if at_ends is None:
                    return
                pool.wait_ge(zero_sent, 16)
                for t in range(NT):
                    if t % GRP == 0:
                        pool.wait_ge(ready, t // GRP + 1)
                    pool.indirect_dma_start(
                        out=ends_table, out_offset=bass.IndirectOffsetOnAxis(ap=graph.end_row[:, t:t + 1], axis=0),
                        in_=rows[:, t, ends_at:ends_at + ends_n], in_offset=None).then_inc(ends_sent, 16)
                pool.wait_ge(ends_sent, 16 * NT)

            @block.tensor
            def _(pe):
                pe.sem_inc(made, J * GRP)
                pe.wait_ge(loaded, loads)
                with pe.Fori(0, NG) as i:
                    for j in range(J):
                        for s in range(GRP):
                            if j == 0:
                                hold(pe, staged, i * GRP + (s + 1), pe_passed)
                            hold(pe, taken, i * (J * GRP) + (j * GRP + s + 1), pe_passed)
                            for k in range(KB):
                                last = pe.matmul(psum[:, s, 0:cols], x[:, s, k, :], w[:, j, k, :],
                                                 start=(k == 0), stop=(k == KB - 1))
                            last.then_inc(made, 1)

            @block.scalar
            def _(act):
                with act.Fori(0, NG) as i:
                    for s in range(GRP):
                        hold(act, made, i * (J * GRP) + ((J - 1) * GRP + s + 1), act_passed)
                        act.activation(x[:, s], xT[:, :, bass.ds(i * UNIT + s * P, P)], ACT.Copy).then_inc(staged, 1)

            @block.vector
            def _(v):
                if at_ends is not None:
                    v.memset(zeros[:], 0.0).then_inc(zero_made, 1)
                v.sem_inc(taken, GRP)
                v.sem_inc(free, spots)
                v.wait_ge(loaded, loads)
                with v.Fori(0, NG) as i:
                    for j, (_, bias, post, _) in enumerate(jobs):
                        hold(v, free, i * J + (j + 1), v_passed)
                        for s in range(GRP):
                            hold(v, made, i * (J * GRP) + (J * GRP + j * GRP + s + 1), v_passed)
                            to, of = rows[:, one(i, j, s), 0:cols], psum[:, s:s + 1, 0:cols]
                            if bias is not None:
                                v.tensor_tensor(to, of, b[:, j:j + 1], ALU.add).then_inc(taken, 1)
                            else:
                                v.tensor_copy(to, of).then_inc(taken, 1)
                        v.drain()
                        if post is not None:
                            post(v, rows[:, spot(i, j), :], scratch)
                            v.drain()
                        v.sem_inc(ready, 1)


def load_rows(nc, pairs, scales=()):
    with phase(nc) as ph:
        loaded = ph.sem("loaded")
        with nc.Block() as block:
            @block.vector
            def _(v):
                if scales:
                    v.wait_ge(loaded, 16 * len(pairs))
                for row, factor in scales:
                    v.tensor_scalar(row, row, factor, None, ALU.mult)

            @block.sync
            def _(sp):
                for to, of in pairs:
                    sp.dma_start(to, of).then_inc(loaded, 16)
                sp.wait_ge(loaded, 16 * len(pairs))


def pick_top(v, scratch, score, chosen, E, K):
    before = scratch
    for x in range(E):
        me = score[:, :, x:x + 1]
        if x:
            v.tensor_tensor(before[:, :, 0:x], score[:, :, 0:x], me.broadcast_to([P, NT, x]), ALU.is_ge)
        if x < E - 1:
            v.tensor_tensor(before[:, :, x:E - 1], score[:, :, x + 1:E], me.broadcast_to([P, NT, E - 1 - x]), ALU.is_gt)
        v.drain()
        v.tensor_reduce(chosen[:, :, x], before[:, :, 0:E - 1], AX.X, ALU.add)
        v.drain()
    v.tensor_scalar(chosen[:], chosen[:], float(K), None, ALU.is_lt)
    v.drain()


def choose_experts(nc, C, logits, gates, E, K, among_chosen):
    with phase(nc) as ph:
        top = ph.sb("top", [P, NT])
        scratch = ph.sb("scratch", [P, NT, E])
        chosen = ph.sb("chosen", [P, NT, E])
        prob = ph.sb("prob", [P, NT, E])
        total = ph.sb("total", [P, NT])
        shifted, powered = ph.sem("shifted"), ph.sem("powered")
        with nc.Block() as block:
            @block.scalar
            def _(act):
                act.wait_ge(shifted, 1)
                act.activation(prob[:], prob[:], ACT.Exp).then_inc(powered, 1)

            @block.vector
            def _(v):
                v.tensor_reduce(top[:], logits[:], AX.X, ALU.max)
                v.drain()
                v.tensor_tensor(prob[:], logits[:], wide(top[:], 2, E), ALU.subtract).then_inc(shifted, 1)
                if among_chosen:
                    pick_top(v, scratch, logits, chosen, E, K)
                v.wait_ge(powered, 1)
                if among_chosen:
                    v.tensor_tensor(prob[:], prob[:], chosen[:], ALU.mult)
                    v.drain()
                v.tensor_reduce(total[:], prob[:], AX.X, ALU.add)
                v.drain()
                v.reciprocal(total[:], total[:])
                v.drain()
                v.tensor_tensor(prob[:], prob[:], wide(total[:], 2, E), ALU.mult)
                v.drain()
                if among_chosen:
                    v.tensor_copy(gates[:], prob[:])
                else:
                    pick_top(v, scratch, prob, chosen, E, K)
                    v.tensor_tensor(gates[:], prob[:], chosen[:], ALU.mult)


def logits_of(nc, C, xT, weight, bias, E, logits):
    with phase(nc) as ph:
        w = ph.sb("w", [P, DC, E])
        b = ph.sb("b", [P, E])
        psum = ph.ps("psum", [P, NT, E])
        loaded, made = ph.sem("loaded"), ph.sem("made")
        with nc.Block() as block:
            @block.sync
            def _(sp):
                sp.dma_start(w[:], weight).then_inc(loaded, 16)
                sp.dma_start(b[:], bias.broadcast_to([P, E])).then_inc(loaded, 16)

            @block.tensor
            def _(pe):
                pe.wait_ge(loaded, 32)
                for t in range(NT):
                    for k in range(DC):
                        last = pe.matmul(psum[:, t, :], xT[:, k, t * P:(t + 1) * P], w[:, k, :],
                                         start=(k == 0), stop=(k == DC - 1))
                last.then_inc(made, 1)

            @block.vector
            def _(v):
                v.wait_ge(made, 1)
                v.tensor_tensor(logits[:], psum[:], wide(b[:], 1, NT), ALU.add)


def experts(nc, C, parts, gates, E, H, func, w1, b1, w2, b2):
    HC = H // P
    with phase(nc) as ph:
        w1_raw = ph.sb("w1_raw", [P, DC, H])
        w2_raw = ph.sb("w2_raw", [P, HC, D])
        w1_high, w1_low = (ph.sb(n, [P, DC, H], F32R) for n in ("w1_high", "w1_low"))
        w2_high, w2_low = (ph.sb(n, [P, HC, D], F32R) for n in ("w2_high", "w2_low"))
        b1s = ph.sb("b1s", [P, E * HC])
        b2s = ph.sb("b2s", [P, E, D])
        x_high, x_low = parts
        hidden = ph.sb("hidden", [P, 2, UNIT])
        hid_high, hid_low = (ph.sb(n, [P, HC, UNIT], F32R) for n in ("hid_high", "hid_low"))
        psum_h = ph.ps("psum_h", [P, 2, 2, 512])
        YB = 4
        psum_y = ph.ps("psum_y", [P, YB, 512])
        w1_in, w2_in, b_in, w1_split, w2_split = (ph.sem(n) for n in (
            "w1_in", "w2_in", "b_in", "w1_split", "w2_split"))
        h_made, h_taken, h_split = (ph.sem_ring(n, 2) for n in ("h_made", "h_taken", "h_split"))
        y_made, y_taken = ph.sem("y_made"), ph.sem("y_taken")
        sp_passed, pool_passed, pe_passed, act_passed, v_passed = (ph.sem(n) for n in (
            "sp_passed", "pool_passed", "pe_passed", "act_passed", "v_passed"))
        H2 = HC // 2

        def each_expert(eng, expert):
            if E > 1:
                with eng.Fori(0, E) as e:
                    expert(e)
            else:
                expert(0)

        with nc.Block() as block:
            @block.sync
            def _(sp):
                sp.dma_start(b1s[:], b1).then_inc(b_in, 16)
                sp.dma_start(b2s[:], b2.rearrange("(o e) f -> o e f", o=1).broadcast_to([P, E, D])).then_inc(b_in, 16)

                def load(e):
                    for raw, w, arrived, split in ((w1_raw, w1, w1_in, w1_split), (w2_raw, w2, w2_in, w2_split)):
                        hold(sp, split, e + 1, sp_passed)
                        sp.dma_start(raw[:], w[bass.ds(e, 1), :, :].rearrange("o (k p) h -> p (o k) h", p=P)
                                     ).then_inc(arrived, 16)

                each_expert(sp, load)

            @block.gpsimd
            def _(pool):
                pool.sem_inc(w1_split, 1)
                pool.sem_inc(w2_split, 1)

                def split(raw, high, low, done):
                    pool.tensor_copy(high[:], raw[:])
                    pool.drain()
                    pool.tensor_tensor(low[:], raw[:], high[:], ALU.subtract)
                    pool.drain()
                    pool.sem_inc(done, 1)

                def expert(e):
                    hold(pool, w1_in, e * 16 + 16, pool_passed)
                    hold(pool, h_made[1], e * (NG * H2) + 1, pool_passed)
                    split(w1_raw, w1_high, w1_low, w1_split)
                    hold(pool, w2_in, e * 16 + 16, pool_passed)
                    hold(pool, y_made, e * NT + 1, pool_passed)
                    split(w2_raw, w2_high, w2_low, w2_split)

                each_expert(pool, expert)

            @block.tensor
            def _(pe):
                for made in (*h_made, y_made):
                    pe.sem_inc(made, 1)

                def product(out, parts, first, last):
                    (lh, ll), (rh, rl) = parts
                    pe.matmul(out, lh, rh, start=first, stop=False)
                    pe.matmul(out, lh, rl, start=False, stop=False)
                    return pe.matmul(out, ll, rh, start=False, stop=last)

                def expert(e):
                    hold(pe, w1_split, e + 2, pe_passed)
                    with pe.Fori(0, NG) as c:
                        u = e * NG + c
                        for m in range(HC):
                            s = m % 2
                            hold(pe, h_taken[s], u * H2 + (m // 2 + 1), pe_passed)
                            for half in range(2):
                                nodes = bass.ds(c * UNIT + half * HALF, HALF)
                                for k in range(DC):
                                    block_of = slice(m * P, (m + 1) * P)
                                    last = product(psum_h[:, s, half, 0:HALF],
                                                   ((w1_high[:, k, block_of], w1_low[:, k, block_of]),
                                                    (x_high[:, k, nodes], x_low[:, k, nodes])), k == 0, k == DC - 1)
                            last.then_inc(h_made[s], 1)
                        hold(pe, w2_split, e + 2, pe_passed)

                        def bank_free(t):
                            before = t - YB if t >= YB else max(q for q in range(GRP) if q % YB == t) - GRP
                            hold(pe, y_taken, u * GRP + (before + 1 + GRP), pe_passed)

                        def second(t, m):
                            tile = slice(t * P, (t + 1) * P)
                            return product(psum_y[:, t % YB, 0:D],
                                           ((hid_high[:, m, tile], hid_low[:, m, tile]),
                                            (w2_high[:, m, :], w2_low[:, m, :])), m == 0, m == HC - 1)

                        for t in range(YB):
                            bank_free(t)
                        for m in range(HC):
                            hold(pe, h_split[m % 2], u * H2 + (m // 2 + 2), pe_passed)
                            for t in range(YB):
                                last = second(t, m)
                                if m == HC - 1:
                                    last.then_inc(y_made, 1)
                        for t in range(YB, GRP):
                            bank_free(t)
                            for m in range(HC):
                                last = second(t, m)
                            last.then_inc(y_made, 1)

                each_expert(pe, expert)

            @block.scalar
            def _(act):
                for s in range(2):
                    act.sem_inc(h_taken[s], 1)
                act.wait_ge(b_in, 32)

                def expert(e):
                    with act.Fori(0, NG) as c:
                        act.preload_act_table(func)
                        u = e * NG + c
                        for m in range(HC):
                            s = m % 2
                            hold(act, h_made[s], u * H2 + (m // 2 + 2), act_passed)
                            hold(act, h_split[s], u * H2 + (m // 2 + 1), act_passed)
                            of = psum_h[:, s, :, 0:HALF]
                            for to in (hidden[:, s], hid_high[:, m]):
                                last = act.activation(to.rearrange("p (a n) -> p a n", a=2), of, func,
                                                      bias=b1s[:, bass.ds(e * HC + m, 1)])
                            last.then_inc(h_taken[s], 1)

                each_expert(act, expert)

            @block.vector
            def _(v):
                v.sem_inc(y_taken, GRP)
                for s in range(2):
                    v.sem_inc(h_split[s], 1)
                v.wait_ge(b_in, 32)

                def expert(e):
                    with v.Fori(0, NG) as c:
                        u = e * NG + c
                        tile = [bass.ds(c * GRP + t, 1) for t in range(GRP)]
                        for m in range(HC):
                            s = m % 2
                            hold(v, h_taken[s], u * H2 + (m // 2 + 2), v_passed)
                            v.tensor_tensor(hid_low[:, m], hidden[:, s], hid_high[:, m],
                                            ALU.subtract).then_inc(h_split[s], 1)
                        for t in range(GRP):
                            v.scalar_tensor_tensor(C.X[:, tile[t], :], b2s[:, bass.ds(e, 1), :],
                                                   gates[:, tile[t], bass.ds(e, 1)], C.X[:, tile[t], :],
                                                   ALU.mult, ALU.add)
                        v.drain()
                        for t in range(GRP):
                            hold(v, y_made, u * GRP + (t + 2), v_passed)
                            v.scalar_tensor_tensor(
                                C.X[:, tile[t], :], psum_y[:, t % YB:t % YB + 1, 0:D],
                                gates[:, tile[t], bass.ds(e, 1)],
                                C.X[:, tile[t], :], ALU.mult, ALU.add).then_inc(y_taken, 1)
                        v.drain()

                each_expert(v, expert)


def channel_mix(nc, C, xT, fc_w, fc_b, ch_w, scale, table):
    with phase(nc) as ph:
        w = ph.sb("w", [P, DC, D])
        b = ph.sb("b", [P, DC])
        mix = ph.sb("mix", [P, DC, P])
        hidden = ph.sb("hidden", [P, DC, UNIT])
        rows = ph.sb("rows", [P, GRP, D])
        psum_h = ph.ps("psum_h", [P, DC, 2, 512])
        psum_y = ph.ps("psum_y", [P, 3, 2, D])
        zeroed, loaded, made, mixed, ready, stored = (ph.sem(n) for n in (
            "zeroed", "loaded", "made", "mixed", "ready", "stored"))
        hid = ph.sem_ring("hid", DC)
        sp_passed, pe_passed, act_passed, v_passed, free = (ph.sem(n) for n in (
            "sp_passed", "pe_passed", "act_passed", "v_passed", "free"))
        CH = D // 4
        with nc.Block() as block:
            @block.sync
            def _(sp):
                sp.wait_ge(zeroed, 1)
                sp.dma_start(w[:], fc_w.rearrange("(k p) c -> p k c", p=P)).then_inc(loaded, 16)
                sp.dma_start(b[:], fc_b).then_inc(loaded, 16)
                for m in range(DC):
                    for c in range(2):
                        sp.dma_start(mix[c * CH:(c + 1) * CH, m, c * CH:(c + 1) * CH], ch_w[2 * m + c]).then_inc(loaded, 16)
                with sp.Fori(0, NG) as i:
                    hold(sp, ready, i + 2, sp_passed)
                    sp.dma_start(node_rows(table, i, D), rows[:]).then_inc(stored, 16)
                    hold(sp, stored, i * 16 + 16, free)

            @block.tensor
            def _(pe):
                pe.wait_ge(loaded, 96)
                with pe.Fori(0, NG) as i:
                    for m in range(DC):
                        hold(pe, hid[m], i + 1, pe_passed)
                        for half in range(2):
                            for k in range(DC):
                                last = pe.matmul(psum_h[:, m, half, 0:HALF], w[:, k, m * P:(m + 1) * P],
                                                 xT[:, k, bass.ds(i * UNIT + half * HALF, HALF)],
                                                 start=(k == 0), stop=(k == DC - 1))
                        last.then_inc(made, 1)
                    hold(pe, ready, i + 1, pe_passed)
                    for m in range(DC):
                        hold(pe, hid[m], i + 2, pe_passed)
                        for t in range(GRP):
                            last = pe.matmul(psum_y[:, t // 2, t % 2, m * P:(m + 1) * P], hidden[:, m, t * P:(t + 1) * P],
                                             mix[:, m, :], start=True, stop=True)
                    last.then_inc(mixed, 1)

            @block.scalar
            def _(act):
                for m in range(DC):
                    act.sem_inc(hid[m], 1)
                with act.Fori(0, NG) as i:
                    for m in range(DC):
                        hold(act, made, i * DC + (m + 1), act_passed)
                        act.activation(hidden[:, m].rearrange("p (a n) -> p a n", a=2), psum_h[:, m, :, 0:HALF],
                                       ACT.Identity, bias=b[:, m:m + 1]).then_inc(hid[m], 1)

            @block.vector
            def _(v):
                v.memset(mix[:], 0.0).then_inc(zeroed, 1)
                v.sem_inc(ready, 1)
                v.sem_inc(free, 1)
                with v.Fori(0, NG) as i:
                    hold(v, mixed, i + 1, v_passed)
                    hold(v, free, i + 1, v_passed)
                    flat = psum_y[:].rearrange("p a b f -> p (a b) f")[:, 0:GRP, :]
                    v.tensor_tensor(rows[:], flat, wide(scale[:, bass.ds(i * GRP, GRP)], 2, D), ALU.mult)
                    v.drain()
                    v.sem_inc(ready, 1)


def add_product(nc, C, xT, weight, bias=None):
    with phase(nc) as ph:
        w = ph.sb("w", [P, DC, D])
        b = ph.sb("b", [P, D])
        x = ph.sb("x", [P, GRP, DC, P])
        staged, act_passed = ph.sem("staged"), ph.sem("act_passed")
        psum = ph.ps("psum", [P, GRP, 512])
        loaded, made, taken = ph.sem("loaded"), ph.sem("made"), ph.sem("taken")
        v_passed, pe_passed = ph.sem("v_passed"), ph.sem("pe_passed")
        loads = 16 * (1 + (bias is not None))
        with nc.Block() as block:
            @block.sync
            def _(sp):
                sp.dma_start(w[:], weight.rearrange("(k p) c -> p k c", p=P)).then_inc(loaded, 16)
                if bias is not None:
                    sp.dma_start(b[:], bias.broadcast_to([P, D])).then_inc(loaded, 16)

            @block.tensor
            def _(pe):
                pe.sem_inc(made, GRP)
                pe.wait_ge(loaded, loads)
                with pe.Fori(0, NG) as i:
                    for s in range(GRP):
                        hold(pe, taken, i * GRP + (s + 1), pe_passed)
                        hold(pe, staged, i * GRP + (s + 1), pe_passed)
                        for k in range(DC):
                            last = pe.matmul(psum[:, s, 0:D], x[:, s, k, :], w[:, k, :],
                                             start=(k == 0), stop=(k == DC - 1))
                        last.then_inc(made, 1)

            @block.scalar
            def _(act):
                with act.Fori(0, NG) as i:
                    for s in range(GRP):
                        hold(act, made, i * GRP + (s + 1), act_passed)
                        act.activation(x[:, s], xT[:, :, bass.ds(i * UNIT + s * P, P)], ACT.Copy).then_inc(staged, 1)

            @block.vector
            def _(v):
                v.sem_inc(taken, GRP)
                v.wait_ge(loaded, loads)
                with v.Fori(0, NG) as i:
                    if bias is not None:
                        tiles = bass.ds(i * GRP, GRP)
                        v.tensor_tensor(C.X[:, tiles, :], C.X[:, tiles, :], wide(b[:], 1, GRP), ALU.add)
                        v.drain()
                    for s in range(GRP):
                        tile = bass.ds(i * GRP + s, 1)
                        hold(v, made, i * GRP + (GRP + s + 1), v_passed)
                        v.tensor_tensor(C.X[:, tile, :], C.X[:, tile, :], psum[:, s:s + 1, 0:D], ALU.add).then_inc(taken, 1)


def take_top_nodes(nc, C, weights, gates, K):
    table = nc.dram_tensor("router_weights", (NT, P), F32, kind="Internal").ap()
    with phase(nc) as ph:
        row = ph.sb("row", [P, NP])
        junk = ph.sb("junk", [P, NP])
        rank = ph.sb("rank", [P, 4, NT])
        total = ph.sb("total", [P, NT])
        turned = ph.sb("turned", [NT, P])
        psum = ph.ps("psum", [P, 512])
        turned_in, copied, stored, spread = (ph.sem(n) for n in ("turned_in", "copied", "stored", "spread"))
        with nc.Block() as block:
            @block.tensor
            def _(pe):
                pe.transpose(psum[0:NT, 0:P], weights[:, :, 0], C.ident[:]).then_inc(turned_in, 1)

            @block.sync
            def _(sp):
                sp.wait_ge(copied, 1)
                sp.dma_start(table, turned[:]).then_inc(stored, 16)
                sp.wait_ge(stored, 16)
                sp.dma_start(row[:], table.rearrange("(o t) q -> o (t q)", o=1).broadcast_to([P, NP])).then_inc(spread, 16)

            @block.vector
            def _(v):
                v.memset(rank[:], 0.0)
                v.wait_ge(turned_in, 1)
                v.tensor_copy(turned[:], psum[0:NT, 0:P]).then_inc(copied, 1)
                v.wait_ge(spread, 16)
                v.drain()

                def count(k, t, lo, hi, op, by):
                    v.scalar_tensor_tensor(junk[:, lo:hi], row[:, lo:hi], weights[:, t, 0:1], by, op, ALU.mult,
                                           accum_out=rank[:, k, t:t + 1])
                    v.drain()

                for t in range(NT):
                    at, end = t * P, min((t + 1) * P, N)
                    if at:
                        count(0, t, 0, at, ALU.is_ge, C.ones[:, 0:1].broadcast_to([P, at]))
                    if end < N:
                        count(1, t, end, N, ALU.is_gt, C.ones[:, 0:1].broadcast_to([P, N - end]))
                    count(2, t, at, end, ALU.is_gt, C.ones[:, 0:end - at])
                    count(3, t, at, end, ALU.is_equal, C.below[:, 0:end - at])
                v.tensor_reduce(total[:], rank[:].rearrange("p k t -> p t k"), AX.X, ALU.add)
                v.drain()
                v.scalar_tensor_tensor(gates[:, :, 0], total[:], float(K), weights[:, :, 0], ALU.is_lt, ALU.mult)


def score_experts(nc, C, table, b_gat, gamma, beta, logits):
    F, E = 16, 4
    with phase(nc) as ph:
        agg = ph.sb("agg", [P, NT, F])
        sq = ph.sb("sq", [P, NT, F])
        rows = ph.sb("rows", [P, 3, F])
        mean = ph.sb("mean", [P, NT])
        var = ph.sb("var", [P, NT])
        loaded, have_var, rooted = ph.sem("loaded"), ph.sem("have_var"), ph.sem("rooted")
        with nc.Block() as block:
            @block.sync
            def _(sp):
                sp.dma_start(agg[:], table.rearrange("(t p) f -> p t f", p=P)).then_inc(loaded, 16)
                for k, of in enumerate((b_gat, gamma, beta)):
                    sp.dma_start(rows[:, k, :], of.broadcast_to([P, F])).then_inc(loaded, 16)

            @block.scalar
            def _(act):
                act.wait_ge(have_var, 1)
                act.activation(var[:], var[:], ACT.Sqrt).then_inc(rooted, 1)

            @block.vector
            def _(v):
                v.wait_ge(loaded, 64)
                v.tensor_tensor(agg[:], agg[:], wide(rows[:, 0], 1, NT), ALU.add)
                v.drain()
                v.tensor_reduce(mean[:], agg[:], AX.X, ALU.add)
                v.drain()
                v.tensor_scalar(mean[:], mean[:], 1.0 / F, None, ALU.mult)
                v.drain()
                v.tensor_tensor(agg[:], agg[:], wide(mean[:], 2, F), ALU.subtract)
                v.drain()
                v.tensor_tensor(sq[:], agg[:], agg[:], ALU.mult)
                v.drain()
                v.tensor_reduce(var[:], sq[:], AX.X, ALU.add)
                v.drain()
                v.tensor_scalar(var[:], var[:], 1.0 / F, LN_EPS, ALU.mult, ALU.add).then_inc(have_var, 1)
                v.wait_ge(rooted, 1)
                v.reciprocal(mean[:], var[:])
                v.drain()
                v.tensor_tensor(agg[:], agg[:], wide(mean[:], 2, F), ALU.mult)
                v.drain()
                v.tensor_tensor(agg[:], agg[:], wide(rows[:, 1], 1, NT), ALU.mult)
                v.drain()
                v.tensor_tensor(agg[:], agg[:], wide(rows[:, 2], 1, NT), ALU.add)
                v.drain()
                v.tensor_reduce(logits[:], agg[:].rearrange("p t (h e) -> p t e h", e=E), AX.X, ALU.add)
                v.drain()
                v.tensor_scalar(logits[:], logits[:], E / F, None, ALU.mult)


def build(nc, a, out, layers=8):
    class C:
        pass

    with ExitStack() as ctx:
        def sb(name, shape, dt=F32):
            return ctx.enter_context(nc.sbuf_tensor(name, shape, dt))

        def dram(name, shape):
            return nc.dram_tensor(name, shape, F32, kind="Internal").ap()

        C.X = sb("node_features", [P, NT, D])
        C.ident, C.ones, C.below, C.above, C.iota_row = (
            sb(n, [P, P]) for n in ("ident", "ones", "below", "above", "iota_row"))
        C.iota_col = sb("iota_col", [P, 1])
        C.node_i = sb("node_i", [P, NT], I32)
        build_constants(nc, C, a["x"])
        main = Graph(nc, sb, "main", a["dst_rows"].shape[0], True)
        sort_edges(nc, C, main, a["dst_rows"], a["dst_cols"], a["src_cols"], a["w_cols"])

        def store_and_stop():
            with phase(nc) as ph:
                sent = ph.sem("sent")
                with nc.Block() as block:
                    @block.sync
                    def _(sp):
                        sp.dma_start(out[0:(NT - 1) * P, :].rearrange("(t p) f -> p t f", p=P),
                                     C.X[:, 0:NT - 1, :]).then_inc(sent, 16)
                        sp.dma_start(out[(NT - 1) * P:N, :], C.X[0:N - (NT - 1) * P, NT - 1, :]).then_inc(sent, 16)
                        sp.wait_ge(sent, 32)

        @contextmanager
        def turned(cols=D, **kw):
            with nc.sbuf_tensor(f"xT_{Phase.count}", [P, cols // P, NP], F32) as xT:
                turn(nc, C, xT, cols=cols, **kw)
                yield xT

        @contextmanager
        def rows(*shapes):
            with ExitStack() as c:
                n = Phase.count
                yield [c.enter_context(nc.sbuf_tensor(f"row{k}_{n}", list(s), F32)) for k, s in enumerate(shapes)]

        @contextmanager
        def split_features():
            n = Phase.count
            with nc.sbuf_tensor(f"x_high_{n}", [P, DC, NP], F32R) as high:
                with nc.sbuf_tensor(f"x_low_{n}", [P, DC, NP], F32R) as low:
                    yield high, low

        def moe(parts, layer, gates, E, H, func):
            experts(nc, C, parts, gates, E, H, func, *(a[f"L{layer}_ffn_{n}"] for n in ("w1", "b1", "w2", "b2")))

        source, target = dram("l0_source", (NP, D + 4)), dram("l0_target", (NP, 4))
        ends = dram("l0_target_ends", (P * main.R, 4))
        with turned() as xT, rows((P, 2, D)) as (att,):
            load_rows(nc, [(att[:, k, :], a["L0_gnn_att"][k:k + 1, :].broadcast_to([P, D])) for k in range(2)])

            def scores(v, r, scratch):
                for k in range(2):
                    v.tensor_tensor(scratch[:], r[:, :, 0:D], wide(att[:, k], 1, GRP), ALU.mult)
                    v.drain()
                    v.tensor_reduce(r[:, :, D + 4 * k:D + 4 * k + 4],
                                    scratch[:].rearrange("p t (h f) -> p t h f", h=4), AX.X, ALU.add)
                    v.drain()

            project(nc, C, xT, [(a["L0_gnn_W"], None, scores, [(source, 0, D + 4), (target, D + 4, 4)])], D, extra=8,
                    at_ends=(main, ends, D + 4, 4))
        edge_pass(nc, C, Pass(main, source, target, D, D + 4, 4, 0.01, "sum", "f", main.is_edge, dead=-1000.0,
                              target_ends=ends),
                  None, ToNodes(C))
        if layers == 1:
            return store_and_stop()

        with rows((P, NT, 8)) as (gates,), split_features() as parts:
            with turned(parts=parts) as xT, rows((P, NT, 8)) as (logits,):
                logits_of(nc, C, xT, a["L0_ffn_gate_w"], a["L0_ffn_gate_b"], 8, logits)
                choose_experts(nc, C, logits, gates, 8, 2, False)
            moe(parts, 0, gates, 8, 512, ACT.Gelu)
        if layers == 2:
            return store_and_stop()

        source, target = dram("l1_source", (NP, D + 8)), dram("l1_target", (NP, 8))
        ends = dram("l1_target_ends", (P * main.R, 8))
        with turned(keep_table=source) as xT:
            project(nc, C, xT, [(a["L1_gnn_W"], a["L1_gnn_b"], None, [(source[:, D:D + 8], 0, 8), (target, 8, 8)])], 16,
                    at_ends=(main, ends, 8, 8))
        edge_pass(nc, C, Pass(main, source, target, D, D + 8, 8, 0.2, "sum", "h", main.is_edge, target_ends=ends), None,
                  ToNodes(C))
        if layers == 3:
            return store_and_stop()

        with rows((P, NT, 1)) as (gates,), split_features() as parts:
            with turned(add=True, parts=parts) as xT, rows((P, NT, 1)) as (weights,):
                logits_of(nc, C, xT, a["L1_ffn_wr"], a["L1_ffn_br"], 1, weights)
                take_top_nodes(nc, C, weights, gates, max(1, N // 2) - 1)
            moe(parts, 1, gates, 1, 1024, ACT.Gelu_apprx_tanh)
        if layers == 4:
            return store_and_stop()

        mixed, conv = dram("l2_mixed", (NP, D)), dram("l2_conv", (NP, D))
        for step in range(3):
            with (turned() if step == 0 else turned(table=conv, norm=False)) as xT:
                if step:
                    add_product(nc, C, xT, a["L2_gnn_mlp_w"][(step - 1) * D:step * D, :])
                channel_mix(nc, C, xT, a["L2_gnn_fc_w"][step], a["L2_gnn_fc_b"][:, step * DC:(step + 1) * DC],
                            a["L2_gnn_ch_w"][step], main.norm_out, mixed)
            with rows((P, D)) as (bias,):
                load_rows(nc, [(bias[:], a["L2_gnn_ch_b"][step:step + 1, :].broadcast_to([P, D]))])
                edge_pass(nc, C, Pass(main, mixed, None, D, D, 1, None, "weight", "f", None), None,
                          ToTable(conv, D, bias=bias, scale=main.norm_in))
        with turned(table=conv, norm=False) as xT:
            add_product(nc, C, xT, a["L2_gnn_mlp_w"][2 * D:3 * D, :], bias=a["L2_gnn_mlp_b"])
        if layers == 5:
            return store_and_stop()

        source, target, agg = dram("l2_source", (NP, 20)), dram("l2_target", (NP, 4)), dram("l2_agg", (NP, 16))
        with rows((P, NT, 4)) as (gates,), ExitStack() as gc:
            route = Graph(nc, lambda n, s, d: gc.enter_context(nc.sbuf_tensor(n, s, d)), "route",
                          a["route_dst_rows"].shape[0], False)
            sort_edges(nc, C, route, a["route_dst_rows"], a["route_dst_cols"], a["route_src_cols"], None)
            ends = dram("l2_target_ends", (P * route.R, 4))
            with split_features() as parts:
                with turned(parts=parts) as xT, rows((P, 2, 16)) as (att,):
                    load_rows(nc, [(att[:, k, :], a["L2_ffn_att"][k:k + 1, :].broadcast_to([P, 16])) for k in range(2)])

                    def scores(v, r, scratch):
                        for k in range(2):
                            v.tensor_tensor(scratch[:], r[:, :, 0:16], wide(att[:, k], 1, GRP), ALU.mult)
                            v.drain()
                            v.tensor_reduce(r[:, :, 16 + 4 * k:20 + 4 * k],
                                            scratch[:].rearrange("p t (h f) -> p t h f", h=4), AX.X, ALU.add)
                            v.drain()

                    project(nc, C, xT, [(a["L2_ffn_W_gat"], None, scores, [(source, 0, 20), (target, 20, 4)])], 16, extra=8,
                            at_ends=(route, ends, 20, 4))
                edge_pass(nc, C, Pass(route, source, target, 16, 20, 4, 0.2, "sum", "f", route.is_any,
                                       target_ends=ends), None,
                          ToTable(agg, 16, raw=True))
                with rows((P, NT, 4)) as (logits,):
                    score_experts(nc, C, agg, a["L2_ffn_b_gat"], a["L2_ffn_ln_gamma"], a["L2_ffn_ln_beta"], logits)
                    choose_experts(nc, C, logits, gates, 4, 2, True)
                moe(parts, 2, gates, 4, 512, ACT.Gelu)
        if layers == 6:
            return store_and_stop()

        pairs = [[dram(f"l3_{side}{k}", (NP, D + 2)) for k in range(2)] for side in ("left", "right")]
        singles = [dram(f"l3_{side}", (NP, D + 1)) for side in ("left", "right")]
        hidden = dram("l3_hidden", (NP, 2 * D))
        slope = 0.2

        def linear_part(att, H):
            def scores(v, r, scratch):
                v.tensor_tensor(scratch[:], r[:, :, 0:D], wide(att[:], 1, GRP), ALU.mult)
                v.drain()
                v.tensor_reduce(r[:, :, D:D + H], scratch[:].rearrange("p t (h f) -> p t h f", h=H), AX.X, ALU.add)
            return scores

        with rows((P, D), (P, D), (P, DC), (P, D), (P, D), (P, DC), (P, D), (P, D), (P, DC)) as kept:
            att, bias, att_col = kept[0::3], kept[1::3], kept[2::3]
            of = [(a["L3_gnn_a1"][0:1], a["L3_gnn_b1"][0:1], a["L3_gnn_a1_cols"][:, 0:2]),
                  (a["L3_gnn_a1"][1:2], a["L3_gnn_b1"][1:2], a["L3_gnn_a1_cols"][:, 2:4]),
                  (a["L3_gnn_a2"], a["L3_gnn_b2"], a["L3_gnn_a2_cols"])]
            load_rows(nc, [(att[k][:], of[k][0].broadcast_to([P, D])) for k in range(3)]
                      + [(bias[k][:], of[k][1].broadcast_to([P, D])) for k in range(3)]
                      + [(att_col[k][:], of[k][2]) for k in range(3)],
                      scales=[(att[k][:], slope) for k in range(3)] + [(att_col[k][:], 1 - slope) for k in range(3)])

            def att_of(k):
                return wide(att_col[k][:], 2, 2)

            with turned() as xT:
                project(nc, C, xT, [(a[f"L3_gnn_{name}"][:, k * D:(k + 1) * D], None, linear_part(att[k], 2),
                                     [(pairs[side][k], 0, D + 2)])
                                    for side, name in enumerate(("W1l", "W1r")) for k in range(2)], D, extra=2)
            for k in range(2):
                edge_pass(nc, C, Pass(main, pairs[0][k], pairs[1][k], D, D + 2, 2, slope, "att", "f", main.is_any),
                          att_of(k), ToTable(hidden[:, k * D:(k + 1) * D], D, bias=bias[k]))
            with turned(cols=2 * D, table=hidden, norm=False) as xT:
                project(nc, C, xT, [(a[f"L3_gnn_{name}"], None, linear_part(att[2], 1), [(singles[side], 0, D + 1)])
                                    for side, name in enumerate(("W2l", "W2r"))], D, K=2 * D, extra=1)
            edge_pass(nc, C, Pass(main, singles[0], singles[1], D, D + 1, 1, slope, "att", "f", main.is_any),
                      att_of(2), ToNodes(C, bias[2]))
        if layers == 7:
            return store_and_stop()

        with rows((P, NT, 8)) as (gates,), split_features() as parts:
            with turned(parts=parts) as xT, rows((P, NT, 8)) as (logits,):
                logits_of(nc, C, xT, a["L3_ffn_Wg"], a["L3_ffn_bg"], 8, logits)
                choose_experts(nc, C, logits, gates, 8, 2, True)
            moe(parts, 3, gates, 8, 1024, ACT.Relu)
        store_and_stop()


LAYERS = 8


def edge_lists(src, dst):
    tiles = -(-len(dst) // (8 * P)) * 8
    pad = (0, tiles * P - len(dst))
    src, dst = (np.pad(v, pad, constant_values=NP - 1).reshape(tiles, P) for v in (src, dst))
    return dst, np.ascontiguousarray(dst.T), np.ascontiguousarray(src.T)


def kernel(**inputs):
    import concourse.bacc as bacc
    from concourse.bass_utils import run_bass_kernel_spmd

    i = {k: np.asarray(v) for k, v in inputs.items()}

    def columns(b):
        return b.reshape(-1, P).T

    def blocks(w):
        return w.reshape(DC, P, -1).transpose(1, 0, 2)

    a = {"x": i["x"]}
    a["dst_rows"], a["dst_cols"], a["src_cols"] = edge_lists(i["src"], i["dst"])
    tiles = a["dst_rows"].shape[0]
    a["w_cols"] = np.pad(i["edge_weight"], (0, tiles * P - len(i["dst"]))).reshape(tiles, P).T
    a["route_dst_rows"], a["route_dst_cols"], a["route_src_cols"] = edge_lists(*i["L2_ffn_edge_index"])
    a["L0_gnn_W"] = i["L0_gnn_W"].transpose(1, 0, 2).reshape(D, D)
    a["L0_gnn_att"] = i["L0_gnn_att"].reshape(4, 2, 64).transpose(1, 0, 2).reshape(2, D)
    a["L0_ffn_gate_w"] = blocks(i["L0_ffn_gate_w"])
    a["L0_ffn_gate_b"] = i["L0_ffn_gate_b"].reshape(1, 8)
    for layer, names in ((0, ("W1", "b1", "W2", "b2")), (1, ("w1", "b1", "w2", "b2")),
                         (2, ("W1", "b1", "W2", "b2")), (3, ("W1", "b1", "W2", "b2"))):
        w1, b1, w2, b2 = (i[f"L{layer}_ffn_{n}"] for n in names)
        if layer == 1:
            w1, w2 = w1[None], w2[None]
        if layer == 3:
            w1, w2 = w1.transpose(0, 2, 1), w2.transpose(0, 2, 1)
        a[f"L{layer}_ffn_w1"], a[f"L{layer}_ffn_w2"] = w1, w2
        a[f"L{layer}_ffn_b1"], a[f"L{layer}_ffn_b2"] = columns(b1), b2.reshape(-1, D)
    a["L1_gnn_W"] = np.concatenate([i["L1_gnn_W_u"], i["L1_gnn_W_v"]]).T
    a["L1_gnn_b"] = np.pad(i["L1_gnn_b_u"], (0, 8)).reshape(1, 16)
    a["L1_ffn_wr"] = blocks(i["L1_ffn_wr"])
    a["L1_ffn_br"] = i["L1_ffn_br"].reshape(1, 1)
    a["L2_gnn_fc_w"] = i["L2_gnn_fc_w"].transpose(0, 2, 1)
    a["L2_gnn_fc_b"] = columns(i["L2_gnn_fc_b"])
    a["L2_gnn_ch_w"] = i["L2_gnn_ch_w"]
    a["L2_gnn_ch_b"] = i["L2_gnn_ch_b"].reshape(3, D)
    a["L2_gnn_mlp_w"] = i["L2_gnn_mlp_w"].T
    a["L2_gnn_mlp_b"] = i["L2_gnn_mlp_b"].reshape(1, D)
    a["L2_ffn_W_gat"] = i["L2_ffn_W_gat"]
    a["L2_ffn_att"] = np.stack([i["L2_ffn_att_src"].reshape(16), i["L2_ffn_att_dst"].reshape(16)])
    for n in ("b_gat", "ln_gamma", "ln_beta"):
        a[f"L2_ffn_{n}"] = i[f"L2_ffn_{n}"].reshape(1, 16)
    for n in ("W1l", "W1r", "W2l", "W2r"):
        a[f"L3_gnn_{n}"] = i[f"L3_gnn_{n}"]
    a["L3_gnn_a1"] = i["L3_gnn_a1"].reshape(2, D)
    a["L3_gnn_a1_cols"] = columns(i["L3_gnn_a1"])
    a["L3_gnn_a2_cols"] = columns(i["L3_gnn_a2"])
    a["L3_gnn_b1"] = i["L3_gnn_b1"].reshape(2, D)
    a["L3_gnn_a2"] = i["L3_gnn_a2"].reshape(1, D)
    a["L3_gnn_b2"] = i["L3_gnn_b2"].reshape(1, D)
    a["L3_ffn_Wg"] = blocks(i["L3_ffn_Wg"].T)
    a["L3_ffn_bg"] = i["L3_ffn_bg"].reshape(1, 8)

    nc = bacc.Bacc("TRN2", target_bir_lowering=False, num_devices=1)
    arrays = {f"in_{k}": np.ascontiguousarray(v) for k, v in a.items()}
    aps = {k: nc.dram_tensor(f"in_{k}", arrays[f"in_{k}"].shape, mybir.dt.from_np(arrays[f"in_{k}"].dtype),
                             kind="ExternalInput").ap() for k in a}
    out = nc.dram_tensor("out", (N, D), F32, kind="ExternalOutput").ap()
    build(nc, aps, out, LAYERS)
    result = run_bass_kernel_spmd(nc, [arrays], core_ids=[0])
    return result.results[0]["out"]
```
